# Optimizing a Trainium2 kernel written in Bass

```python
import numpy as np
import jax
import jax.numpy as jnp

def _softmax(x, axis=-1):
    return jax.nn.softmax(x, axis=axis)

def _gelu(x):
    return jax.nn.gelu(x, approximate=True)

def _silu(x):
    return jax.nn.silu(x)

def _sigmoid(x):
    return jax.nn.sigmoid(x)

def _layernorm(x, axis=-1, eps=1e-05):
    m = jnp.mean(x, axis=axis, keepdims=True)
    v = jnp.var(x, axis=axis, keepdims=True)
    return (x - m) / jnp.sqrt(v + eps)

def _scatter_add(tgt, idx, src, axis=0):
    return tgt.at[idx].add(src)

def _segment_sum(src, seg, n):
    return jax.ops.segment_sum(src, seg, n)
kernel_name = 'mk_vit_tower_d1_tok_img768_r4_f9647e'

def setup_inputs(seed: int=0):
    np.random.seed(seed)
    _w = jnp.asarray

    def _rec_inputs():
        import jax
        import jax.numpy as jnp
        _rk = jax.random.key(seed)
        x = -0.000222058 + 0.999998 * jax.random.normal(jax.random.fold_in(_rk, 1), (16, 3, 96, 96), jnp.float32)
        return x
    x = _rec_inputs()

    def _L0_tok_setup():
        import jax, jax.numpy as jnp
        import numpy as np
        from jax import lax
        HIDDEN = 192
        C_IN = 3
        PATCH = 16
        SIDE = 32
        NUM_PATCHES = SIDE * SIDE

        def _position_ids(nb_h, nb_w):
            boundaries = np.arange(1.0 / SIDE, 1.0, 1.0 / SIDE, dtype=np.float32)
            frac_h = np.arange(0.0, 1.0 - 1e-06, 1.0 / nb_h, dtype=np.float32)
            frac_w = np.arange(0.0, 1.0 - 1e-06, 1.0 / nb_w, dtype=np.float32)
            bh = np.searchsorted(boundaries, frac_h, side='right')
            bw = np.searchsorted(boundaries, frac_w, side='right')
            return jnp.asarray((bh[:, None] * SIDE + bw).reshape(-1), dtype=jnp.int32)
        key = jax.random.key(seed)
        k1, k2, k3 = jax.random.split(key, 3)
        pixel_values = jax.random.normal(k1, (32, C_IN, 128, 128), dtype=jnp.float32)
        conv_w = jax.random.normal(k2, (HIDDEN, C_IN, PATCH, PATCH), dtype=jnp.float32) * 0.02
        conv_b = jnp.zeros((HIDDEN,), dtype=jnp.float32)
        pos_table = jax.random.normal(k3, (NUM_PATCHES, HIDDEN), dtype=jnp.float32) * 0.02
        return {'pixel_values': pixel_values, 'conv_w': conv_w, 'conv_b': conv_b, 'pos_table': pos_table}
    _L0_tok_all = _L0_tok_setup()
    _L0_tok_in = {k: v for k, v in _L0_tok_all.items() if k in ('conv_w', 'conv_b', 'pos_table')}
    del _L0_tok_all

    def _L0_attn_setup():
        import jax, jax.numpy as jnp
        import numpy as np
        B_, L_, D_ = (4, 512, 192)
        D_INNER = 2 * D_
        HEADDIM = 2 * D_
        NHEADS = D_INNER // HEADDIM
        D_STATE = 128
        D_CONV = 4
        CONV_DIM = D_INNER + 2 * D_STATE
        D_IN_PROJ = 2 * D_INNER + 2 * D_STATE + NHEADS
        D_FF = 4 * D_
        EPS = 1e-05

        def _rmsnorm(x, w):
            return x * jax.lax.rsqrt(jnp.mean(x * x, -1, keepdims=True) + EPS) * w

        def _causal_dwconv(xBC, w, b):
            xc = xBC.transpose(0, 2, 1)
            y = jax.lax.conv_general_dilated(xc, w[:, None, :], window_strides=(1,), padding=[(D_CONV - 1, 0)], feature_group_count=CONV_DIM)
            return (y + b[None, :, None]).transpose(0, 2, 1)

        def _ssd_scan(xh, dt, A, Bm, Cm):
            dA = jnp.exp(dt * A)
            dBx = jnp.einsum('blhp,bln,blh->blhpn', xh, Bm, dt)

            def step(h, inp):
                dA_t, dBx_t, C_t = inp
                h = h * dA_t[:, :, None, None] + dBx_t
                y = jnp.einsum('bhpn,bn->bhp', h, C_t)
                return (h, y)
            h0 = jnp.zeros((xh.shape[0], NHEADS, HEADDIM, D_STATE), xh.dtype)
            _, ys = jax.lax.scan(step, h0, (dA.transpose(1, 0, 2), dBx.transpose(1, 0, 2, 3, 4), Cm.transpose(1, 0, 2)))
            return ys.transpose(1, 0, 2, 3)

        def _mamba2(u, in_proj_W, conv_w, conv_b, dt_bias, A_log, D, ssm_norm_w, out_proj_W):
            zxbcdt = u @ in_proj_W
            z = zxbcdt[..., :D_INNER]
            xBC = zxbcdt[..., D_INNER:D_INNER + CONV_DIM]
            dt = jax.nn.softplus(zxbcdt[..., -NHEADS:] + dt_bias)
            xBC = jax.nn.silu(_causal_dwconv(xBC, conv_w, conv_b))
            xs = xBC[..., :D_INNER]
            Bm = xBC[..., D_INNER:D_INNER + D_STATE]
            Cm = xBC[..., D_INNER + D_STATE:]
            A = -jnp.exp(A_log)
            xh = xs.reshape(xs.shape[0], xs.shape[1], NHEADS, HEADDIM)
            y = _ssd_scan(xh, dt, A, Bm, Cm) + xh * D[None, None, :, None]
            y = y.reshape(y.shape[0], y.shape[1], D_INNER)
            y = _rmsnorm(y * jax.nn.silu(z), ssm_norm_w)
            return y @ out_proj_W
        key = jax.random.key(seed)
        ks = jax.random.split(key, 8)
        s = 0.02
        return {'x': jax.random.normal(ks[0], (B_, L_, D_), jnp.float32), 'norm1_w': jnp.ones((D_,), jnp.float32), 'in_proj_W': jax.random.normal(ks[1], (D_, D_IN_PROJ), jnp.float32) * s, 'conv_w': jax.random.normal(ks[2], (CONV_DIM, D_CONV), jnp.float32) * 0.1, 'conv_b': jnp.zeros((CONV_DIM,), jnp.float32), 'dt_bias': jax.random.normal(ks[3], (NHEADS,), jnp.float32) * 0.1, 'A_log': jnp.zeros((NHEADS,), jnp.float32), 'D': jnp.ones((NHEADS,), jnp.float32), 'ssm_norm_w': jnp.ones((D_INNER,), jnp.float32), 'out_proj_W': jax.random.normal(ks[4], (D_INNER, D_), jnp.float32) * s, 'norm2_w': jnp.ones((D_,), jnp.float32), 'mlp_W1': jax.random.normal(ks[5], (D_, D_FF), jnp.float32) * s, 'mlp_W2': jax.random.normal(ks[6], (D_FF, D_), jnp.float32) * s}
    _L0_attn_all = _L0_attn_setup()
    _L0_attn_in = {k: v for k, v in _L0_attn_all.items() if k in ('norm1_w', 'in_proj_W', 'conv_w', 'conv_b', 'dt_bias', 'A_log', 'D', 'ssm_norm_w', 'out_proj_W', 'norm2_w', 'mlp_W1', 'mlp_W2')}
    del _L0_attn_all

    def _L0_ffn_setup():
        import jax, jax.numpy as jnp
        import numpy as np
        B, S, D, H, E, K = (1, 512, 192, 384, 8, 2)
        key = jax.random.key(seed)
        ks = jax.random.split(key, 6)
        scale_d = 1.0 / np.sqrt(D)
        scale_h = 1.0 / np.sqrt(H)
        return {'x': jax.random.normal(ks[0], (B, S, D), dtype=jnp.float32), 'Wg': jax.random.uniform(ks[1], (D, E), minval=-scale_d, maxval=scale_d, dtype=jnp.float32), 'W1': jax.random.uniform(ks[2], (E, D, H), minval=-scale_d, maxval=scale_d, dtype=jnp.float32), 'b1': jax.random.uniform(ks[3], (E, H), minval=-scale_d, maxval=scale_d, dtype=jnp.float32), 'W2': jax.random.uniform(ks[4], (E, H, D), minval=-scale_h, maxval=scale_h, dtype=jnp.float32), 'b2': jax.random.uniform(ks[5], (E, D), minval=-scale_h, maxval=scale_h, dtype=jnp.float32)}
    _L0_ffn_all = _L0_ffn_setup()
    _L0_ffn_in = {k: v for k, v in _L0_ffn_all.items() if k in ('Wg', 'W1', 'b1', 'W2', 'b2')}
    del _L0_ffn_all
    return {'x': x, 'L0_tok_conv_w': _L0_tok_in['conv_w'], 'L0_tok_conv_b': _L0_tok_in['conv_b'], 'L0_tok_pos_table': _L0_tok_in['pos_table'], 'L0_attn_norm1_w': _L0_attn_in['norm1_w'], 'L0_attn_in_proj_W': _L0_attn_in['in_proj_W'], 'L0_attn_conv_w': _L0_attn_in['conv_w'], 'L0_attn_conv_b': _L0_attn_in['conv_b'], 'L0_attn_dt_bias': _L0_attn_in['dt_bias'], 'L0_attn_A_log': _L0_attn_in['A_log'], 'L0_attn_D': _L0_attn_in['D'], 'L0_attn_ssm_norm_w': _L0_attn_in['ssm_norm_w'], 'L0_attn_out_proj_W': _L0_attn_in['out_proj_W'], 'L0_attn_norm2_w': _L0_attn_in['norm2_w'], 'L0_attn_mlp_W1': _L0_attn_in['mlp_W1'], 'L0_attn_mlp_W2': _L0_attn_in['mlp_W2'], 'L0_ffn_Wg': _L0_ffn_in['Wg'], 'L0_ffn_W1': _L0_ffn_in['W1'], 'L0_ffn_b1': _L0_ffn_in['b1'], 'L0_ffn_W2': _L0_ffn_in['W2'], 'L0_ffn_b2': _L0_ffn_in['b2']}

def reference(x, L0_tok_conv_w, L0_tok_conv_b, L0_tok_pos_table, L0_attn_norm1_w, L0_attn_in_proj_W, L0_attn_conv_w, L0_attn_conv_b, L0_attn_dt_bias, L0_attn_A_log, L0_attn_D, L0_attn_ssm_norm_w, L0_attn_out_proj_W, L0_attn_norm2_w, L0_attn_mlp_W1, L0_attn_mlp_W2, L0_ffn_Wg, L0_ffn_W1, L0_ffn_b1, L0_ffn_W2, L0_ffn_b2):
    import jax
    import jax.numpy as jnp

    def _L0_tok_ref(pixel_values, conv_w, conv_b, pos_table):
        import jax, jax.numpy as jnp
        import numpy as np
        from jax import lax
        HIDDEN = 192
        C_IN = 3
        PATCH = 16
        SIDE = 32
        NUM_PATCHES = SIDE * SIDE

        def _position_ids(nb_h, nb_w):
            boundaries = np.arange(1.0 / SIDE, 1.0, 1.0 / SIDE, dtype=np.float32)
            frac_h = np.arange(0.0, 1.0 - 1e-06, 1.0 / nb_h, dtype=np.float32)
            frac_w = np.arange(0.0, 1.0 - 1e-06, 1.0 / nb_w, dtype=np.float32)
            bh = np.searchsorted(boundaries, frac_h, side='right')
            bw = np.searchsorted(boundaries, frac_w, side='right')
            return jnp.asarray((bh[:, None] * SIDE + bw).reshape(-1), dtype=jnp.int32)
        B, _, H, W = pixel_values.shape
        nb_h, nb_w = (H // PATCH, W // PATCH)
        patches = lax.conv_general_dilated(pixel_values, conv_w, window_strides=(PATCH, PATCH), padding='VALID', dimension_numbers=('NCHW', 'OIHW', 'NCHW'))
        patches = patches + conv_b[None, :, None, None]
        embeddings = patches.reshape(B, HIDDEN, nb_h * nb_w).transpose(0, 2, 1)
        pos_ids = _position_ids(nb_h, nb_w)
        pos_emb = pos_table[pos_ids]
        return embeddings + pos_emb[None, :, :]

    def _L0_attn_ref(x, norm1_w, in_proj_W, conv_w, conv_b, dt_bias, A_log, D, ssm_norm_w, out_proj_W, norm2_w, mlp_W1, mlp_W2):
        import jax, jax.numpy as jnp
        import numpy as np
        B_, L_, D_ = (4, 512, 192)
        D_INNER = 2 * D_
        HEADDIM = 2 * D_
        NHEADS = D_INNER // HEADDIM
        D_STATE = 128
        D_CONV = 4
        CONV_DIM = D_INNER + 2 * D_STATE
        D_IN_PROJ = 2 * D_INNER + 2 * D_STATE + NHEADS
        D_FF = 4 * D_
        EPS = 1e-05

        def _rmsnorm(x, w):
            return x * jax.lax.rsqrt(jnp.mean(x * x, -1, keepdims=True) + EPS) * w

        def _causal_dwconv(xBC, w, b):
            xc = xBC.transpose(0, 2, 1)
            y = jax.lax.conv_general_dilated(xc, w[:, None, :], window_strides=(1,), padding=[(D_CONV - 1, 0)], feature_group_count=CONV_DIM)
            return (y + b[None, :, None]).transpose(0, 2, 1)

        def _ssd_scan(xh, dt, A, Bm, Cm):
            dA = jnp.exp(dt * A)
            dBx = jnp.einsum('blhp,bln,blh->blhpn', xh, Bm, dt)

            def step(h, inp):
                dA_t, dBx_t, C_t = inp
                h = h * dA_t[:, :, None, None] + dBx_t
                y = jnp.einsum('bhpn,bn->bhp', h, C_t)
                return (h, y)
            h0 = jnp.zeros((xh.shape[0], NHEADS, HEADDIM, D_STATE), xh.dtype)
            _, ys = jax.lax.scan(step, h0, (dA.transpose(1, 0, 2), dBx.transpose(1, 0, 2, 3, 4), Cm.transpose(1, 0, 2)))
            return ys.transpose(1, 0, 2, 3)

        def _mamba2(u, in_proj_W, conv_w, conv_b, dt_bias, A_log, D, ssm_norm_w, out_proj_W):
            zxbcdt = u @ in_proj_W
            z = zxbcdt[..., :D_INNER]
            xBC = zxbcdt[..., D_INNER:D_INNER + CONV_DIM]
            dt = jax.nn.softplus(zxbcdt[..., -NHEADS:] + dt_bias)
            xBC = jax.nn.silu(_causal_dwconv(xBC, conv_w, conv_b))
            xs = xBC[..., :D_INNER]
            Bm = xBC[..., D_INNER:D_INNER + D_STATE]
            Cm = xBC[..., D_INNER + D_STATE:]
            A = -jnp.exp(A_log)
            xh = xs.reshape(xs.shape[0], xs.shape[1], NHEADS, HEADDIM)
            y = _ssd_scan(xh, dt, A, Bm, Cm) + xh * D[None, None, :, None]
            y = y.reshape(y.shape[0], y.shape[1], D_INNER)
            y = _rmsnorm(y * jax.nn.silu(z), ssm_norm_w)
            return y @ out_proj_W
        res = x + _mamba2(_rmsnorm(x, norm1_w), in_proj_W, conv_w, conv_b, dt_bias, A_log, D, ssm_norm_w, out_proj_W)
        h = _rmsnorm(res, norm2_w)
        return jax.nn.gelu(h @ mlp_W1, approximate=False) @ mlp_W2

    def _L0_ffn_ref(x, Wg, W1, b1, W2, b2):
        import jax, jax.numpy as jnp
        import numpy as np
        B, S, D, H, E, K = (1, 512, 192, 384, 8, 2)
        gate_scores = jnp.einsum('bsd,de->bse', x, Wg)
        topk_scores, topk_idx = jax.lax.top_k(gate_scores, K)
        topk_probs = jax.nn.softmax(topk_scores, axis=-1)
        h = jax.nn.gelu(jnp.einsum('bsd,edh->bseh', x, W1) + b1, approximate=False)
        y = jnp.einsum('bseh,eho->bseo', h, W2) + b2
        y_sel = jnp.take_along_axis(y, topk_idx[..., None], axis=2)
        return jnp.sum(topk_probs[..., None] * y_sel, axis=2)
    h = _L0_tok_ref(x, L0_tok_conv_w, L0_tok_conv_b, L0_tok_pos_table)
    h = h + _L0_attn_ref(_layernorm(h, axis=-1), L0_attn_norm1_w, L0_attn_in_proj_W, L0_attn_conv_w, L0_attn_conv_b, L0_attn_dt_bias, L0_attn_A_log, L0_attn_D, L0_attn_ssm_norm_w, L0_attn_out_proj_W, L0_attn_norm2_w, L0_attn_mlp_W1, L0_attn_mlp_W2)
    h = h + _L0_ffn_ref(_layernorm(h, axis=-1), L0_ffn_Wg, L0_ffn_W1, L0_ffn_b1, L0_ffn_W2, L0_ffn_b2)
    return h

_drawn_inputs = setup_inputs


def setup_inputs(seed=0):
    import zlib

    import numpy as np

    out = dict(_drawn_inputs(seed))
    spreads = {'L0_tok_conv_b': (0.0, 0.1),
     'L0_attn_norm1_w': (1.0, 0.2),
     'L0_attn_conv_b': (0.0, 0.1),
     'L0_attn_ssm_norm_w': (1.0, 0.6),
     'L0_attn_norm2_w': (1.0, 0.2)}
    factors = {'L0_ffn_b1': 3.071}
    for name, (base, spread) in spreads.items():
        noise = np.random.default_rng([zlib.crc32(name.encode()), seed]).standard_normal(out[name].shape)
        drawn = base * np.exp(spread * noise) if base else spread * noise
        out[name] = jnp.asarray(drawn.astype(out[name].dtype))
    for name, factor in factors.items():
        out[name] = (out[name] * factor).astype(out[name].dtype)
    return out
```

```python
from contextlib import ExitStack

import concourse.bass as bass
from concourse import mybir

ALU = mybir.AluOpType
ACT = mybir.ActivationFunctionType
F32 = mybir.dt.float32
F32R = mybir.dt.float32r
U32 = mybir.dt.uint32

P = 128
IMAGES, LENGTH = 16, 36
T = IMAGES * LENGTH
D = 192
REST = D - P
PATCH_CHUNKS = 768 // P
INNER = 384
IC = INNER // P
STATE = 128
TAPS = 4
PROJ = 2 * INNER + 2 * STATE + 1
FF = 768
FC = FF // P
EXPERTS = 8
HID = 384
HC = HID // P
EPS = 1e-5

TILES = [(k * P, min(P, T - k * P)) for k in range((T + P - 1) // P)]
NT = len(TILES)
HALF_TILES = [range(0, 2), range(2, NT)]
HALVES = [(0, 2 * P), (2 * P, T - 2 * P)]
PER = 3
GROUP = PER * LENGTH
GROUPS = [(g * GROUP, min(GROUP, T - g * GROUP)) for g in range((T + GROUP - 1) // GROUP)]
NG = len(GROUPS)
FULL = T // GROUP
LAST = T - FULL * GROUP

B_, C_, X0 = 0, 1, 2
CONV_SRC = [3, 4, 0, 1, 2]
PROJ_COL = [INNER + P * s for s in CONV_SRC] + [P * j for j in range(IC)]
NQ = len(CONV_SRC)
ITEMS = [(0, 0), (1, 0), (2, 0), (3, 0), (0, 1), (1, 1), (2, 1), (3, 1)] + \
    [(q, h) for q in range(4, NQ + IC) for h in range(2)]

V_CONVW = 0
V_CONVB = V_CONVW + NQ * TAPS
V_N1A = V_CONVB + NQ
V_N1C = V_N1A + 1
V_N2A = V_N1C + 1
V_N2C = V_N2A + 1
V_SSM = V_N2C + 1
V_DTB = V_SSM + IC
V_ALOG = V_DTB + 1
V_D = V_ALOG + 1
V_WGA = V_D + 1
V_WGC = V_WGA + EXPERTS
V_ALL = V_WGC + EXPERTS

EXPERT_W1 = 2 * HID
EXPERT_W2 = HC * D
SPREAD = 32 + EXPERTS


def build(nc, patches, posbias, vectors, in_proj, out_proj, mlp1, mlp2, first, second, b2, out):
    with ExitStack() as ctx:
        def sb(name, shape, dt=F32):
            return ctx.enter_context(nc.sbuf_tensor(name, shape, dt))

        def sem(name):
            return ctx.enter_context(nc.semaphore(name))

        bank = [ctx.enter_context(nc.psum_tensor(f"bank{i}", [P, 512], F32)) for i in range(8)]
        TILE_BANK = bank[0:5]
        WORK = bank[5:8]
        TURN = [(bank[0][:, 0:256], bank[0][0:REST, 256:512]), (bank[2][:, 0:320], bank[3][0:REST, 0:320])]
        PROJ_RING = [bank[5], bank[6], bank[7], bank[1]]
        DT_ROW = [bank[4][0:1, 0:256], bank[0][0:1, 0:320]]
        DT_COL = bank[2]

        def scan_pair(n, m, first_bank, second_bank):
            return first_bank[0:m, n * GROUP:n * GROUP + m] if n < 4 else \
                second_bank[0:m, (n - 4) * GROUP:(n - 4) * GROUP + m]

        pt = sb("pt", [P, PATCH_CHUNKS, T + D])
        pos = sb("pos", [P, NT + 1, D])
        vec = sb("vec", [P, V_ALL])
        w_in = sb("w_in", [P, 2, PROJ])
        w_out = sb("w_out", [P, IC, D])
        w_m1 = sb("w_m1", [P, 2, FF])
        w_m2 = sb("w_m2", [P, FC, D])
        w_e1 = [sb(f"w_e1{s}", [P, EXPERT_W1 + HC]) for s in range(2)]
        w_e2 = [sb(f"w_e2{s}", [P, HC, D]) for s in range(2)]
        b2_sb = sb("b2_sb", [SPREAD, D])

        in_h = sb("in_h", [P, 2, PROJ], F32R)
        in_l = sb("in_l", [P, 2, PROJ], F32R)
        out_h = sb("out_h", [P, IC, D], F32R)
        out_l = sb("out_l", [P, IC, D], F32R)
        m1_h = sb("m1_h", [P, 2, FF], F32R)
        m1_l = sb("m1_l", [P, 2, FF], F32R)
        m2 = sb("m2", [P, FC, 2, D], F32R)
        e1_h = [sb(f"e1_h{s}", [P, 2, HID], F32R) for s in range(2)]
        e1_l = [sb(f"e1_l{s}", [P, 2, HID], F32R) for s in range(2)]
        e2 = [sb(f"e2{s}", [P, HC, 2, D], F32R) for s in range(2)]
        wg_h = sb("wg_h", [P, 2, EXPERTS], F32R)
        wg_l = sb("wg_l", [P, 2, EXPERTS], F32R)
        b2s = sb("b2s", [SPREAD, 2, D], F32R)

        ident = sb("ident", [P, P])
        upto = sb("upto", [GROUP, GROUP])
        after = sb("after", [GROUP, GROUP])
        skip = sb("skip", [GROUP, GROUP])
        ones = sb("ones", [P, 1])
        minus_half = sb("minus_half", [P, NT])
        column = sb("column", [P, EXPERTS])

        h0 = sb("h0", [P, NT, D])
        xln = sb("xln", [P, NT, D])
        rows = sb("rows", [P, NT, D])
        res = sb("res", [P, NT, D])
        acc = sb("acc", [P, NT, D])
        stats = sb("stats", [P, NT, 6])
        mv = sb("mv", [P, NT, 2])
        rstd = sb("rstd", [P, NT])
        ustd = sb("ustd", [P, NT])
        ss3 = sb("ss3", [P, NT])
        ss4 = sb("ss4", [P, NT])
        squares = sb("squares", [P, D])

        xa_h = sb("xa_h", [P, T], F32R)
        xa_l = sb("xa_l", [P, T], F32R)
        xc = sb("xc", [P, T], F32R)
        xraw = sb("xraw", [P, NQ, T])
        hid = sb("hid", [P, FC, T])
        conv = hid[:, 0:NQ, :]
        ctmp = hid[:, NQ, :]
        pt_flat = pt[:, :, :].rearrange("p c n -> p (c n)")
        zs = pt_flat[:, 0:IC * T].rearrange("p (c t) -> p c t", c=IC)
        yz = pt_flat[:, IC * T:2 * IC * T].rearrange("p (c t) -> p c t", c=IC)
        cb = pt_flat[:, 0:EXPERTS * T]
        yz2 = w_in[:, :, :].rearrange("p a n -> p (a n)")[:, 0:IC * T].rearrange("p (c t) -> p c t", c=IC)
        hid_h = sb("hid_h", [P, FC, T], F32R)
        hid_l = sb("hid_l", [P, FC, T], F32R)
        yz_h = hid_h[:, 0:IC, :]
        yz_l = hid_l[:, 0:IC, :]

        dt_row = sb("dt_row", [1, T])
        dtv = sb("dtv", [GROUP, NG])
        dt_abs = sb("dt_abs", [GROUP, NG])
        dt_exp = sb("dt_exp", [GROUP, NG])
        dt_ln = sb("dt_ln", [GROUP, NG])
        dt_pos = sb("dt_pos", [GROUP, NG])
        dt = sb("dt", [GROUP, NG])
        exp_a = sb("exp_a", [GROUP, 1])
        da = sb("da", [GROUP, NG])
        da_after, decay, mix = (
            t[0:GROUP, :, :].rearrange("p k n -> p (k n)")[:, 0:NG * GROUP].rearrange("p (g n) -> p g n", g=NG)
            for t in (rows, res, acc))
        xt = xraw[0:GROUP, :, :].rearrange("p q t -> p (q t)")[:, 0:NG * INNER].rearrange(
            "p (g c) -> p g c", g=NG)

        scoreT = rows[0:EXPERTS, :, :].rearrange("e k n -> e (k n)")[:, 0:T]
        cwT = res[0:EXPERTS, :, :].rearrange("e k n -> e (k n)")[:, 0:T]
        gate_rows = nc.dram_tensor("gate_rows", (EXPERTS, T), F32).ap()
        cs = sb("cs", [SPREAD, T], F32R)
        gs = sb("gs", [P, NT, EXPERTS])
        top = sb("top", [P, NT, EXPERTS])
        top_i = sb("top_i", [P, NT, EXPERTS], U32)
        top_f = sb("top_f", [P, NT, 2])
        gap = sb("gap", [P, NT])
        th = sb("th", [P, NT])
        prob = sb("prob", [P, NT, 2])
        share = sb("share", [P, NT, EXPERTS])
        share2 = sb("share2", [P, NT, EXPERTS])
        cw = sb("cw", [P, NT, EXPERTS])

        ld_patch = [sem(f"ld_patch{c}") for c in range(PATCH_CHUNKS)]
        ld_pos, ld_vec, ld_in, ld_out = sem("ld_pos"), sem("ld_vec"), sem("ld_in"), sem("ld_out")
        ld_m1, ld_m2, ld_b2 = sem("ld_m1"), sem("ld_m2"), sem("ld_b2")
        ld_e1 = [sem("ld_e10"), sem("ld_e11")]
        ld_e2 = [sem("ld_e20"), sem("ld_e21")]
        ld_cb0, ld_cb, st_gate = sem("ld_cb0"), sem("ld_cb"), sem("st_gate")
        stored = sem("stored")
        pool_own, act_own, dve_own = sem("pool_own"), sem("act_own"), sem("dve_own")
        consts, skip_ready, zeroed = sem("consts"), sem("skip_ready"), sem("zeroed")
        in_hi, in_lo = sem("in_hi"), sem("in_lo")
        out_hi, out_lo = sem("out_hi"), sem("out_lo")
        m1_hi, m1_lo = sem("m1_hi"), sem("m1_lo")
        m2_hi, m2_lo = sem("m2_hi"), sem("m2_lo")
        small_ready = sem("small_ready")
        ex_hi, ex_lo = sem("ex_hi"), sem("ex_lo")
        tok_done, h0_done = sem("tok_done"), sem("h0_done")
        base_ready, power_done = sem("base_ready"), sem("power_done")
        xln_done, rows_done = sem("xln_done"), sem("rows_done")
        turned, turned_hi, turned_lo = sem("turned"), sem("turned_hi"), sem("turned_lo")
        proj_done, proj_used = sem("proj_done"), sem("proj_used")
        dtr_done, dtr_read, dtc_done, dt_in, dt_soft = (sem("dtr_done"), sem("dtr_read"), sem("dtc_done"),
                                                        sem("dt_in"), sem("dt_soft"))
        a_ready, da_ready = sem("a_ready"), sem("da_ready")
        seg_done, exp_done, decay_done = sem("seg_done"), sem("exp_done"), sem("decay_done")
        conv_done, conv2_done = sem("conv_done"), sem("conv2_done")
        silu_done = sem("silu_done")
        g_done, mix_raw, mix_done = sem("g_done"), sem("mix_raw"), sem("mix_done")
        xt_done, xt_used = sem("xt_done"), sem("xt_used")
        y_done, yz_done, yz_hi, yz_lo, yz_sq = (sem("y_done"), sem("yz_done"), sem("yz_hi"),
                                                sem("yz_lo"), sem("yz_sq"))
        ss3_sum, ss3_base = sem("ss3_sum"), sem("ss3_base")
        out_done, res_done, ss4_done = sem("out_done"), sem("res_done"), sem("ss4_done")
        up_done, up_used = sem("up_done"), sem("up_used")
        scaled, hid_hi, hid_split = sem("scaled"), sem("hid_hi"), sem("hid_split")
        mlp_done, h1_half, h1_done = sem("mlp_done"), sem("h1_half"), sem("h1_done")
        gate_done, gate_read, score_done = sem("gate_done"), sem("gate_read"), sem("score_done")
        gs_done, gap_done, th_done, cw_done = (sem("gs_done"), sem("gap_done"), sem("th_done"),
                                               sem("cw_done"))
        cwT_done, cwT_hi, cwT_copy, cwT_lo = (sem("cwT_done"), sem("cwT_hi"), sem("cwT_copy"),
                                              sem("cwT_lo"))
        moe_done, sum_half, sum_done = sem("moe_done"), sem("sum_half"), sem("sum_done")

        MLP_UPS = 2 * FC
        UPS = 2 * HC
        PERIODS = EXPERTS - 2

        def w1_at(e):
            return 1 if isinstance(e, int) and e == 0 else e * 2

        def w2_at(e):
            return 2 * e + 2 if isinstance(e, int) and e == EXPERTS - 1 else e * 2 + 3

        POW_U, POW_X, POW_3, POW_4, POW_2 = 0, 2, 3, 3 + NT, 3 + NT + 2

        def work(n):
            return WORK[n % len(WORK)]

        def covering(k):
            return -(-(TILES[k][0] + TILES[k][1]) // GROUP)

        block = ctx.enter_context(nc.Block())

        @block.sync
        def _(sp):
            for c in range(PATCH_CHUNKS):
                sp.dma_start(pt[:, c, :], patches[c]).then_inc(ld_patch[c], 16)
                if c == 1:
                    sp.dma_start(vec[:, :], vectors).then_inc(ld_vec, 16)
                if c == 2:
                    sp.dma_start(w_in[:, :, :], in_proj).then_inc(ld_in, 16)
                if c == 4:
                    sp.dma_start(pos[:, :, :], posbias).then_inc(ld_pos, 16)
            sp.dma_start(w_out[:, :, :], out_proj).then_inc(ld_out, 16)
            sp.dma_start(b2_sb[0:EXPERTS, :], b2).then_inc(ld_b2, 16)
            sp.dma_start(b2_sb[32:SPREAD, :], b2).then_inc(ld_b2, 16)
            sp.dma_start(w_m1[:, :, :], mlp1).then_inc(ld_m1, 16)
            sp.dma_start(w_m2[:, :, :], mlp2).then_inc(ld_m2, 16)
            for e in range(2):
                sp.dma_start(w_e1[e][:, :], first[e]).then_inc(ld_e1[e], 16)
                sp.dma_start(w_e2[e][:, :, :], second[e]).then_inc(ld_e2[e], 16)
            sp.wait_ge(cwT_copy, 2)
            sp.dma_start(gate_rows[:, :], cwT).then_inc(st_gate, 16)
            sp.wait_ge(st_gate, 16)
            for e in range(EXPERTS):
                sp.dma_start(cb[:, e * T:(e + 1) * T], gate_rows[e:e + 1, :].broadcast_to([P, T]))\
                    .then_inc(ld_cb if e else ld_cb0, 16)
            with sp.Fori(0, PERIODS // 2) as i:
                for s in range(2):
                    sp.wait_ge(up_used, i * (2 * UPS) + (MLP_UPS + (s + 1) * UPS))
                    sp.dma_start(w_e1[s][:, :], first[bass.ds(i * 2 + (s + 2), 1), :, :].rearrange(
                        "a p n -> (a p) n")).then_inc(ld_e1[s], 16)
                    sp.wait_ge(ex_lo, i * 4 + (2 * s + 3))
                    sp.dma_start(w_e2[s][:, :, :].rearrange("p c n -> p (c n)"),
                                 second[bass.ds(i * 2 + (s + 2), 1), :, :].rearrange(
                                     "a p n -> (a p) n")).then_inc(ld_e2[s], 16)
            for k, (t0, m) in enumerate(TILES):
                sp.wait_ge(sum_done, k + 1)
                sp.dma_start(out[t0:t0 + m, :], acc[0:m, k, :]).then_inc(stored, 16)
            sp.wait_ge(stored, 16 * NT)

        @block.gpsimd
        def _(pool):
            own = [0]

            def link(ins):
                own[0] += 1
                ins.then_inc(pool_own, 1)
                pool.wait_ge(pool_own, own[0])

            g = nc.gpsimd

            def power(t, a, b):
                g.tensor_tensor(t[:, a:b], t[:, a:b], minus_half[:, 0:b - a], ALU.pow).then_inc(power_done, 1)

            link(g.memset(ident[:, :], 0.0))
            g.affine_select(out=ident[:, :], in_=ident[:, :], compare_op=ALU.not_equal, fill=1.0, base=0,
                            pattern=[[-1, P]], channel_multiplier=1).then_inc(consts, 1)
            g.memset(ones[:, :], 1.0).then_inc(consts, 1)
            g.memset(minus_half[:, :], -0.5).then_inc(consts, 1)
            for m, low, high in ((upto, (0, 0), (0, 1)), (after, (-1, -1), (LENGTH - 1, 0))):
                v = m[:, :].rearrange("r (j c) -> r j c", j=PER)
                link(g.memset(m[:, :], 1.0))
                link(g.affine_select(out=v, in_=v, compare_op=ALU.is_ge, fill=0.0, base=low[0],
                                     pattern=[[-LENGTH, PER], [low[1], LENGTH]], channel_multiplier=1))
                g.affine_select(out=v, in_=v, compare_op=ALU.is_ge, fill=0.0, base=high[0],
                                pattern=[[LENGTH, PER], [high[1], LENGTH]],
                                channel_multiplier=-1).then_inc(consts, 1)
            g.iota(column[:, :], pattern=[[1, EXPERTS]], base=0, channel_multiplier=0,
                   allow_small_or_imprecise_dtypes=True).then_inc(consts, 1)
            g.memset(cs[:, :].bitcast(F32), 0.0).then_inc(zeroed, 1)
            pool.wait_ge(ld_vec, 16)
            pool.wait_ge(consts, 6)
            g.tensor_scalar(skip[:, :], ident[0:GROUP, 0:GROUP], vec[0:GROUP, V_D:V_D + 1], 0.0, ALU.mult,
                            ALU.add).then_inc(skip_ready, 1)
            for n, tiles in enumerate(HALF_TILES):
                pool.wait_ge(base_ready, n + 1)
                power(ustd, tiles.start, tiles.stop)
            power(rstd, 0, NT)
            c2 = NQ - 1
            pool.wait_ge(proj_used, 2 * NQ)
            cv = conv[:, c2, :].rearrange("p (i l) -> p i l", i=IMAGES)
            xv = xraw[:, c2, :].rearrange("p (i l) -> p i l", i=IMAGES)
            tv = ctmp[:, :].rearrange("p (i l) -> p i l", i=IMAGES)
            w0 = V_CONVW + CONV_SRC[c2] * TAPS
            for k in range(1, TAPS):
                link(g.tensor_scalar(tv[:, :, k:], xv[:, :, 0:LENGTH - k],
                                     vec[:, w0 + TAPS - 1 - k:w0 + TAPS - k], 0.0, ALU.mult, ALU.add))
                ins = g.tensor_tensor(cv[:, :, k:], cv[:, :, k:], tv[:, :, k:], ALU.add)
                if k < TAPS - 1:
                    link(ins)
            ins.then_inc(conv2_done, 1)
            pool.wait_ge(exp_done, 3)
            g.tensor_tensor(decay[:, 0:FULL, :], decay[:, 0:FULL, :],
                            upto[:, :].rearrange("r (a c) -> r a c", a=1).broadcast_to([GROUP, FULL, GROUP]),
                            ALU.mult).then_inc(decay_done, 1)
            g.tensor_tensor(decay[0:LAST, FULL, 0:LAST], decay[0:LAST, FULL, 0:LAST], upto[0:LAST, 0:LAST],
                            ALU.mult).then_inc(decay_done, 1)
            for n, (t0, m) in enumerate(GROUPS):
                pool.wait_ge(mix_raw, n + 1)
                g.tensor_tensor(mix[0:m, n, 0:m], mix[0:m, n, 0:m], skip[0:m, 0:m], ALU.add)\
                    .then_inc(mix_done, 1)
            for n in range(NG + 1):
                if n < NG:
                    t0, m = GROUPS[n]
                    pool.wait_ge(yz_done, n + 1)
                    v = yz[:, :, t0:t0 + m]
                    g.tensor_tensor(yz2[:, :, t0:t0 + m], v, v, ALU.mult).then_inc(yz_sq, 1)
                for k in range(NT):
                    if covering(k) + 1 == n or (n == NG and covering(k) == NG):
                        pool.wait_ge(ss3_base, k + 1)
                        power(ss3, k, k + 1)
            for n, tiles in enumerate(HALF_TILES):
                pool.wait_ge(ss4_done, tiles.stop)
                s = ss4[:, tiles.start:tiles.stop]
                link(g.tensor_scalar(s, s, 1.0 / D, EPS, ALU.mult, ALU.add))
                power(ss4, tiles.start, tiles.stop)

            pool.wait_ge(m2_hi, 1)
            g.tensor_tensor(m2[:, :, 1, :], w_m2[:, :, :], m2[:, :, 0, :].bitcast(F32), ALU.subtract)\
                .then_inc(m2_lo, 1)

            def low1(s, count):
                pool.wait_ge(ex_hi, count)
                g.tensor_tensor(e1_l[s][:, :, :].rearrange("p a n -> p (a n)"), w_e1[s][:, 0:EXPERT_W1],
                                e1_h[s][:, :, :].rearrange("p a n -> p (a n)").bitcast(F32),
                                ALU.subtract).then_inc(ex_lo, 1)

            def low2(s, count):
                pool.wait_ge(ex_hi, count)
                g.tensor_tensor(e2[s][:, :, 1, :], w_e2[s][:, :, :], e2[s][:, :, 0, :].bitcast(F32),
                                ALU.subtract).then_inc(ex_lo, 1)

            low1(0, 1)
            low1(1, 2)
            low2(0, 3)
            for n, tiles in enumerate(HALF_TILES):
                pool.wait_ge(base_ready, 3 + n)
                power(rstd, tiles.start, tiles.stop)
            with pool.Fori(0, PERIODS // 2) as i:
                for s in range(2):
                    low1(s, i * 4 + (2 * s + 4))
                    low2(1 - s, i * 4 + (2 * s + 5))
            low2(1, w2_at(EXPERTS - 1))

        @block.scalar
        def _(act):
            a = nc.scalar
            own = [0]

            def link(ins):
                own[0] += 1
                ins.then_inc(act_own, 1)
                act.wait_ge(act_own, own[0])

            act.wait_ge(ld_vec, 16)
            a.activation(exp_a[:, :], vec[0:GROUP, V_ALOG:V_ALOG + 1], ACT.Exp).then_inc(a_ready, 1)
            act.wait_ge(ld_in, 16)
            for j, v in enumerate((V_N1A, V_N1C)):
                a.activation(in_h[:, j, :], w_in[:, j, :], ACT.Copy, scale=vec[:, v:v + 1]).then_inc(in_hi, 1)
            act.wait_ge(ld_out, 16)
            for c in range(IC):
                a.activation(out_h[:, c, :], w_out[:, c, :], ACT.Copy,
                             scale=vec[:, V_SSM + c:V_SSM + c + 1]).then_inc(out_hi, 1)

            def turn_high(n):
                t0, m = HALVES[n % 2]
                srcA, srcB = TURN[n % 2]
                act.wait_ge(turned, n + 1)
                a.copy(xa_h[:, t0:t0 + m], srcA).then_inc(turned_hi, 1)
                a.copy(xc[0:REST, t0:t0 + m], srcB).then_inc(turned_hi, 1)

            def take_item(n):
                q, h = ITEMS[n]
                t0, m = HALVES[h]
                src = PROJ_RING[n % 4][:, 0:m]
                act.wait_ge(proj_done, n + 1)
                if q >= NQ:
                    a.activation(zs[:, q - NQ, t0:t0 + m], src, ACT.Silu).then_inc(proj_used, 1)
                    return
                w = V_CONVW + CONV_SRC[q] * TAPS + TAPS - 1
                b = V_CONVB + CONV_SRC[q]
                a.copy(xraw[:, q, t0:t0 + m], src)
                a.activation(conv[:, q, t0:t0 + m], src, ACT.Identity, scale=vec[:, w:w + 1],
                             bias=vec[:, b:b + 1]).then_inc(proj_used, 1)

            turn_high(0)
            take_item(0)
            take_item(1)
            turn_high(1)
            for n in range(2, 6):
                take_item(n)
            act.wait_ge(dtr_done, 1)
            for (t0, m), src in zip(HALVES, DT_ROW):
                a.copy(dt_row[:, t0:t0 + m], src).then_inc(dtr_read, 1)
            take_item(6)
            take_item(7)
            act.wait_ge(dt_in, 1)
            link(a.activation(dt_abs[:, :], dtv[:, :], ACT.Abs))
            link(a.activation(dt_exp[:, :], dt_abs[:, :], ACT.Exp, scale=-1.0))
            a.activation(dt_ln[:, :], dt_exp[:, :], ACT.Ln, bias=1.0).then_inc(dt_soft, 1)
            take_item(8)
            take_item(9)
            act.wait_ge(seg_done, 1)
            a.activation(decay[:, 0:4, :].rearrange("p g t -> p (g t)"), bank[3][0:GROUP, 0:4 * GROUP],
                         ACT.Exp).then_inc(exp_done, 1)
            act.wait_ge(seg_done, 2)
            a.activation(decay[:, 4, :], bank[0][0:GROUP, 0:GROUP], ACT.Exp).then_inc(exp_done, 1)
            a.activation(decay[0:LAST, FULL, 0:LAST], bank[0][0:LAST, GROUP:GROUP + LAST], ACT.Exp)\
                .then_inc(exp_done, 1)

            def silu(q, ready, count):
                act.wait_ge(ready, count)
                a.activation(conv[:, q, :], conv[:, q, :], ACT.Silu).then_inc(silu_done, 1)

            take_item(10)
            take_item(11)
            silu(B_, conv_done, 1)
            silu(C_, conv_done, 2)
            for n in range(12, 16):
                take_item(n)
            silu(X0, conv_done, 3)
            silu(X0 + 1, conv_done, 4)
            silu(X0 + 2, conv2_done, 1)
            for n, (t0, m) in enumerate(GROUPS):
                act.wait_ge(xt_done, n + 1)
                a.copy(xt[0:m, n, :], work(n)[0:m, 0:INNER]).then_inc(xt_used, 1)
            act.wait_ge(ld_m1, 16)
            for j, v in enumerate((V_N2A, V_N2C)):
                a.activation(m1_h[:, j, :], w_m1[:, j, :], ACT.Copy, scale=vec[:, v:v + 1]).then_inc(m1_hi, 1)
            for n, (t0, m) in enumerate(GROUPS):
                act.wait_ge(yz_done, n + 1)
                a.copy(yz_h[:, :, t0:t0 + m], yz[:, :, t0:t0 + m]).then_inc(yz_hi, 1)
            act.wait_ge(ld_m2, 16)
            a.copy(m2[:, :, 0, :], w_m2[:, :, :]).then_inc(m2_hi, 1)
            for k, (t0, m) in enumerate(TILES):
                act.wait_ge(res_done, k + 1)
                if k:
                    act.wait_ge(ss4_done, k)
                a.activation(squares[0:m, :], res[0:m, k, :], ACT.Square, accum_out=ss4[0:m, k:k + 1])\
                    .then_inc(ss4_done, 1)

            def gelu(bk, chunk, h, ups, bias):
                t0, m = HALVES[h]
                act.wait_ge(up_done, ups)
                a.activation(hid[:, chunk, t0:t0 + m], bk[:, 0:m], ACT.Gelu, bias=bias)\
                    .then_inc(up_used, 1)

            turn_high(2)
            for n in range(MLP_UPS):
                gelu(work(n), n % FC, n // FC, n + 1, 0.0)
                if n == 2:
                    turn_high(3)

            def high1(s, loads):
                act.wait_ge(ld_e1[s], loads)
                a.copy(e1_h[s][:, :, :].rearrange("p a n -> p (a n)"), w_e1[s][:, 0:EXPERT_W1])\
                    .then_inc(ex_hi, 1)

            def high2(s, loads):
                act.wait_ge(ld_e2[s], loads)
                a.copy(e2[s][:, :, 0, :], w_e2[s][:, :, :]).then_inc(ex_hi, 1)

            high1(0, 16)
            high1(1, 16)
            high2(0, 16)
            turn_high(4)
            turn_high(5)
            act.wait_ge(gate_done, 1)
            for (t0, m), bk in zip(HALVES, (bank[1], bank[4])):
                a.copy(scoreT[:, t0:t0 + m], bk[0:EXPERTS, 0:m]).then_inc(gate_read, 1)

            def expert_gelu(s, j, ups):
                h, c = divmod(j, HC)
                gelu(work(j), s * HC + c, h, ups + (j + 1),
                     w_e1[s][:, EXPERT_W1 + c:EXPERT_W1 + c + 1])

            def expert_high(s, j, before):
                h, c = divmod(j, HC)
                t0, m = HALVES[h]
                act.wait_ge(scaled, before + (j + 1))
                a.copy(hid_h[:, s * HC + c, t0:t0 + m], hid[:, s * HC + c, t0:t0 + m]).then_inc(hid_hi, 1)

            for j in range(HC):
                expert_gelu(0, j, MLP_UPS)
            act.wait_ge(gap_done, 1)
            a.activation(th[:, :], gap[:, :], ACT.Tanh, scale=0.5).then_inc(th_done, 1)
            for j in range(HC, UPS):
                expert_gelu(0, j, MLP_UPS)
            act.wait_ge(cwT_done, 1)
            for t0, t1, bk in ((0, 512, bank[2]), (512, T, bank[3])):
                a.copy(cwT[:, t0:t1], bk[0:EXPERTS, 0:t1 - t0]).then_inc(cwT_copy, 1)
            act.wait_ge(zeroed, 1)
            for t0, t1, bk in ((0, 512, bank[2]), (512, T, bank[3])):
                a.copy(cs[0:EXPERTS, t0:t1], bk[0:EXPERTS, 0:t1 - t0]).then_inc(cwT_hi, 1)
            for j in range(UPS):
                expert_high(0, j, 0)

            def expert(s, before):
                for j in range(UPS + 1):
                    if j < UPS:
                        expert_gelu(s, j, before + MLP_UPS)
                    if j:
                        expert_high(s, j - 1, before)

            with act.Fori(0, PERIODS // 2) as i:
                for s in range(2):
                    expert(1 - s, i * (2 * UPS) + (s + 1) * UPS)
                    high1(s, i * 16 + 32)
                    high2(1 - s, i * 16 + (16 if s == 0 else 32))
            expert(1, (EXPERTS - 1) * UPS)
            high2(1, 16 * (EXPERTS // 2))

        @block.vector
        def _(dve):
            v = nc.vector
            own = [0]

            def step(ins):
                own[0] += 1
                ins.then_inc(dve_own, 1)

            def link(ins):
                step(ins)
                dve.wait_ge(dve_own, own[0])

            for small in (mv, rstd, ustd, ss3, ss4, gap, dtv, th):
                step(v.memset(small[:], 1.0))
            step(v.memset(top_i[:, :, :], 0))
            link(v.memset(b2s[:, :, :].bitcast(F32), 0.0))
            dve.wait_ge(ld_vec, 16)
            wg = vec[:, V_WGA:V_ALL].rearrange("p (a e) -> p a e", a=2)
            link(v.tensor_copy(wg_h[:, :, :], wg))
            v.tensor_tensor(wg_l[:, :, :], wg, wg_h[:, :, :].bitcast(F32), ALU.subtract).then_inc(small_ready, 1)
            for j, (w, r) in enumerate(((V_N1A, P), (V_N1C, REST))):
                dve.wait_ge(in_hi, j + 1)
                v.scalar_tensor_tensor(in_l[0:r, j, :], w_in[0:r, j, :], vec[0:r, w:w + 1],
                                       in_h[0:r, j, :].bitcast(F32), ALU.mult, ALU.subtract).then_inc(in_lo, 1)
            dve.wait_ge(ld_pos, 16)
            link(v.tensor_tensor(pos[:, 0:NT, :], pos[:, 0:NT, :],
                                 pos[:, NT:NT + 1, :].broadcast_to([P, NT, D]), ALU.add))

            def embed(k):
                m = TILES[k][1]
                dve.wait_ge(tok_done, k + 1)
                v.tensor_tensor(h0[0:m, k, :], TILE_BANK[k][0:m, 0:D], pos[0:m, k, :], ALU.add)\
                    .then_inc(h0_done, 1)

            def embed_stats(k, last):
                m = TILES[k][1]
                dve.wait_ge(h0_done, k + 1)
                link(v.bn_stats(stats[0:m, k, :], h0[0:m, k, :]))
                ins = v.bn_aggr(mv[0:m, k, :], stats[0:m, k, :])
                (link if last else step)(ins)

            def embed_base(tiles):
                a, b = tiles.start, tiles.stop
                v.tensor_scalar(ustd[:, a:b], mv[:, a:b, 1], 1.0 + EPS, EPS * EPS, ALU.mult, ALU.add)\
                    .then_inc(base_ready, 1)

            def embed_rows(n):
                dve.wait_ge(power_done, POW_U + n + 1)
                for k in HALF_TILES[n]:
                    m = TILES[k][1]
                    v.tensor_scalar(rows[0:m, k, :], h0[0:m, k, :], mv[0:m, k, 0:1], ustd[0:m, k:k + 1],
                                    ALU.subtract, ALU.mult).then_inc(rows_done, 1)

            def turn_low(n):
                t0, m = HALVES[n % 2]
                srcA, srcB = TURN[n % 2]
                dve.wait_ge(turned_hi, 2 * n + 2)
                v.tensor_tensor(xa_l[:, t0:t0 + m], srcA, xa_h[:, t0:t0 + m].bitcast(F32), ALU.subtract)\
                    .then_inc(turned_lo, 1)
                v.tensor_tensor(xc[REST:P, t0:t0 + m], srcB, xc[0:REST, t0:t0 + m].bitcast(F32),
                                ALU.subtract).then_inc(turned_lo, 1)

            embed(0)
            embed(1)
            embed_stats(0, False)
            embed_stats(1, True)
            embed_base(HALF_TILES[0])
            embed(2)
            embed_stats(2, False)
            embed_rows(0)
            embed(3)
            embed(4)
            embed_stats(3, False)
            embed_stats(4, True)
            v.tensor_scalar(rstd[:, :], mv[:, :, 1], EPS, None, ALU.add).then_inc(dve_own, 1)
            own[0] += 1
            dve.wait_ge(dve_own, own[0])
            embed_base(HALF_TILES[1])
            turn_low(0)
            embed_rows(1)
            dve.wait_ge(power_done, POW_X + 1)
            for k, (t0, m) in enumerate(TILES[0:2]):
                v.tensor_scalar(xln[0:m, k, :], h0[0:m, k, :], mv[0:m, k, 0:1], rstd[0:m, k:k + 1],
                                ALU.subtract, ALU.mult).then_inc(xln_done, 1)
            turn_low(1)
            for k in range(2, NT):
                m = TILES[k][1]
                v.tensor_scalar(xln[0:m, k, :], h0[0:m, k, :], mv[0:m, k, 0:1], rstd[0:m, k:k + 1],
                                ALU.subtract, ALU.mult).then_inc(xln_done, 1)
            for c in range(IC):
                dve.wait_ge(out_hi, c + 1)
                v.scalar_tensor_tensor(out_l[:, c, :], w_out[:, c, :], vec[:, V_SSM + c:V_SSM + c + 1],
                                       out_h[:, c, :].bitcast(F32), ALU.mult, ALU.subtract).then_inc(out_lo, 1)

            def taps(qs, items):
                for k in range(1, TAPS):
                    for q, item in zip(qs, items):
                        cv = conv[:, q, :].rearrange("p (i l) -> p i l", i=IMAGES)
                        xv = xraw[:, q, :].rearrange("p (i l) -> p i l", i=IMAGES)
                        w = V_CONVW + CONV_SRC[q] * TAPS + TAPS - 1 - k
                        if k == 1:
                            dve.wait_ge(proj_used, item)
                        else:
                            dve.wait_ge(dve_own, own[0] - (len(qs) - 1))
                        ins = v.scalar_tensor_tensor(cv[:, :, k:], xv[:, :, 0:LENGTH - k], vec[:, w:w + 1],
                                                     cv[:, :, k:], ALU.mult, ALU.add)
                        if k < TAPS - 1:
                            step(ins)
                        else:
                            ins.then_inc(conv_done, 1)
                            if q != qs[-1]:
                                dve.wait_ge(dve_own, own[0])

            taps((B_, C_), (5, 6))
            dve.wait_ge(dtc_done, 1)
            step(v.tensor_scalar(dtv[:, 0:FULL], DT_COL[0:GROUP, 0:FULL], vec[0:GROUP, V_DTB:V_DTB + 1], None,
                                 ALU.add))
            dve.wait_ge(dve_own, own[0])
            v.tensor_scalar(dtv[0:LAST, FULL:NG], DT_COL[0:LAST, FULL:NG], vec[0:LAST, V_DTB:V_DTB + 1], None,
                            ALU.add).then_inc(dt_in, 1)
            dve.wait_ge(dt_in, 1)
            link(v.tensor_scalar(dt_pos[:, :], dtv[:, :], 0.0, None, ALU.max))
            dve.wait_ge(dt_soft, 1)
            link(v.tensor_tensor(dt[:, :], dt_pos[:, :], dt_ln[:, :], ALU.add))
            dve.wait_ge(a_ready, 1)
            link(v.tensor_scalar(da[:, :], dt[:, :], exp_a[:, 0:1], -1.0, ALU.mult, ALU.mult))
            dve.wait_ge(consts, 6)
            for n in range(NG):
                v.tensor_scalar(da_after[:, n, :], after[:, :], da[:, n:n + 1], None, ALU.mult)\
                    .then_inc(da_ready, 1)
            taps((X0, X0 + 1), (7, 8))
            for n, (t0, m) in enumerate(GROUPS):
                dve.wait_ge(g_done, 1 if n < 4 else 2)
                dve.wait_ge(decay_done, 2 if n == FULL else 1)
                v.scalar_tensor_tensor(mix[0:m, n, 0:m], scan_pair(n, m, bank[4], bank[2]), dt[0:m, n:n + 1],
                                       decay[0:m, n, 0:m], ALU.mult, ALU.mult).then_inc(mix_raw, 1)
            for n in range(NG + 2):
                if n < NG:
                    t0, m = GROUPS[n]
                    dve.wait_ge(y_done, n + 1)
                    src = work(n)[:, 0:IC * m].rearrange("p (c t) -> p c t", c=IC)
                    v.tensor_tensor(yz[:, :, t0:t0 + m], src, zs[:, :, t0:t0 + m], ALU.mult)\
                        .then_inc(yz_done, 1)
                if 1 <= n <= NG:
                    t0, m = GROUPS[n - 1]
                    dve.wait_ge(yz_hi, n)
                    v.tensor_tensor(yz_l[:, :, t0:t0 + m], yz[:, :, t0:t0 + m],
                                    yz_h[:, :, t0:t0 + m].bitcast(F32), ALU.subtract).then_inc(yz_lo, 1)
                for k in range(NT):
                    if covering(k) + 1 == n:
                        m = TILES[k][1]
                        dve.wait_ge(ss3_sum, k + 1)
                        v.tensor_scalar(ss3[0:m, k:k + 1], TILE_BANK[k][0:m, 0:1], 1.0 / INNER, EPS, ALU.mult,
                                        ALU.add).then_inc(ss3_base, 1)
                        if k == 0:
                            dve.wait_ge(ld_b2, 32)
                            for r in (0, 32):
                                step(v.tensor_copy(b2s[r:r + EXPERTS, 0, :], b2_sb[r:r + EXPERTS, :]))
                            dve.wait_ge(dve_own, own[0])
                            v.tensor_tensor(b2s[0:EXPERTS, 1, :], b2_sb[0:EXPERTS, :],
                                            b2s[0:EXPERTS, 0, :].bitcast(F32), ALU.subtract)\
                                .then_inc(small_ready, 1)
            for j, (w, r) in enumerate(((V_N2A, P), (V_N2C, REST))):
                dve.wait_ge(m1_hi, j + 1)
                v.scalar_tensor_tensor(m1_l[0:r, j, :], w_m1[0:r, j, :], vec[0:r, w:w + 1],
                                       m1_h[0:r, j, :].bitcast(F32), ALU.mult, ALU.subtract).then_inc(m1_lo, 1)

            def residual(k):
                m = TILES[k][1]
                dve.wait_ge(power_done, POW_3 + k + 1)
                dve.wait_ge(out_done, k + 1)
                v.scalar_tensor_tensor(res[0:m, k, :], TILE_BANK[k][0:m, 0:D], ss3[0:m, k:k + 1],
                                       xln[0:m, k, :], ALU.mult, ALU.add).then_inc(res_done, 1)

            def mlp_rows(n):
                dve.wait_ge(power_done, POW_4 + n + 1)
                for k in HALF_TILES[n]:
                    m = TILES[k][1]
                    v.tensor_scalar(rows[0:m, k, :], res[0:m, k, :], ss4[0:m, k:k + 1], None, ALU.mult)\
                        .then_inc(rows_done, 1)

            dve.wait_ge(xln_done, NT)
            for k in range(NT):
                residual(k)
            mlp_rows(0)
            mlp_rows(1)
            turn_low(2)

            def split_hidden(n):
                h, c = divmod(n, FC)
                t0, m = HALVES[h]
                dve.wait_ge(up_used, n + 1)
                link(v.tensor_copy(hid_h[:, c, t0:t0 + m], hid[:, c, t0:t0 + m]))
                v.tensor_tensor(hid_l[:, c, t0:t0 + m], hid[:, c, t0:t0 + m],
                                hid_h[:, c, t0:t0 + m].bitcast(F32), ALU.subtract).then_inc(hid_split, 1)

            for n in range(MLP_UPS):
                split_hidden(n)
                if n == 2:
                    turn_low(3)

            for n, tiles in enumerate(HALF_TILES):
                for k in tiles:
                    m = TILES[k][1]
                    dve.wait_ge(mlp_done, k + 1)
                    v.tensor_tensor(acc[0:m, k, :], TILE_BANK[k][0:m, 0:D], h0[0:m, k, :], ALU.add)\
                        .then_inc(h1_half, 1)
                    dve.wait_ge(h1_half, k + 1)
                    v.tensor_tensor(acc[0:m, k, :], TILE_BANK[k][0:m, D:2 * D], acc[0:m, k, :], ALU.add)\
                        .then_inc(h1_done, 1)
                    dve.wait_ge(h1_done, k + 1)
                    link(v.bn_stats(stats[0:m, k, :], acc[0:m, k, :]))
                    link(v.bn_aggr(mv[0:m, k, :], stats[0:m, k, :]))
                a, b = tiles.start, tiles.stop
                v.tensor_scalar(rstd[:, a:b], mv[:, a:b, 1], EPS, None, ALU.add).then_inc(base_ready, 1)
                if n == 0:
                    dve.wait_ge(power_done, POW_2 + 1)
                    for k in tiles:
                        m = TILES[k][1]
                        v.tensor_scalar(rows[0:m, k, :], acc[0:m, k, :], mv[0:m, k, 0:1], rstd[0:m, k:k + 1],
                                        ALU.subtract, ALU.mult).then_inc(rows_done, 1)
            turn_low(4)
            dve.wait_ge(power_done, POW_2 + 2)
            for k in HALF_TILES[1]:
                m = TILES[k][1]
                v.tensor_scalar(rows[0:m, k, :], acc[0:m, k, :], mv[0:m, k, 0:1], rstd[0:m, k:k + 1],
                                ALU.subtract, ALU.mult).then_inc(rows_done, 1)
            turn_low(5)

            dve.wait_ge(score_done, 1)
            v.tensor_copy(gs[:, 0:NT - 1, :].rearrange("p k e -> p (k e)"), bank[0][:, 0:(NT - 1) * EXPERTS])\
                .then_inc(gs_done, 1)
            m = TILES[-1][1]
            v.tensor_copy(gs[0:m, NT - 1, :], bank[0][0:m, (NT - 1) * EXPERTS:NT * EXPERTS])\
                .then_inc(gs_done, 1)
            dve.wait_ge(gs_done, 2)
            for k, (t0, m) in enumerate(TILES):
                step(v.max(top[0:m, k, :], gs[0:m, k, :]))
            dve.wait_ge(dve_own, own[0])
            for k, (t0, m) in enumerate(TILES):
                step(v.tensor_tensor(gap[0:m, k:k + 1], top[0:m, k, 0:1], top[0:m, k, 1:2], ALU.subtract))
            dve.wait_ge(dve_own, own[0])
            for k, (t0, m) in enumerate(TILES):
                ins = v.max_index(top_i[0:m, k, :], top[0:m, k, :], gs[0:m, k, :])
                if k == 0:
                    ins.then_inc(gap_done, 1)
                else:
                    step(ins)
            dve.wait_ge(dve_own, own[0])
            dve.wait_ge(gap_done, 1)
            step(v.tensor_copy(top_f[:, :, :], top_i[:, :, 0:2]))
            dve.wait_ge(th_done, 1)
            step(v.tensor_scalar(prob[:, :, 0], th[:, :], 0.5, 0.5, ALU.mult, ALU.add))
            link(v.tensor_scalar(prob[:, :, 1], th[:, :], -0.5, 0.5, ALU.mult, ALU.add))
            for k in range(NT):
                for j, to in enumerate((share, share2)):
                    step(v.tensor_scalar(to[:, k, :], column[:, :], top_f[:, k, j:j + 1], prob[:, k, j:j + 1],
                                         ALU.is_equal, ALU.mult))
            dve.wait_ge(dve_own, own[0])
            v.tensor_tensor(cw[:, :, :], share[:, :, :], share2[:, :, :], ALU.add).then_inc(cw_done, 1)
            dve.wait_ge(cwT_hi, 2)
            for t0, t1, bk in ((0, 512, bank[2]), (512, T, bank[3])):
                v.tensor_tensor(cs[32:SPREAD, t0:t1], bk[0:EXPERTS, 0:t1 - t0],
                                cs[0:EXPERTS, t0:t1].bitcast(F32), ALU.subtract).then_inc(cwT_lo, 1)

            def expert(e, s, before):
                for j in range(UPS + 1):
                    if j < UPS:
                        h, c = divmod(j, HC)
                        t0, m = HALVES[h]
                        weight = cb[:, e * T + t0:e * T + t0 + m] if isinstance(e, int) \
                            else cb[:, bass.ds(e * T + t0, m)]
                        dve.wait_ge(up_used, before + (MLP_UPS + j + 1))
                        v.tensor_tensor(hid[:, s * HC + c, t0:t0 + m], hid[:, s * HC + c, t0:t0 + m], weight,
                                        ALU.mult).then_inc(scaled, 1)
                    if j:
                        h, c = divmod(j - 1, HC)
                        t0, m = HALVES[h]
                        dve.wait_ge(hid_hi, before + j)
                        v.tensor_tensor(hid_l[:, s * HC + c, t0:t0 + m], hid[:, s * HC + c, t0:t0 + m],
                                        hid_h[:, s * HC + c, t0:t0 + m].bitcast(F32), ALU.subtract)\
                            .then_inc(hid_split, 1)

            dve.wait_ge(ld_cb0, 16)
            expert(0, 0, 0)
            dve.wait_ge(ld_cb, 16 * (EXPERTS - 1))
            with dve.Fori(0, PERIODS // 2) as i:
                for s in range(2):
                    expert(i * 2 + (s + 1), 1 - s, i * (2 * UPS) + (s + 1) * UPS)
            expert(EXPERTS - 1, 1, (EXPERTS - 1) * UPS)
            for k, (t0, m) in enumerate(TILES):
                dve.wait_ge(moe_done, k + 1)
                v.tensor_tensor(acc[0:m, k, :], TILE_BANK[k][0:m, 0:D], acc[0:m, k, :], ALU.add)\
                    .then_inc(sum_half, 1)
                dve.wait_ge(sum_half, k + 1)
                v.tensor_tensor(acc[0:m, k, :], TILE_BANK[k][0:m, D:2 * D], acc[0:m, k, :], ALU.add)\
                    .then_inc(sum_done, 1)

        @block.tensor
        def _(pe):
            mm = nc.tensor.matmul
            turn_to = nc.tensor.transpose
            for c in range(PATCH_CHUNKS):
                pe.wait_ge(ld_patch[c], 16)
                for k, (t0, m) in enumerate(TILES):
                    ins = mm(TILE_BANK[k][0:m, 0:D], pt[:, c, t0:t0 + m], pt[:, c, T:T + D],
                             start=(c == 0), stop=(c == PATCH_CHUNKS - 1))
                    if c == PATCH_CHUNKS - 1:
                        ins.then_inc(tok_done, 1)

            def turn(n):
                at0, width = HALVES[n % 2]
                toA, toB = TURN[n % 2]
                for k in HALF_TILES[n % 2]:
                    t0, m = TILES[k]
                    at = t0 - at0
                    pe.wait_ge(rows_done, NT * (n // 2) + k + 1)
                    turn_to(toA[:, at:at + m], rows[0:m, k, 0:P], ident[0:m, 0:m])
                    ins = turn_to(toB[:, at:at + m], rows[0:m, k, P:D], ident[0:m, 0:m])
                ins.then_inc(turned, 1)

            def product192(dst, w_h, w_l, c0, n, t0, m):
                wah, wch = w_h[:, 0, c0:c0 + n], w_h[:, 1, c0:c0 + n]
                wal, wcl = w_l[:, 0, c0:c0 + n], w_l[0:REST, 1, c0:c0 + n]
                mm(dst, wah, xa_h[:, t0:t0 + m], start=True, stop=False)
                mm(dst, wah, xa_l[:, t0:t0 + m], start=False, stop=False)
                mm(dst, wal, xa_h[:, t0:t0 + m], start=False, stop=False)
                mm(dst, wch, xc[:, t0:t0 + m], start=False, stop=False)
                return mm(dst, wcl, xc[0:REST, t0:t0 + m], start=False, stop=True)

            def item(n):
                q, h = ITEMS[n]
                t0, m = HALVES[h]
                if n >= 4:
                    pe.wait_ge(proj_used, n - 3)
                product192(PROJ_RING[n % 4][:, 0:m], in_h, in_l, PROJ_COL[q], P, t0, m).then_inc(proj_done, 1)

            pe.wait_ge(consts, 6)
            turn(0)
            pe.wait_ge(in_lo, 2)
            pe.wait_ge(turned_lo, 2)
            item(0)
            item(1)
            turn(1)
            item(2)
            item(3)
            pe.wait_ge(turned_lo, 4)
            item(4)
            item(5)
            for (t0, m), dst in zip(HALVES, DT_ROW):
                ins = product192(dst, in_h, in_l, PROJ - 1, 1, t0, m)
            ins.then_inc(dtr_done, 1)
            item(6)
            item(7)
            pe.wait_ge(dtr_read, 2)
            for n, (t0, m) in enumerate(GROUPS):
                ins = mm(DT_COL[0:m, n:n + 1], dt_row[:, t0:t0 + m], ones[0:1, :], start=True, stop=True)
            ins.then_inc(dtc_done, 1)
            item(8)
            item(9)
            for n, (t0, m) in enumerate(GROUPS):
                pe.wait_ge(da_ready, n + 1)
                ins = mm(scan_pair(n, m, bank[3], bank[0]), da_after[0:m, n, 0:m], upto[0:m, 0:m],
                         start=True, stop=True)
                if n in (3, NG - 1):
                    ins.then_inc(seg_done, 1)
            for n in range(10, len(ITEMS)):
                item(n)
            pe.wait_ge(silu_done, 2)
            for n, (t0, m) in enumerate(GROUPS):
                ins = mm(scan_pair(n, m, bank[4], bank[2]), conv[:, B_, t0:t0 + m], conv[:, C_, t0:t0 + m],
                         start=True, stop=True)
                if n in (3, NG - 1):
                    ins.then_inc(g_done, 1)
            pe.wait_ge(silu_done, 5)
            pe.wait_ge(proj_used, len(ITEMS))
            for n, (t0, m) in enumerate(GROUPS):
                if n >= 3:
                    pe.wait_ge(xt_used, n - 2)
                for c in range(IC):
                    ins = turn_to(work(n)[0:m, c * P:(c + 1) * P], conv[:, X0 + c, t0:t0 + m], ident[:, :])
                ins.then_inc(xt_done, 1)

            def mixed(n):
                t0, m = GROUPS[n]
                pe.wait_ge(xt_used, min(n + 4, NG))
                pe.wait_ge(mix_done, n + 1)
                if n >= 3:
                    pe.wait_ge(yz_done, n - 2)
                for c in range(IC):
                    ins = mm(work(n)[:, c * m:(c + 1) * m], xt[0:m, n, c * P:(c + 1) * P],
                             mix[0:m, n, 0:m], start=True, stop=True)
                ins.then_inc(y_done, 1)

            def square_sum(k):
                t0, m = TILES[k]
                pe.wait_ge(yz_sq, covering(k))
                for c in range(IC):
                    ins = mm(TILE_BANK[k][0:m, 0:1], yz2[:, c, t0:t0 + m], ones[:, :], start=(c == 0),
                             stop=(c == IC - 1))
                ins.then_inc(ss3_sum, 1)

            def output(k):
                t0, m = TILES[k]
                pe.wait_ge(ss3_base, k + 1)
                pe.wait_ge(yz_lo, covering(k))
                dst = TILE_BANK[k][0:m, 0:D]
                for c in range(IC):
                    mm(dst, yz_h[:, c, t0:t0 + m], out_h[:, c, :], start=(c == 0), stop=False)
                    mm(dst, yz_h[:, c, t0:t0 + m], out_l[:, c, :], start=False, stop=False)
                    ins = mm(dst, yz_l[:, c, t0:t0 + m], out_h[:, c, :], start=False, stop=(c == IC - 1))
                ins.then_inc(out_done, 1)

            mixed(0)
            mixed(1)
            mixed(2)
            pe.wait_ge(exp_done, 3)
            pe.wait_ge(mix_raw, NG)
            pe.wait_ge(out_lo, IC)
            square_sum(0)
            mixed(3)
            square_sum(1)
            output(0)
            mixed(4)
            square_sum(2)
            output(1)
            mixed(5)
            square_sum(3)
            output(2)
            square_sum(4)
            output(3)
            output(4)

            def down(k, w, chunks, chunk0, start, stop):
                t0, m = TILES[k]
                both, high = TILE_BANK[k][0:m, 0:2 * D], TILE_BANK[k][0:m, 0:D]
                for c in range(chunks):
                    pair = w[:, c, :, :].rearrange("p a n -> p (a n)")
                    mm(both, hid_h[:, chunk0 + c, t0:t0 + m], pair, start=start and c == 0, stop=False)
                    ins = mm(high, hid_l[:, chunk0 + c, t0:t0 + m], w[:, c, 0, :], start=False,
                             stop=stop and c == chunks - 1)
                return ins

            turn(2)
            pe.wait_ge(m1_lo, 2)
            pe.wait_ge(turned_lo, 6)
            for n in range(MLP_UPS):
                h, c = divmod(n, FC)
                t0, m = HALVES[h]
                if n == 3:
                    turn(3)
                if n == FC:
                    pe.wait_ge(turned_lo, 8)
                if n >= 3:
                    pe.wait_ge(up_used, n - 2)
                product192(work(n)[:, 0:m], m1_h, m1_l, c * P, P, t0, m).then_inc(up_done, 1)
            pe.wait_ge(m2_lo, 1)
            for k in range(NT):
                pe.wait_ge(hid_split, FC if k in HALF_TILES[0] else 2 * FC)
                down(k, m2, FC, 0, True, True).then_inc(mlp_done, 1)
            turn(4)
            turn(5)
            pe.wait_ge(small_ready, 2)
            pe.wait_ge(turned_lo, 12)
            for (t0, m), bk in zip(HALVES, (bank[1], bank[4])):
                ins = product192(bk[0:EXPERTS, 0:m], wg_h, wg_l, 0, EXPERTS, t0, m)
            ins.then_inc(gate_done, 1)

            def up(s, j, before):
                h, c = divmod(j, HC)
                t0, m = HALVES[h]
                pe.wait_ge(up_used, before + (MLP_UPS + j - 2))
                product192(work(j)[:, 0:m], e1_h[s], e1_l[s], c * P, P, t0, m).then_inc(up_done, 1)

            pe.wait_ge(ex_lo, w1_at(0))
            for j in range(HC):
                up(0, j, 0)
            pe.wait_ge(gate_read, 2)
            for k, (t0, m) in enumerate(TILES):
                ins = turn_to(bank[0][0:m, k * EXPERTS:(k + 1) * EXPERTS], scoreT[:, t0:t0 + m],
                              ident[0:EXPERTS, 0:EXPERTS])
            ins.then_inc(score_done, 1)
            for j in range(HC, UPS):
                up(0, j, 0)
            pe.wait_ge(cw_done, 1)
            for k, (t0, m) in enumerate(TILES):
                ins = turn_to(bank[2 + t0 // 512][0:EXPERTS, t0 % 512:t0 % 512 + m], cw[0:m, k, :],
                              ident[0:m, 0:m])
            ins.then_inc(cwT_done, 1)

            def up_all(s, before, split):
                pe.wait_ge(ex_lo, split)
                for j in range(UPS):
                    up(s, j, before)

            def down_all(s, before, split, stop):
                pe.wait_ge(ex_lo, split)
                for k in range(NT):
                    if k in (0, HALF_TILES[1].start):
                        pe.wait_ge(hid_split, before + (MLP_UPS + (HC if k == 0 else UPS)))
                    ins = down(k, e2[s], HC, s * HC, False, stop)
                    if stop:
                        ins.then_inc(moe_done, 1)

            up_all(1, UPS, w1_at(1))
            pe.wait_ge(cwT_lo, 2)
            for k, (t0, m) in enumerate(TILES):
                mm(TILE_BANK[k][0:m, 0:2 * D], cs[:, t0:t0 + m], b2s[:, :, :].rearrange("e a n -> e (a n)"),
                   start=True, stop=False)
            down_all(0, 0, w2_at(0), False)
            with pe.Fori(0, PERIODS // 2) as i:
                for s in range(2):
                    up_all(s, i * (2 * UPS) + (s + 2) * UPS, i * 4 + (2 * s + 4))
                    down_all(1 - s, i * (2 * UPS) + (s + 1) * UPS, i * 4 + (2 * s + 5), False)
            down_all(1, (EXPERTS - 1) * UPS, w2_at(EXPERTS - 1), True)


def _position_ids():
    import numpy as np
    side, n = 32, 6
    boundaries = np.arange(1.0 / side, 1.0, 1.0 / side, dtype=np.float32)
    frac = np.arange(0.0, 1.0 - 1e-06, 1.0 / n, dtype=np.float32)
    at = np.searchsorted(boundaries, frac, side="right")
    return (at[:, None] * side + at).reshape(-1)


def kernel(**inputs):
    import numpy as np
    import concourse.bacc as bacc
    from concourse.bass_utils import run_bass_kernel_spmd

    x = {n: np.asarray(a) for n, a in inputs.items()}

    def spread(v):
        return np.broadcast_to(np.reshape(v, (1, -1)), (P, np.size(v)))

    def twice(w):
        rest = w[P:D]
        return np.stack([w[0:P], np.concatenate([rest, rest])], axis=1)

    def chunked(w):
        return np.reshape(w, (-1, P, w.shape[1])).transpose(1, 0, 2)

    patches = x["x"].reshape(IMAGES, 3, 6, 16, 6, 16).transpose(1, 3, 5, 0, 2, 4)
    patches = patches.reshape(PATCH_CHUNKS, P, T)
    tok_w = x["L0_tok_conv_w"].reshape(D, PATCH_CHUNKS, P).transpose(1, 2, 0)
    pos = x["L0_tok_pos_table"][_position_ids()]
    pos = np.concatenate([pos] * IMAGES + [np.zeros((NT * P - T, D), np.float32)])
    posbias = np.concatenate([chunked(pos), np.broadcast_to(x["L0_tok_conv_b"], (P, 1, D))], axis=1)
    column = lambda v: np.reshape(v, (P, 1))
    vectors = np.concatenate([
        np.reshape(x["L0_attn_conv_w"], (NQ, P, TAPS)).transpose(1, 0, 2).reshape(P, NQ * TAPS),
        np.reshape(x["L0_attn_conv_b"], (NQ, P)).T,
        twice(x["L0_attn_norm1_w"][:, None])[:, :, 0],
        twice(x["L0_attn_norm2_w"][:, None])[:, :, 0],
        np.reshape(x["L0_attn_ssm_norm_w"], (IC, P)).T,
        spread(x["L0_attn_dt_bias"]), spread(x["L0_attn_A_log"]), spread(x["L0_attn_D"]),
        twice(x["L0_ffn_Wg"]).reshape(P, 2 * EXPERTS)], axis=1)
    first = np.stack([np.concatenate([
        twice(x["L0_ffn_W1"][e]).reshape(P, EXPERT_W1),
        np.reshape(x["L0_ffn_b1"][e], (HC, P)).T], axis=1) for e in range(EXPERTS)])
    arrays = {
        "patches": np.concatenate([patches, tok_w], axis=2),
        "posbias": posbias,
        "vectors": vectors,
        "in_proj": twice(x["L0_attn_in_proj_W"]),
        "out_proj": chunked(x["L0_attn_out_proj_W"]),
        "mlp1": twice(x["L0_attn_mlp_W1"]),
        "mlp2": chunked(x["L0_attn_mlp_W2"]).reshape(P, FC * D),
        "first": first,
        "second": np.stack([chunked(w).reshape(P, EXPERT_W2) for w in x["L0_ffn_W2"]]),
        "b2": x["L0_ffn_b2"],
    }
    nc = bacc.Bacc("TRN2", target_bir_lowering=False, num_devices=1)
    sent, args = {}, []
    for name, a in arrays.items():
        sent[f"in_{name}"] = np.ascontiguousarray(a)
        args.append(nc.dram_tensor(f"in_{name}", a.shape, mybir.dt.from_np(a.dtype), kind="ExternalInput").ap())
    args.append(nc.dram_tensor("out_0", (T, D), F32, kind="ExternalOutput").ap())
    build(nc, *args)
    r = run_bass_kernel_spmd(nc, [sent], core_ids=[0])
    return np.reshape(r.results[0]["out_0"], (IMAGES, LENGTH, D))
```

```python
from contextlib import ExitStack

import concourse.bass as bass
from concourse import mybir

ALU = mybir.AluOpType
ACT = mybir.ActivationFunctionType
F32 = mybir.dt.float32
F32R = mybir.dt.float32r
U32 = mybir.dt.uint32

P = 128
IMAGES, LENGTH = 16, 36
T = IMAGES * LENGTH
D = 192
REST = D - P
PATCH_CHUNKS = 768 // P
INNER = 384
IC = INNER // P
STATE = 128
TAPS = 4
PROJ = 2 * INNER + 2 * STATE + 1
FF = 768
FC = FF // P
EXPERTS = 8
HID = 384
HC = HID // P
EPS = 1e-5

TILES = [(k * P, min(P, T - k * P)) for k in range((T + P - 1) // P)]
NT = len(TILES)
HALF_TILES = [range(0, 2), range(2, NT)]
HALVES = [(0, 2 * P), (2 * P, T - 2 * P)]
PER = 3
GROUP = PER * LENGTH
GROUPS = [(g * GROUP, min(GROUP, T - g * GROUP)) for g in range((T + GROUP - 1) // GROUP)]
NG = len(GROUPS)
FULL = T // GROUP
LAST = T - FULL * GROUP

B_, C_, X0 = 0, 1, 2
CONV_SRC = [3, 4, 0, 1, 2]
PROJ_COL = [INNER + P * s for s in CONV_SRC] + [P * j for j in range(IC)]
NQ = len(CONV_SRC)
ITEMS = [(0, 0), (1, 0), (2, 0), (3, 0), (0, 1), (1, 1), (2, 1), (3, 1)] + \
    [(q, h) for q in range(4, NQ + IC) for h in range(2)]

V_CONVW = 0
V_CONVB = V_CONVW + NQ * TAPS
V_N1A = V_CONVB + NQ
V_N1C = V_N1A + 1
V_N2A = V_N1C + 1
V_N2C = V_N2A + 1
V_SSM = V_N2C + 1
V_DTB = V_SSM + IC
V_ALOG = V_DTB + 1
V_D = V_ALOG + 1
V_WGA = V_D + 1
V_WGC = V_WGA + EXPERTS
V_ALL = V_WGC + EXPERTS

EXPERT_W1 = 2 * HID
EXPERT_W2 = HC * D
SPREAD = 32 + EXPERTS


def build(nc, patches, posbias, vectors, in_proj, out_proj, mlp1, mlp2, first, second, b2, out):
    with ExitStack() as ctx:
        def sb(name, shape, dt=F32):
            return ctx.enter_context(nc.sbuf_tensor(name, shape, dt))

        def sem(name):
            return ctx.enter_context(nc.semaphore(name))

        bank = [ctx.enter_context(nc.psum_tensor(f"bank{i}", [P, 512], F32)) for i in range(8)]
        TILE_BANK = bank[0:5]
        WORK = bank[5:8]
        TURN = [(bank[0][:, 0:256], bank[0][0:REST, 256:512]), (bank[2][:, 0:320], bank[3][0:REST, 0:320])]
        PROJ_RING = [bank[5], bank[6], bank[7], bank[1]]
        DT_ROW = [bank[4][0:1, 0:256], bank[0][0:1, 0:320]]
        DT_COL = bank[2]

        def scan_pair(n, m, first_bank, second_bank):
            return first_bank[0:m, n * GROUP:n * GROUP + m] if n < 4 else \
                second_bank[0:m, (n - 4) * GROUP:(n - 4) * GROUP + m]

        pt = sb("pt", [P, PATCH_CHUNKS, T + D])
        pos = sb("pos", [P, NT + 1, D])
        vec = sb("vec", [P, V_ALL])
        w_in = sb("w_in", [P, 2, PROJ])
        w_out = sb("w_out", [P, IC, D])
        w_m1 = sb("w_m1", [P, 2, FF])
        w_m2 = sb("w_m2", [P, FC, D])
        w_e1 = [sb(f"w_e1{s}", [P, EXPERT_W1 + HC]) for s in range(2)]
        w_e2 = [sb(f"w_e2{s}", [P, HC, D]) for s in range(2)]
        b2_sb = sb("b2_sb", [SPREAD, D])

        in_h = sb("in_h", [P, 2, PROJ], F32R)
        in_l = sb("in_l", [P, 2, PROJ], F32R)
        out_h = sb("out_h", [P, IC, D], F32R)
        out_l = sb("out_l", [P, IC, D], F32R)
        m1_h = sb("m1_h", [P, 2, FF], F32R)
        m1_l = sb("m1_l", [P, 2, FF], F32R)
        m2 = sb("m2", [P, FC, 2, D], F32R)
        e1_h = [sb(f"e1_h{s}", [P, 2, HID], F32R) for s in range(2)]
        e1_l = [sb(f"e1_l{s}", [P, 2, HID], F32R) for s in range(2)]
        e2 = [sb(f"e2{s}", [P, HC, 2, D], F32R) for s in range(2)]
        wg_h = sb("wg_h", [P, 2, EXPERTS], F32R)
        wg_l = sb("wg_l", [P, 2, EXPERTS], F32R)
        b2s = sb("b2s", [SPREAD, 2, D], F32R)

        ident = sb("ident", [P, P])
        upto = sb("upto", [GROUP, GROUP])
        after = sb("after", [GROUP, GROUP])
        skip = sb("skip", [GROUP, GROUP])
        ones = sb("ones", [P, 1])
        minus_half = sb("minus_half", [P, NT])
        column = sb("column", [P, EXPERTS])

        h0 = sb("h0", [P, NT, D])
        xln = sb("xln", [P, NT, D])
        rows = sb("rows", [P, NT, D])
        res = sb("res", [P, NT, D])
        acc = sb("acc", [P, NT, D])
        stats = sb("stats", [P, NT, 6])
        mv = sb("mv", [P, NT, 2])
        rstd = sb("rstd", [P, NT])
        ustd = sb("ustd", [P, NT])
        ss3 = sb("ss3", [P, NT])
        ss4 = sb("ss4", [P, NT])
        squares = sb("squares", [P, D])

        xa_h = sb("xa_h", [P, T], F32R)
        xa_l = sb("xa_l", [P, T], F32R)
        xc = sb("xc", [P, T], F32R)
        xraw = sb("xraw", [P, NQ, T])
        hid = sb("hid", [P, FC, T])
        conv = hid[:, 0:NQ, :]
        ctmp = hid[:, NQ, :]
        pt_flat = pt[:, :, :].rearrange("p c n -> p (c n)")
        zs = pt_flat[:, 0:IC * T].rearrange("p (c t) -> p c t", c=IC)
        yz = pt_flat[:, IC * T:2 * IC * T].rearrange("p (c t) -> p c t", c=IC)
        cb = pt_flat[:, 0:EXPERTS * T]
        yz2 = w_in[:, :, :].rearrange("p a n -> p (a n)")[:, 0:IC * T].rearrange("p (c t) -> p c t", c=IC)
        hid_h = sb("hid_h", [P, FC, T], F32R)
        hid_l = sb("hid_l", [P, FC, T], F32R)
        yz_h = hid_h[:, 0:IC, :]
        yz_l = hid_l[:, 0:IC, :]

        dt_row = sb("dt_row", [1, T])
        dtv = sb("dtv", [GROUP, NG])
        dt_abs = sb("dt_abs", [GROUP, NG])
        dt_exp = sb("dt_exp", [GROUP, NG])
        dt_ln = sb("dt_ln", [GROUP, NG])
        dt_pos = sb("dt_pos", [GROUP, NG])
        dt = sb("dt", [GROUP, NG])
        exp_a = sb("exp_a", [GROUP, 1])
        da = sb("da", [GROUP, NG])
        da_after, decay, mix = (
            t[0:GROUP, :, :].rearrange("p k n -> p (k n)")[:, 0:NG * GROUP].rearrange("p (g n) -> p g n", g=NG)
            for t in (rows, res, acc))
        xt = xraw[0:GROUP, :, :].rearrange("p q t -> p (q t)")[:, 0:NG * INNER].rearrange(
            "p (g c) -> p g c", g=NG)

        scoreT = rows[0:EXPERTS, :, :].rearrange("e k n -> e (k n)")[:, 0:T]
        cwT = res[0:EXPERTS, :, :].rearrange("e k n -> e (k n)")[:, 0:T]
        gate_rows = nc.dram_tensor("gate_rows", (EXPERTS, T), F32).ap()
        cs = sb("cs", [SPREAD, T], F32R)
        gs = sb("gs", [P, NT, EXPERTS])
        top = sb("top", [P, NT, EXPERTS])
        top_i = sb("top_i", [P, NT, EXPERTS], U32)
        top_f = sb("top_f", [P, NT, 2])
        gap = sb("gap", [P, NT])
        th = sb("th", [P, NT])
        prob = sb("prob", [P, NT, 2])
        chosen = sb("chosen", [P, NT, 2, EXPERTS])
        share = sb("share", [P, NT, 2, EXPERTS])
        cw = sb("cw", [P, NT, EXPERTS])

        ld_patch = [sem(f"ld_patch{c}") for c in range(PATCH_CHUNKS)]
        ld_pos, ld_vec, ld_in, ld_out = sem("ld_pos"), sem("ld_vec"), sem("ld_in"), sem("ld_out")
        ld_m1, ld_m2, ld_b2 = sem("ld_m1"), sem("ld_m2"), sem("ld_b2")
        ld_e1 = [sem("ld_e10"), sem("ld_e11")]
        ld_e2 = [sem("ld_e20"), sem("ld_e21")]
        ld_cb0, ld_cb, st_gate = sem("ld_cb0"), sem("ld_cb"), sem("st_gate")
        stored = sem("stored")
        pool_own, act_own, dve_own = sem("pool_own"), sem("act_own"), sem("dve_own")
        consts, skip_ready, zeroed = sem("consts"), sem("skip_ready"), sem("zeroed")
        in_hi, in_lo = sem("in_hi"), sem("in_lo")
        out_hi, out_lo = sem("out_hi"), sem("out_lo")
        m1_hi, m1_lo = sem("m1_hi"), sem("m1_lo")
        m2_hi, m2_lo = sem("m2_hi"), sem("m2_lo")
        small_ready = sem("small_ready")
        ex_hi, ex_lo = sem("ex_hi"), sem("ex_lo")
        tok_done, h0_done = sem("tok_done"), sem("h0_done")
        base_ready, power_done = sem("base_ready"), sem("power_done")
        xln_done, rows_done = sem("xln_done"), sem("rows_done")
        turned, turned_hi, turned_lo = sem("turned"), sem("turned_hi"), sem("turned_lo")
        proj_done, proj_used = sem("proj_done"), sem("proj_used")
        dtr_done, dtr_read, dtc_done, dt_in, dt_soft = (sem("dtr_done"), sem("dtr_read"), sem("dtc_done"),
                                                        sem("dt_in"), sem("dt_soft"))
        a_ready, da_in, da_ready = sem("a_ready"), sem("da_in"), sem("da_ready")
        seg_done, exp_done, decay_done = sem("seg_done"), sem("exp_done"), sem("decay_done")
        conv_done, conv2_done = sem("conv_done"), sem("conv2_done")
        silu_done = sem("silu_done")
        g_done, mix_raw, mix_done = sem("g_done"), sem("mix_raw"), sem("mix_done")
        xt_done, xt_even, xt_odd = sem("xt_done"), sem("xt_even"), sem("xt_odd")
        y_done, yz_done, yz_hi, yz_lo = sem("y_done"), sem("yz_done"), sem("yz_hi"), sem("yz_lo")
        yz_sq, yz_sum = sem("yz_sq"), sem("yz_sum")
        ss3_sum, ss3_base = sem("ss3_sum"), sem("ss3_base")
        out_done, res_done, ss4_done = sem("out_done"), sem("res_done"), sem("ss4_done")
        up_done, up_used = sem("up_done"), sem("up_used")
        scaled, hid_hi, hid_split = sem("scaled"), sem("hid_hi"), sem("hid_split")
        mlp_done, h1_half, h1_done = sem("mlp_done"), sem("h1_half"), sem("h1_done")
        gate_done, gate_read, score_done = sem("gate_done"), sem("gate_read"), sem("score_done")
        gs_done, gap_done, th_done, cw_done = (sem("gs_done"), sem("gap_done"), sem("th_done"),
                                               sem("cw_done"))
        weight0_done = sem("weight0_done")
        cwT_done, cwT_hi, cwT_copy, cwT_lo = (sem("cwT_done"), sem("cwT_hi"), sem("cwT_copy"),
                                              sem("cwT_lo"))
        moe_done, sum_half, sum_done = sem("moe_done"), sem("sum_half"), sem("sum_done")

        MLP_UPS = 2 * FC
        UPS = 2 * HC
        PERIODS = EXPERTS - 2

        def w1_at(e):
            return 1 if isinstance(e, int) and e == 0 else e * 2

        def w2_at(e):
            return 2 * e + 2 if isinstance(e, int) and e == EXPERTS - 1 else e * 2 + 3

        POW_U, POW_X, POW_3, POW_4, POW_2 = 0, 2, 3, 3 + NT, 3 + NT + 2

        def work(n):
            return WORK[n % len(WORK)]

        def covering(k):
            return -(-(TILES[k][0] + TILES[k][1]) // GROUP)

        block = ctx.enter_context(nc.Block())

        @block.sync
        def _(sp):
            for c in range(PATCH_CHUNKS):
                sp.dma_start(pt[:, c, :], patches[c]).then_inc(ld_patch[c], 16)
                if c == 1:
                    sp.dma_start(vec[:, :], vectors).then_inc(ld_vec, 16)
                if c == 2:
                    sp.dma_start(w_in[:, :, :], in_proj).then_inc(ld_in, 16)
                if c == 4:
                    sp.dma_start(pos[:, :, :], posbias).then_inc(ld_pos, 16)
            sp.dma_start(w_out[:, :, :], out_proj).then_inc(ld_out, 16)
            sp.dma_start(b2_sb[0:EXPERTS, :], b2).then_inc(ld_b2, 16)
            sp.dma_start(b2_sb[32:SPREAD, :], b2).then_inc(ld_b2, 16)
            sp.dma_start(w_m1[:, :, :], mlp1).then_inc(ld_m1, 16)
            sp.dma_start(w_m2[:, :, :], mlp2).then_inc(ld_m2, 16)
            for e in range(2):
                sp.dma_start(w_e1[e][:, :], first[e]).then_inc(ld_e1[e], 16)
                sp.dma_start(w_e2[e][:, :, :], second[e]).then_inc(ld_e2[e], 16)
            sp.wait_ge(cwT_copy, 2)
            sp.dma_start(gate_rows[:, :], cwT).then_inc(st_gate, 16)
            sp.wait_ge(st_gate, 16)

            def gate_weights(e, landed):
                sp.dma_start(cb[:, e * T:(e + 1) * T], gate_rows[e:e + 1, :].broadcast_to([P, T]))\
                    .then_inc(landed, 16)

            gate_weights(1, ld_cb0)
            for e in (2, 3):
                sp.wait_ge(up_used, MLP_UPS + (UPS + HC if e == 2 else 2 * UPS))
                sp.dma_start(w_e1[e - 2][:, :], first[e]).then_inc(ld_e1[e - 2], 16)
                sp.wait_ge(ex_lo, w2_at(e - 2))
                sp.dma_start(w_e2[e - 2][:, :, :], second[e]).then_inc(ld_e2[e - 2], 16)
                if e == 2:
                    for other in range(2, EXPERTS):
                        gate_weights(other, ld_cb)
            with sp.Fori(0, PERIODS // 2 - 1) as i:
                for s in range(2):
                    sp.wait_ge(up_used, i * (2 * UPS) + (MLP_UPS + (s + 3) * UPS))
                    sp.dma_start(w_e1[s][:, :], first[bass.ds(i * 2 + (s + 4), 1), :, :].rearrange(
                        "a p n -> (a p) n")).then_inc(ld_e1[s], 16)
                    sp.wait_ge(ex_lo, i * 4 + (2 * s + 7))
                    sp.dma_start(w_e2[s][:, :, :].rearrange("p c n -> p (c n)"),
                                 second[bass.ds(i * 2 + (s + 4), 1), :, :].rearrange(
                                     "a p n -> (a p) n")).then_inc(ld_e2[s], 16)
            for k, (t0, m) in enumerate(TILES):
                sp.wait_ge(sum_done, k + 1)
                sp.dma_start(out[t0:t0 + m, :], acc[0:m, k, :]).then_inc(stored, 16)
            sp.wait_ge(stored, 16 * NT)

        @block.gpsimd
        def _(pool):
            own = [0]

            def link(ins):
                own[0] += 1
                ins.then_inc(pool_own, 1)
                pool.wait_ge(pool_own, own[0])

            g = nc.gpsimd

            def power(t, a, b):
                g.tensor_tensor(t[:, a:b], t[:, a:b], minus_half[:, 0:b - a], ALU.pow).then_inc(power_done, 1)

            link(g.memset(ident[:, :], 0.0))
            g.affine_select(out=ident[:, :], in_=ident[:, :], compare_op=ALU.not_equal, fill=1.0, base=0,
                            pattern=[[-1, P]], channel_multiplier=1).then_inc(consts, 1)
            g.memset(ones[:, :], 1.0).then_inc(consts, 1)
            g.memset(minus_half[:, :], -0.5).then_inc(consts, 1)
            for m, low, high in ((upto, (0, 0), (0, 1)), (after, (-1, -1), (LENGTH - 1, 0))):
                v = m[:, :].rearrange("r (j c) -> r j c", j=PER)
                link(g.memset(m[:, :], 1.0))
                link(g.affine_select(out=v, in_=v, compare_op=ALU.is_ge, fill=0.0, base=low[0],
                                     pattern=[[-LENGTH, PER], [low[1], LENGTH]], channel_multiplier=1))
                g.affine_select(out=v, in_=v, compare_op=ALU.is_ge, fill=0.0, base=high[0],
                                pattern=[[LENGTH, PER], [high[1], LENGTH]],
                                channel_multiplier=-1).then_inc(consts, 1)
            g.iota(column[:, :], pattern=[[1, EXPERTS]], base=0, channel_multiplier=0,
                   allow_small_or_imprecise_dtypes=True).then_inc(consts, 1)
            g.memset(cs[:, :].bitcast(F32), 0.0).then_inc(zeroed, 1)
            pool.wait_ge(ld_vec, 16)
            pool.wait_ge(consts, 6)
            g.tensor_scalar(skip[:, :], ident[0:GROUP, 0:GROUP], vec[0:GROUP, V_D:V_D + 1], 0.0, ALU.mult,
                            ALU.add).then_inc(skip_ready, 1)
            for n, tiles in enumerate(HALF_TILES):
                pool.wait_ge(base_ready, n + 1)
                power(ustd, tiles.start, tiles.stop)
            power(rstd, 0, NT)
            pool.wait_ge(da_in, 1)
            for n in range(NG):
                g.tensor_scalar(da_after[:, n, :], after[:, :], da[:, n:n + 1], 0.0, ALU.mult, ALU.add)\
                    .then_inc(da_ready, 1)
            c2 = NQ - 1
            pool.wait_ge(proj_used, 2 * NQ)
            cv = conv[:, c2, :].rearrange("p (i l) -> p i l", i=IMAGES)
            xv = xraw[:, c2, :].rearrange("p (i l) -> p i l", i=IMAGES)
            tv = ctmp[:, :].rearrange("p (i l) -> p i l", i=IMAGES)
            w0 = V_CONVW + CONV_SRC[c2] * TAPS
            for k in range(1, TAPS):
                link(g.tensor_scalar(tv[:, :, k:], xv[:, :, 0:LENGTH - k],
                                     vec[:, w0 + TAPS - 1 - k:w0 + TAPS - k], 0.0, ALU.mult, ALU.add))
                ins = g.tensor_tensor(cv[:, :, k:], cv[:, :, k:], tv[:, :, k:], ALU.add)
                if k < TAPS - 1:
                    link(ins)
            ins.then_inc(conv2_done, 1)
            for n, (t0, m) in enumerate(GROUPS):
                pool.wait_ge(mix_raw, n + 1)
                g.tensor_tensor(mix[0:m, n, 0:m], mix[0:m, n, 0:m], skip[0:m, 0:m], ALU.add)\
                    .then_inc(mix_done, 1)
            for n in range(NG + 1):
                if n < NG:
                    t0, m = GROUPS[n]
                    pool.wait_ge(yz_sq, n + 1)
                    total = yz2[:, 0, t0:t0 + m]
                    link(g.tensor_tensor(total, total, yz2[:, 1, t0:t0 + m], ALU.add))
                    g.tensor_tensor(total, total, yz2[:, 2, t0:t0 + m], ALU.add).then_inc(yz_sum, 1)
                for k in range(NT):
                    if covering(k) + 1 == n or (n == NG and covering(k) == NG):
                        pool.wait_ge(ss3_base, k + 1)
                        power(ss3, k, k + 1)
            for n, tiles in enumerate(HALF_TILES):
                pool.wait_ge(ss4_done, tiles.stop)
                s = ss4[:, tiles.start:tiles.stop]
                link(g.tensor_scalar(s, s, 1.0 / D, EPS, ALU.mult, ALU.add))
                power(ss4, tiles.start, tiles.stop)

            pool.wait_ge(m2_hi, 1)
            g.tensor_tensor(m2[:, :, 1, :], w_m2[:, :, :], m2[:, :, 0, :].bitcast(F32), ALU.subtract)\
                .then_inc(m2_lo, 1)

            def low1(s, count):
                pool.wait_ge(ex_hi, count)
                g.tensor_tensor(e1_l[s][:, :, :].rearrange("p a n -> p (a n)"), w_e1[s][:, 0:EXPERT_W1],
                                e1_h[s][:, :, :].rearrange("p a n -> p (a n)").bitcast(F32),
                                ALU.subtract).then_inc(ex_lo, 1)

            def low2(s, count):
                pool.wait_ge(ex_hi, count)
                g.tensor_tensor(e2[s][:, :, 1, :], w_e2[s][:, :, :], e2[s][:, :, 0, :].bitcast(F32),
                                ALU.subtract).then_inc(ex_lo, 1)

            low1(0, 1)
            low1(1, 2)
            low2(0, 3)
            for n, tiles in enumerate(HALF_TILES):
                pool.wait_ge(base_ready, 3 + n)
                power(rstd, tiles.start, tiles.stop)
            with pool.Fori(0, PERIODS // 2) as i:
                for s in range(2):
                    low1(s, i * 4 + (2 * s + 4))
                    low2(1 - s, i * 4 + (2 * s + 5))
            low2(1, w2_at(EXPERTS - 1))

        @block.scalar
        def _(act):
            a = nc.scalar
            own = [0]

            def link(ins):
                own[0] += 1
                ins.then_inc(act_own, 1)
                act.wait_ge(act_own, own[0])

            act.wait_ge(ld_vec, 16)
            act.wait_ge(consts, 2)
            a.activation(dt_ln[:, 0:1], ones[0:GROUP, :], ACT.Ln)
            a.activation(exp_a[:, :], vec[0:GROUP, V_ALOG:V_ALOG + 1], ACT.Exp).then_inc(a_ready, 1)
            act.wait_ge(ld_in, 16)
            for j, v in enumerate((V_N1A, V_N1C)):
                a.activation(in_h[:, j, :], w_in[:, j, :], ACT.Copy, scale=vec[:, v:v + 1]).then_inc(in_hi, 1)
            act.wait_ge(ld_out, 16)
            for c in range(IC):
                a.activation(out_h[:, c, :], w_out[:, c, :], ACT.Copy,
                             scale=vec[:, V_SSM + c:V_SSM + c + 1]).then_inc(out_hi, 1)

            def turn_high(n):
                t0, m = HALVES[n % 2]
                srcA, srcB = TURN[n % 2]
                act.wait_ge(turned, n + 1)
                a.copy(xa_h[:, t0:t0 + m], srcA).then_inc(turned_hi, 1)
                a.copy(xc[0:REST, t0:t0 + m], srcB).then_inc(turned_hi, 1)

            def take_item(n):
                q, h = ITEMS[n]
                t0, m = HALVES[h]
                src = PROJ_RING[n % 4][:, 0:m]
                act.wait_ge(proj_done, n + 1)
                if q >= NQ:
                    a.activation(zs[:, q - NQ, t0:t0 + m], src, ACT.Silu).then_inc(proj_used, 1)
                    return
                w = V_CONVW + CONV_SRC[q] * TAPS + TAPS - 1
                b = V_CONVB + CONV_SRC[q]
                a.copy(xraw[:, q, t0:t0 + m], src)
                a.activation(conv[:, q, t0:t0 + m], src, ACT.Identity, scale=vec[:, w:w + 1],
                             bias=vec[:, b:b + 1]).then_inc(proj_used, 1)

            turn_high(0)
            take_item(0)
            take_item(1)
            turn_high(1)
            for n in range(2, 6):
                take_item(n)
            act.wait_ge(dtr_done, 1)
            for (t0, m), src in zip(HALVES, DT_ROW):
                a.copy(dt_row[:, t0:t0 + m], src).then_inc(dtr_read, 1)
            take_item(6)
            take_item(7)
            act.wait_ge(dt_in, 1)
            link(a.activation(dt_abs[:, :], dtv[:, :], ACT.Abs))
            link(a.activation(dt_exp[:, :], dt_abs[:, :], ACT.Exp, scale=-1.0))
            a.activation(dt_ln[:, :], dt_exp[:, :], ACT.Ln, bias=1.0).then_inc(dt_soft, 1)
            take_item(8)
            take_item(9)
            act.wait_ge(seg_done, 1)
            a.activation(decay[:, 0:4, :].rearrange("p g t -> p (g t)"), bank[3][0:GROUP, 0:4 * GROUP],
                         ACT.Exp).then_inc(exp_done, 1)
            act.wait_ge(seg_done, 2)
            a.activation(decay[:, 4, :], bank[0][0:GROUP, 0:GROUP], ACT.Exp).then_inc(exp_done, 1)
            a.activation(decay[0:LAST, FULL, 0:LAST], bank[0][0:LAST, GROUP:GROUP + LAST], ACT.Exp)\
                .then_inc(exp_done, 1)

            def silu(q, ready, count):
                act.wait_ge(ready, count)
                a.activation(conv[:, q, :], conv[:, q, :], ACT.Silu).then_inc(silu_done, 1)

            take_item(10)
            take_item(11)
            silu(B_, conv_done, 1)
            silu(C_, conv_done, 2)
            for n in range(12, 16):
                take_item(n)
            silu(X0, conv_done, 3)
            silu(X0 + 1, conv_done, 4)
            silu(X0 + 2, conv2_done, 1)
            for n in range(0, NG, 2):
                m = GROUPS[n][1]
                act.wait_ge(xt_done, n + 1)
                a.copy(xt[0:m, n, :], work(n)[0:m, 0:INNER]).then_inc(xt_even, 1)
            act.wait_ge(ld_m1, 16)
            for j, v in enumerate((V_N2A, V_N2C)):
                a.activation(m1_h[:, j, :], w_m1[:, j, :], ACT.Copy, scale=vec[:, v:v + 1]).then_inc(m1_hi, 1)
            for n, (t0, m) in enumerate(GROUPS):
                act.wait_ge(yz_done, n + 1)
                a.activation(yz2[:, :, t0:t0 + m], yz[:, :, t0:t0 + m], ACT.Square).then_inc(yz_sq, 1)
                a.copy(yz_h[:, :, t0:t0 + m], yz[:, :, t0:t0 + m]).then_inc(yz_hi, 1)
            act.wait_ge(ld_m2, 16)
            a.copy(m2[:, :, 0, :], w_m2[:, :, :]).then_inc(m2_hi, 1)
            for k, (t0, m) in enumerate(TILES):
                act.wait_ge(res_done, k + 1)
                if k:
                    act.wait_ge(ss4_done, k)
                a.activation(squares[0:m, :], res[0:m, k, :], ACT.Square, accum_out=ss4[0:m, k:k + 1])\
                    .then_inc(ss4_done, 1)

            def gelu(bk, chunk, h, ups, bias):
                t0, m = HALVES[h]
                act.wait_ge(up_done, ups)
                a.activation(hid[:, chunk, t0:t0 + m], bk[:, 0:m], ACT.Gelu, bias=bias)\
                    .then_inc(up_used, 1)

            def high1(s, loads):
                act.wait_ge(ld_e1[s], loads)
                a.copy(e1_h[s][:, :, :].rearrange("p a n -> p (a n)"), w_e1[s][:, 0:EXPERT_W1])\
                    .then_inc(ex_hi, 1)

            def high2(s, loads):
                act.wait_ge(ld_e2[s], loads)
                a.copy(e2[s][:, :, 0, :], w_e2[s][:, :, :]).then_inc(ex_hi, 1)

            turn_high(2)
            for n in range(MLP_UPS):
                gelu(work(n), n % FC, n // FC, n + 1, 0.0)
                if n == 2:
                    turn_high(3)
                if n == 4:
                    high1(0, 16)
                if n == 6:
                    high1(1, 16)
                if n == 8:
                    high2(0, 16)

            def expert_gelu(s, j, ups):
                h, c = divmod(j, HC)
                gelu(work(j), s * HC + c, h, ups, w_e1[s][:, EXPERT_W1 + c:EXPERT_W1 + c + 1])

            def expert_high(s, j, before):
                h, c = divmod(j, HC)
                t0, m = HALVES[h]
                act.wait_ge(scaled, before + (j + 1))
                a.copy(hid_h[:, s * HC + c, t0:t0 + m], hid[:, s * HC + c, t0:t0 + m]).then_inc(hid_hi, 1)

            turn_high(4)
            for j in range(2 * HC):
                expert_gelu(j // HC, j % HC, MLP_UPS + j + 1)
                if j == 0:
                    turn_high(5)
            act.wait_ge(gate_done, 1)
            for (t0, m), bk in zip(HALVES, (bank[1], bank[4])):
                a.copy(scoreT[:, t0:t0 + m], bk[0:EXPERTS, 0:m]).then_inc(gate_read, 1)
            for j in range(HC):
                expert_gelu(0, HC + j, MLP_UPS + UPS + j + 1)
            act.wait_ge(gap_done, 1)
            a.activation(th[:, :], gap[:, :], ACT.Tanh, scale=0.5).then_inc(th_done, 1)
            for j in range(HC):
                expert_gelu(1, HC + j, MLP_UPS + UPS + HC + j + 1)
            act.wait_ge(cwT_done, 1)
            for t0, t1, bk in ((0, 512, bank[2]), (512, T, bank[3])):
                a.copy(cwT[:, t0:t1], bk[0:EXPERTS, 0:t1 - t0]).then_inc(cwT_copy, 1)
            for j in range(UPS):
                expert_high(0, j, 0)
                if j == 1:
                    act.wait_ge(zeroed, 1)
                    for t0, t1, bk in ((0, 512, bank[2]), (512, T, bank[3])):
                        a.copy(cs[0:EXPERTS, t0:t1], bk[0:EXPERTS, 0:t1 - t0]).then_inc(cwT_hi, 1)
            for j in range(UPS):
                expert_high(1, j, UPS)
                if j == 1:
                    high1(0, 32)
                    high2(1, 16)

            def expert(s, before, loads1, loads2):
                for j in range(UPS + 1):
                    if j < UPS:
                        expert_gelu(s, j, before + (MLP_UPS + j + 1))
                    if j:
                        expert_high(s, j - 1, before)
                    if j == 2 and loads1 is not None:
                        high1(1 - s, loads1)
                    if j == 4:
                        high2(s, loads2)

            with act.Fori(0, PERIODS // 2 - 1) as i:
                for s in range(2):
                    expert(s, i * (2 * UPS) + (s + 2) * UPS, i * 16 + (32 if s == 0 else 48), i * 16 + 32)
            expert(0, PERIODS * UPS, 16 * (EXPERTS // 2), 16 * (EXPERTS // 2))
            expert(1, (EXPERTS - 1) * UPS, None, 16 * (EXPERTS // 2))

        @block.vector
        def _(dve):
            v = nc.vector
            own = [0]

            def step(ins):
                own[0] += 1
                ins.then_inc(dve_own, 1)

            def link(ins):
                step(ins)
                dve.wait_ge(dve_own, own[0])

            for small in (mv, rstd, ustd, ss3, ss4, dtv, gs):
                step(v.memset(small[:], 1.0))
            link(v.memset(b2s[:, :, :].bitcast(F32), 0.0))
            dve.wait_ge(ld_vec, 16)
            wg = vec[:, V_WGA:V_ALL].rearrange("p (a e) -> p a e", a=2)
            link(v.tensor_copy(wg_h[:, :, :], wg))
            v.tensor_tensor(wg_l[:, :, :], wg, wg_h[:, :, :].bitcast(F32), ALU.subtract).then_inc(small_ready, 1)
            for j, (w, r) in enumerate(((V_N1A, P), (V_N1C, REST))):
                dve.wait_ge(in_hi, j + 1)
                v.scalar_tensor_tensor(in_l[0:r, j, :], w_in[0:r, j, :], vec[0:r, w:w + 1],
                                       in_h[0:r, j, :].bitcast(F32), ALU.mult, ALU.subtract).then_inc(in_lo, 1)
            dve.wait_ge(ld_pos, 16)
            link(v.tensor_tensor(pos[:, 0:NT, :], pos[:, 0:NT, :],
                                 pos[:, NT:NT + 1, :].broadcast_to([P, NT, D]), ALU.add))

            def embed(k):
                m = TILES[k][1]
                dve.wait_ge(tok_done, k + 1)
                v.tensor_tensor(h0[0:m, k, :], TILE_BANK[k][0:m, 0:D], pos[0:m, k, :], ALU.add)\
                    .then_inc(h0_done, 1)

            def embed_stats(k, last):
                m = TILES[k][1]
                dve.wait_ge(h0_done, k + 1)
                link(v.bn_stats(stats[0:m, k, :], h0[0:m, k, :]))
                ins = v.bn_aggr(mv[0:m, k, :], stats[0:m, k, :])
                (link if last else step)(ins)

            def embed_base(tiles):
                a, b = tiles.start, tiles.stop
                v.tensor_scalar(ustd[:, a:b], mv[:, a:b, 1], 1.0 + EPS, EPS * EPS, ALU.mult, ALU.add)\
                    .then_inc(base_ready, 1)

            def embed_rows(n):
                dve.wait_ge(power_done, POW_U + n + 1)
                for k in HALF_TILES[n]:
                    m = TILES[k][1]
                    v.tensor_scalar(rows[0:m, k, :], h0[0:m, k, :], mv[0:m, k, 0:1], ustd[0:m, k:k + 1],
                                    ALU.subtract, ALU.mult).then_inc(rows_done, 1)

            def turn_low(n):
                t0, m = HALVES[n % 2]
                srcA, srcB = TURN[n % 2]
                dve.wait_ge(turned_hi, 2 * n + 2)
                v.tensor_tensor(xa_l[:, t0:t0 + m], srcA, xa_h[:, t0:t0 + m].bitcast(F32), ALU.subtract)\
                    .then_inc(turned_lo, 1)
                v.tensor_tensor(xc[REST:P, t0:t0 + m], srcB, xc[0:REST, t0:t0 + m].bitcast(F32),
                                ALU.subtract).then_inc(turned_lo, 1)

            embed(0)
            embed(1)
            embed_stats(0, False)
            embed_stats(1, True)
            embed_base(HALF_TILES[0])
            embed(2)
            embed_stats(2, False)
            embed_rows(0)
            embed(3)
            embed(4)
            for k in (3, 4):
                m = TILES[k][1]
                dve.wait_ge(h0_done, k + 1)
                step(v.bn_stats(stats[0:m, k, :], h0[0:m, k, :]))
            turn_low(0)
            dve.wait_ge(dve_own, own[0])
            for k in (3, 4):
                m = TILES[k][1]
                step(v.bn_aggr(mv[0:m, k, :], stats[0:m, k, :]))
            dve.wait_ge(dve_own, own[0])
            link(v.tensor_scalar(rstd[:, :], mv[:, :, 1], EPS, None, ALU.add))
            embed_base(HALF_TILES[1])
            embed_rows(1)
            dve.wait_ge(power_done, POW_X + 1)
            for k, (t0, m) in enumerate(TILES[0:2]):
                v.tensor_scalar(xln[0:m, k, :], h0[0:m, k, :], mv[0:m, k, 0:1], rstd[0:m, k:k + 1],
                                ALU.subtract, ALU.mult).then_inc(xln_done, 1)
            turn_low(1)
            for k in range(2, NT):
                m = TILES[k][1]
                v.tensor_scalar(xln[0:m, k, :], h0[0:m, k, :], mv[0:m, k, 0:1], rstd[0:m, k:k + 1],
                                ALU.subtract, ALU.mult).then_inc(xln_done, 1)
            for c in range(IC):
                dve.wait_ge(out_hi, c + 1)
                v.scalar_tensor_tensor(out_l[:, c, :], w_out[:, c, :], vec[:, V_SSM + c:V_SSM + c + 1],
                                       out_h[:, c, :].bitcast(F32), ALU.mult, ALU.subtract).then_inc(out_lo, 1)

            def taps(qs, items):
                for k in range(1, TAPS):
                    for q, item in zip(qs, items):
                        cv = conv[:, q, :].rearrange("p (i l) -> p i l", i=IMAGES)
                        xv = xraw[:, q, :].rearrange("p (i l) -> p i l", i=IMAGES)
                        w = V_CONVW + CONV_SRC[q] * TAPS + TAPS - 1 - k
                        if k == 1:
                            dve.wait_ge(proj_used, item)
                        else:
                            dve.wait_ge(dve_own, own[0] - (len(qs) - 1))
                        ins = v.scalar_tensor_tensor(cv[:, :, k:], xv[:, :, 0:LENGTH - k], vec[:, w:w + 1],
                                                     cv[:, :, k:], ALU.mult, ALU.add)
                        if k < TAPS - 1:
                            step(ins)
                        else:
                            ins.then_inc(conv_done, 1)
                            if q != qs[-1]:
                                dve.wait_ge(dve_own, own[0])

            taps((B_, C_), (5, 6))
            dve.wait_ge(dtc_done, 1)
            link(v.tensor_scalar(dtv[:, 0:FULL], DT_COL[0:GROUP, 0:FULL], vec[0:GROUP, V_DTB:V_DTB + 1], None,
                                 ALU.add))
            v.tensor_scalar(dtv[0:LAST, FULL:NG], DT_COL[0:LAST, FULL:NG], vec[0:LAST, V_DTB:V_DTB + 1], None,
                            ALU.add).then_inc(dt_in, 1)
            dve.wait_ge(dt_in, 1)
            link(v.tensor_scalar(dt_pos[:, :], dtv[:, :], 0.0, None, ALU.max))
            dve.wait_ge(dt_soft, 1)
            link(v.tensor_tensor(dt[:, :], dt_pos[:, :], dt_ln[:, :], ALU.add))
            dve.wait_ge(a_ready, 1)
            v.tensor_scalar(da[:, :], dt[:, :], exp_a[:, 0:1], -1.0, ALU.mult, ALU.mult).then_inc(da_in, 1)
            taps((X0, X0 + 1), (7, 8))
            dve.wait_ge(exp_done, 3)
            dve.wait_ge(consts, 6)
            v.tensor_tensor(decay[:, 0:FULL, :], decay[:, 0:FULL, :],
                            upto[:, :].rearrange("r (a c) -> r a c", a=1).broadcast_to([GROUP, FULL, GROUP]),
                            ALU.mult).then_inc(decay_done, 1)
            v.tensor_tensor(decay[0:LAST, FULL, 0:LAST], decay[0:LAST, FULL, 0:LAST], upto[0:LAST, 0:LAST],
                            ALU.mult).then_inc(decay_done, 1)
            for n, (t0, m) in enumerate(GROUPS):
                dve.wait_ge(g_done, 1 if n < 4 else 2)
                dve.wait_ge(decay_done, 2 if n == FULL else 1)
                v.scalar_tensor_tensor(mix[0:m, n, 0:m], scan_pair(n, m, bank[4], bank[2]), dt[0:m, n:n + 1],
                                       decay[0:m, n, 0:m], ALU.mult, ALU.mult).then_inc(mix_raw, 1)
            for n in range(1, NG, 2):
                m = GROUPS[n][1]
                dve.wait_ge(xt_done, n + 1)
                v.tensor_copy(xt[0:m, n, :], work(n)[0:m, 0:INNER]).then_inc(xt_odd, 1)
            for n in range(NG + 2):
                if n < NG:
                    t0, m = GROUPS[n]
                    dve.wait_ge(y_done, n + 1)
                    src = work(n)[:, 0:IC * m].rearrange("p (c t) -> p c t", c=IC)
                    v.tensor_tensor(yz[:, :, t0:t0 + m], src, zs[:, :, t0:t0 + m], ALU.mult)\
                        .then_inc(yz_done, 1)
                if 1 <= n <= NG:
                    t0, m = GROUPS[n - 1]
                    dve.wait_ge(yz_hi, n)
                    v.tensor_tensor(yz_l[:, :, t0:t0 + m], yz[:, :, t0:t0 + m],
                                    yz_h[:, :, t0:t0 + m].bitcast(F32), ALU.subtract).then_inc(yz_lo, 1)
                for k in range(NT):
                    if covering(k) + 1 == n:
                        m = TILES[k][1]
                        dve.wait_ge(ss3_sum, k + 1)
                        v.tensor_scalar(ss3[0:m, k:k + 1], TILE_BANK[k][0:m, 0:1], 1.0 / INNER, EPS, ALU.mult,
                                        ALU.add).then_inc(ss3_base, 1)
                        if k == 0:
                            dve.wait_ge(ld_b2, 32)
                            for r in (0, 32):
                                step(v.tensor_copy(b2s[r:r + EXPERTS, 0, :], b2_sb[r:r + EXPERTS, :]))
                            dve.wait_ge(dve_own, own[0])
                            v.tensor_tensor(b2s[0:EXPERTS, 1, :], b2_sb[0:EXPERTS, :],
                                            b2s[0:EXPERTS, 0, :].bitcast(F32), ALU.subtract)\
                                .then_inc(small_ready, 1)
                            for j, (w, r) in enumerate(((V_N2A, P), (V_N2C, REST))):
                                dve.wait_ge(m1_hi, j + 1)
                                v.scalar_tensor_tensor(m1_l[0:r, j, :], w_m1[0:r, j, :], vec[0:r, w:w + 1],
                                                       m1_h[0:r, j, :].bitcast(F32), ALU.mult, ALU.subtract).then_inc(m1_lo, 1)

            def residual(k):
                m = TILES[k][1]
                dve.wait_ge(power_done, POW_3 + k + 1)
                dve.wait_ge(out_done, k + 1)
                v.scalar_tensor_tensor(res[0:m, k, :], TILE_BANK[k][0:m, 0:D], ss3[0:m, k:k + 1],
                                       xln[0:m, k, :], ALU.mult, ALU.add).then_inc(res_done, 1)

            def mlp_rows(n):
                dve.wait_ge(power_done, POW_4 + n + 1)
                for k in HALF_TILES[n]:
                    m = TILES[k][1]
                    v.tensor_scalar(rows[0:m, k, :], res[0:m, k, :], ss4[0:m, k:k + 1], None, ALU.mult)\
                        .then_inc(rows_done, 1)

            dve.wait_ge(xln_done, NT)
            for n, tiles in enumerate(HALF_TILES):
                for k in tiles:
                    residual(k)
                mlp_rows(n)
            turn_low(2)

            def split_hidden(n):
                h, c = divmod(n, FC)
                t0, m = HALVES[h]
                dve.wait_ge(up_used, n + 1)
                link(v.tensor_copy(hid_h[:, c, t0:t0 + m], hid[:, c, t0:t0 + m]))
                v.tensor_tensor(hid_l[:, c, t0:t0 + m], hid[:, c, t0:t0 + m],
                                hid_h[:, c, t0:t0 + m].bitcast(F32), ALU.subtract).then_inc(hid_split, 1)

            for n in range(MLP_UPS):
                split_hidden(n)
                if n == 2:
                    turn_low(3)

            def second_residual(k):
                m = TILES[k][1]
                dve.wait_ge(mlp_done, k + 1)
                v.tensor_tensor(acc[0:m, k, :], TILE_BANK[k][0:m, 0:D], h0[0:m, k, :], ALU.add)\
                    .then_inc(h1_half, 1)
                dve.wait_ge(h1_half, k + 1)
                v.tensor_tensor(acc[0:m, k, :], TILE_BANK[k][0:m, D:2 * D], acc[0:m, k, :], ALU.add)\
                    .then_inc(h1_done, 1)
                dve.wait_ge(h1_done, k + 1)
                link(v.bn_stats(stats[0:m, k, :], acc[0:m, k, :]))
                link(v.bn_aggr(mv[0:m, k, :], stats[0:m, k, :]))

            def second_base(tiles):
                a, b = tiles.start, tiles.stop
                v.tensor_scalar(rstd[:, a:b], mv[:, a:b, 1], EPS, None, ALU.add).then_inc(base_ready, 1)

            def expert_rows(n):
                dve.wait_ge(power_done, POW_2 + n + 1)
                for k in HALF_TILES[n]:
                    m = TILES[k][1]
                    v.tensor_scalar(rows[0:m, k, :], acc[0:m, k, :], mv[0:m, k, 0:1], rstd[0:m, k:k + 1],
                                    ALU.subtract, ALU.mult).then_inc(rows_done, 1)

            second_residual(0)
            second_residual(1)
            second_base(HALF_TILES[0])
            second_residual(2)
            expert_rows(0)
            second_residual(3)
            turn_low(4)
            second_residual(4)
            second_base(HALF_TILES[1])
            expert_rows(1)
            turn_low(5)

            dve.wait_ge(score_done, 1)
            v.tensor_copy(gs[:, 0:NT - 1, :].rearrange("p k e -> p (k e)"), bank[0][:, 0:(NT - 1) * EXPERTS])\
                .then_inc(gs_done, 1)
            m = TILES[-1][1]
            v.tensor_copy(gs[0:m, NT - 1, :], bank[0][0:m, (NT - 1) * EXPERTS:NT * EXPERTS])\
                .then_inc(gs_done, 1)
            dve.wait_ge(gs_done, 2)
            for k in range(NT):
                step(v.max(top[:, k, :], gs[:, k, :]))
            dve.wait_ge(dve_own, own[0])
            v.tensor_tensor(gap[:, :], top[:, :, 0], top[:, :, 1], ALU.subtract).then_inc(gap_done, 1)
            for k in range(NT):
                step(v.max_index(top_i[:, k, :], top[:, k, :], gs[:, k, :]))
            dve.wait_ge(dve_own, own[0])
            step(v.tensor_copy(top_f[:, :, :], top_i[:, :, 0:2]))
            dve.wait_ge(th_done, 1)
            step(v.tensor_scalar(prob[:, :, 0], th[:, :], 0.5, 0.5, ALU.mult, ALU.add))
            step(v.tensor_scalar(prob[:, :, 1], th[:, :], -0.5, 0.5, ALU.mult, ALU.add))
            dve.wait_ge(dve_own, own[0] - 2)
            dve.wait_ge(consts, 6)
            link(v.tensor_tensor(chosen[:, :, :, :].rearrange("p k j e -> p (k j) e"),
                                 column[:, :].rearrange("p (a e) -> p a e", a=1).broadcast_to(
                                     [P, 2 * NT, EXPERTS]),
                                 top_f[:, :, :].rearrange("p k (j a) -> p (k j) a", a=1).broadcast_to(
                                     [P, 2 * NT, EXPERTS]), ALU.is_equal))
            link(v.tensor_tensor(share[:, :, :, :].rearrange("p k j e -> p (k j) e"),
                                 chosen[:, :, :, :].rearrange("p k j e -> p (k j) e"),
                                 prob[:, :, :].rearrange("p k (j a) -> p (k j) a", a=1).broadcast_to(
                                     [P, 2 * NT, EXPERTS]), ALU.mult))
            v.tensor_tensor(cw[:, :, :], share[:, :, 0, :], share[:, :, 1, :], ALU.add).then_inc(cw_done, 1)

            def expert(e, s, before):
                for j in range(UPS + 1):
                    if j < UPS:
                        h, c = divmod(j, HC)
                        t0, m = HALVES[h]
                        if not isinstance(e, int):
                            weight = cb[:, bass.ds(e * T + t0, m)]
                        elif e == 0:
                            weight = bank[h][:, 0:m]
                        else:
                            weight = cb[:, e * T + t0:e * T + t0 + m]
                        ups = UPS + j - HC if isinstance(e, int) and e == 0 and h else j
                        dve.wait_ge(up_used, before + (MLP_UPS + ups + 1))
                        v.tensor_tensor(hid[:, s * HC + c, t0:t0 + m], hid[:, s * HC + c, t0:t0 + m], weight,
                                        ALU.mult).then_inc(scaled, 1)
                    if j:
                        h, c = divmod(j - 1, HC)
                        t0, m = HALVES[h]
                        dve.wait_ge(hid_hi, before + j)
                        v.tensor_tensor(hid_l[:, s * HC + c, t0:t0 + m], hid[:, s * HC + c, t0:t0 + m],
                                        hid_h[:, s * HC + c, t0:t0 + m].bitcast(F32), ALU.subtract)\
                            .then_inc(hid_split, 1)

            dve.wait_ge(weight0_done, 1)
            expert(0, 0, 0)
            dve.wait_ge(cwT_hi, 2)
            for t0, t1, bk in ((0, 512, bank[2]), (512, T, bank[3])):
                v.tensor_tensor(cs[32:SPREAD, t0:t1], bk[0:EXPERTS, 0:t1 - t0],
                                cs[0:EXPERTS, t0:t1].bitcast(F32), ALU.subtract).then_inc(cwT_lo, 1)
            dve.wait_ge(ld_cb0, 16)
            expert(1, 1, UPS)
            dve.wait_ge(ld_cb, 16 * (EXPERTS - 2))
            with dve.Fori(0, PERIODS // 2 - 1) as i:
                for s in range(2):
                    expert(i * 2 + (s + 2), s, i * (2 * UPS) + (s + 2) * UPS)
            expert(EXPERTS - 2, 0, (EXPERTS - 2) * UPS)
            expert(EXPERTS - 1, 1, (EXPERTS - 1) * UPS)
            for k, (t0, m) in enumerate(TILES):
                dve.wait_ge(moe_done, k + 1)
                v.tensor_tensor(acc[0:m, k, :], TILE_BANK[k][0:m, 0:D], acc[0:m, k, :], ALU.add)\
                    .then_inc(sum_half, 1)
                dve.wait_ge(sum_half, k + 1)
                v.tensor_tensor(acc[0:m, k, :], TILE_BANK[k][0:m, D:2 * D], acc[0:m, k, :], ALU.add)\
                    .then_inc(sum_done, 1)

        @block.tensor
        def _(pe):
            mm = nc.tensor.matmul
            turn_to = nc.tensor.transpose
            for c in range(PATCH_CHUNKS):
                pe.wait_ge(ld_patch[c], 16)
                for k, (t0, m) in enumerate(TILES):
                    ins = mm(TILE_BANK[k][0:m, 0:D], pt[:, c, t0:t0 + m], pt[:, c, T:T + D],
                             start=(c == 0), stop=(c == PATCH_CHUNKS - 1))
                    if c == PATCH_CHUNKS - 1:
                        ins.then_inc(tok_done, 1)

            def turn(n):
                at0, width = HALVES[n % 2]
                toA, toB = TURN[n % 2]
                for k in HALF_TILES[n % 2]:
                    t0, m = TILES[k]
                    at = t0 - at0
                    pe.wait_ge(rows_done, NT * (n // 2) + k + 1)
                    turn_to(toA[:, at:at + m], rows[0:m, k, 0:P], ident[0:m, 0:m])
                    ins = turn_to(toB[:, at:at + m], rows[0:m, k, P:D], ident[0:m, 0:m])
                ins.then_inc(turned, 1)

            def product192(dst, w_h, w_l, c0, n, t0, m):
                wah, wch = w_h[:, 0, c0:c0 + n], w_h[:, 1, c0:c0 + n]
                wal, wcl = w_l[:, 0, c0:c0 + n], w_l[0:REST, 1, c0:c0 + n]
                mm(dst, wah, xa_h[:, t0:t0 + m], start=True, stop=False)
                mm(dst, wah, xa_l[:, t0:t0 + m], start=False, stop=False)
                mm(dst, wal, xa_h[:, t0:t0 + m], start=False, stop=False)
                mm(dst, wch, xc[:, t0:t0 + m], start=False, stop=False)
                return mm(dst, wcl, xc[0:REST, t0:t0 + m], start=False, stop=True)

            def item(n):
                q, h = ITEMS[n]
                t0, m = HALVES[h]
                if n >= 4:
                    pe.wait_ge(proj_used, n - 3)
                product192(PROJ_RING[n % 4][:, 0:m], in_h, in_l, PROJ_COL[q], P, t0, m).then_inc(proj_done, 1)

            pe.wait_ge(consts, 6)
            turn(0)
            pe.wait_ge(in_lo, 2)
            pe.wait_ge(turned_lo, 2)
            item(0)
            item(1)
            turn(1)
            item(2)
            item(3)
            pe.wait_ge(turned_lo, 4)
            item(4)
            item(5)
            for (t0, m), dst in zip(HALVES, DT_ROW):
                ins = product192(dst, in_h, in_l, PROJ - 1, 1, t0, m)
            ins.then_inc(dtr_done, 1)
            item(6)
            item(7)
            pe.wait_ge(dtr_read, 2)
            for n, (t0, m) in enumerate(GROUPS):
                ins = mm(DT_COL[0:m, n:n + 1], dt_row[:, t0:t0 + m], ones[0:1, :], start=True, stop=True)
            ins.then_inc(dtc_done, 1)
            item(8)
            item(9)
            item(10)
            item(11)
            for n, (t0, m) in enumerate(GROUPS):
                pe.wait_ge(da_ready, n + 1)
                ins = mm(scan_pair(n, m, bank[3], bank[0]), da_after[0:m, n, 0:m], upto[0:m, 0:m],
                         start=True, stop=True)
                if n in (3, NG - 1):
                    ins.then_inc(seg_done, 1)
            for n in range(12, len(ITEMS)):
                item(n)
            pe.wait_ge(silu_done, 2)
            for n, (t0, m) in enumerate(GROUPS):
                ins = mm(scan_pair(n, m, bank[4], bank[2]), conv[:, B_, t0:t0 + m], conv[:, C_, t0:t0 + m],
                         start=True, stop=True)
                if n in (3, NG - 1):
                    ins.then_inc(g_done, 1)
            pe.wait_ge(silu_done, 5)
            pe.wait_ge(proj_used, len(ITEMS))
            for n, (t0, m) in enumerate(GROUPS):
                if n >= 3:
                    pe.wait_ge(xt_odd if n % 2 == 0 else xt_even, (n - 3) // 2 + 1)
                for c in range(IC):
                    ins = turn_to(work(n)[0:m, c * P:(c + 1) * P], conv[:, X0 + c, t0:t0 + m], ident[:, :])
                ins.then_inc(xt_done, 1)

            def mixed(n):
                t0, m = GROUPS[n]
                at = min(n + 3, NG - 1)
                pe.wait_ge(xt_even, at // 2 + 1)
                pe.wait_ge(xt_odd, (at + 1) // 2)
                pe.wait_ge(mix_done, n + 1)
                if n >= 3:
                    pe.wait_ge(yz_done, n - 2)
                for c in range(IC):
                    ins = mm(work(n)[:, c * m:(c + 1) * m], xt[0:m, n, c * P:(c + 1) * P],
                             mix[0:m, n, 0:m], start=True, stop=True)
                ins.then_inc(y_done, 1)

            def square_sum(k):
                t0, m = TILES[k]
                pe.wait_ge(yz_sum, covering(k))
                mm(TILE_BANK[k][0:m, 0:1], yz2[:, 0, t0:t0 + m], ones[:, :], start=True, stop=True)\
                    .then_inc(ss3_sum, 1)

            def output(k):
                t0, m = TILES[k]
                pe.wait_ge(ss3_base, k + 1)
                pe.wait_ge(yz_lo, covering(k))
                dst = TILE_BANK[k][0:m, 0:D]
                for c in range(IC):
                    mm(dst, yz_h[:, c, t0:t0 + m], out_h[:, c, :], start=(c == 0), stop=False)
                    mm(dst, yz_h[:, c, t0:t0 + m], out_l[:, c, :], start=False, stop=False)
                    ins = mm(dst, yz_l[:, c, t0:t0 + m], out_h[:, c, :], start=False, stop=(c == IC - 1))
                ins.then_inc(out_done, 1)

            for n in range(4):
                mixed(n)
            pe.wait_ge(exp_done, 3)
            pe.wait_ge(mix_raw, NG)
            pe.wait_ge(out_lo, IC)
            square_sum(0)
            mixed(4)
            output(0)
            square_sum(1)
            mixed(5)
            output(1)
            square_sum(2)
            square_sum(3)
            output(2)
            square_sum(4)
            output(3)
            turn(2)
            output(4)

            def down(k, w, chunks, chunk0, start, stop):
                t0, m = TILES[k]
                both, high = TILE_BANK[k][0:m, 0:2 * D], TILE_BANK[k][0:m, 0:D]
                for c in range(chunks):
                    pair = w[:, c, :, :].rearrange("p a n -> p (a n)")
                    mm(both, hid_h[:, chunk0 + c, t0:t0 + m], pair, start=start and c == 0, stop=False)
                    ins = mm(high, hid_l[:, chunk0 + c, t0:t0 + m], w[:, c, 0, :], start=False,
                             stop=stop and c == chunks - 1)
                return ins

            pe.wait_ge(m1_lo, 2)
            pe.wait_ge(turned_lo, 6)
            for n in range(MLP_UPS):
                h, c = divmod(n, FC)
                t0, m = HALVES[h]
                if n == 3:
                    turn(3)
                if n == FC:
                    pe.wait_ge(turned_lo, 8)
                if n >= 3:
                    pe.wait_ge(up_used, n - 2)
                product192(work(n)[:, 0:m], m1_h, m1_l, c * P, P, t0, m).then_inc(up_done, 1)
            pe.wait_ge(m2_lo, 1)
            for k in range(NT):
                if k == NT - 1:
                    turn(4)
                pe.wait_ge(hid_split, FC if k in HALF_TILES[0] else 2 * FC)
                down(k, m2, FC, 0, True, True).then_inc(mlp_done, 1)

            def gate(h, bk):
                t0, m = HALVES[h]
                return product192(bk[0:EXPERTS, 0:m], wg_h, wg_l, 0, EXPERTS, t0, m)

            def up(s, j, before):
                h, c = divmod(j, HC)
                t0, m = HALVES[h]
                pe.wait_ge(up_used, before + (MLP_UPS + j - 2))
                product192(work(j)[:, 0:m], e1_h[s], e1_l[s], c * P, P, t0, m).then_inc(up_done, 1)

            pe.wait_ge(small_ready, 2)
            pe.wait_ge(turned_lo, 10)
            pe.wait_ge(ex_lo, w1_at(1))
            gate(0, bank[1])
            for j in range(HC):
                up(0, j, 0)
            turn(5)
            for j in range(HC):
                up(1, j, HC)
            pe.wait_ge(turned_lo, 12)
            gate(1, bank[4]).then_inc(gate_done, 1)
            up(0, HC, HC)
            pe.wait_ge(gate_read, 2)
            for k, (t0, m) in enumerate(TILES):
                ins = turn_to(bank[0][0:m, k * EXPERTS:(k + 1) * EXPERTS], scoreT[:, t0:t0 + m],
                              ident[0:EXPERTS, 0:EXPERTS])
            ins.then_inc(score_done, 1)
            for j in range(HC + 1, UPS):
                up(0, j, HC)
            for j in range(HC, UPS):
                up(1, j, UPS)
            pe.wait_ge(cw_done, 1)
            for (h0, _), bk, tiles in zip(HALVES, bank, HALF_TILES):
                for k in tiles:
                    t0, m = TILES[k]
                    ins = mm(bk[:, t0 - h0:t0 - h0 + m], cw[0:m, k, 0:1].broadcast_to([m, P]),
                             ident[0:m, 0:m], start=True, stop=True)
            ins.then_inc(weight0_done, 1)
            for k, (t0, m) in enumerate(TILES):
                ins = turn_to(bank[2 + t0 // 512][0:EXPERTS, t0 % 512:t0 % 512 + m], cw[0:m, k, :],
                              ident[0:m, 0:m])
            ins.then_inc(cwT_done, 1)

            def up_all(s, before, split):
                pe.wait_ge(ex_lo, split)
                for j in range(UPS):
                    up(s, j, before)

            def down_all(s, before, split, stop):
                pe.wait_ge(ex_lo, split)
                for k in range(NT):
                    if k in (0, HALF_TILES[1].start):
                        pe.wait_ge(hid_split, before + (MLP_UPS + (HC if k == 0 else UPS)))
                    ins = down(k, e2[s], HC, s * HC, False, stop)
                    if stop:
                        ins.then_inc(moe_done, 1)

            pe.wait_ge(scaled, UPS)
            pe.wait_ge(cwT_lo, 2)
            for k, (t0, m) in enumerate(TILES):
                mm(TILE_BANK[k][0:m, 0:2 * D], cs[:, t0:t0 + m], b2s[:, :, :].rearrange("e a n -> e (a n)"),
                   start=True, stop=False)
            down_all(0, 0, w2_at(0), False)
            with pe.Fori(0, PERIODS // 2) as i:
                for s in range(2):
                    up_all(s, i * (2 * UPS) + (s + 2) * UPS, i * 4 + (2 * s + 4))
                    down_all(1 - s, i * (2 * UPS) + (s + 1) * UPS, i * 4 + (2 * s + 5), False)
            down_all(1, (EXPERTS - 1) * UPS, w2_at(EXPERTS - 1), True)


def _position_ids():
    import numpy as np
    side, n = 32, 6
    boundaries = np.arange(1.0 / side, 1.0, 1.0 / side, dtype=np.float32)
    frac = np.arange(0.0, 1.0 - 1e-06, 1.0 / n, dtype=np.float32)
    at = np.searchsorted(boundaries, frac, side="right")
    return (at[:, None] * side + at).reshape(-1)


def kernel(**inputs):
    import numpy as np
    import concourse.bacc as bacc
    from concourse.bass_utils import run_bass_kernel_spmd

    x = {n: np.asarray(a) for n, a in inputs.items()}

    def spread(v):
        return np.broadcast_to(np.reshape(v, (1, -1)), (P, np.size(v)))

    def twice(w):
        rest = w[P:D]
        return np.stack([w[0:P], np.concatenate([rest, rest])], axis=1)

    def chunked(w):
        return np.reshape(w, (-1, P, w.shape[1])).transpose(1, 0, 2)

    patches = x["x"].reshape(IMAGES, 3, 6, 16, 6, 16).transpose(1, 3, 5, 0, 2, 4)
    patches = patches.reshape(PATCH_CHUNKS, P, T)
    tok_w = x["L0_tok_conv_w"].reshape(D, PATCH_CHUNKS, P).transpose(1, 2, 0)
    pos = x["L0_tok_pos_table"][_position_ids()]
    pos = np.concatenate([pos] * IMAGES + [np.zeros((NT * P - T, D), np.float32)])
    posbias = np.concatenate([chunked(pos), np.broadcast_to(x["L0_tok_conv_b"], (P, 1, D))], axis=1)
    column = lambda v: np.reshape(v, (P, 1))
    vectors = np.concatenate([
        np.reshape(x["L0_attn_conv_w"], (NQ, P, TAPS)).transpose(1, 0, 2).reshape(P, NQ * TAPS),
        np.reshape(x["L0_attn_conv_b"], (NQ, P)).T,
        twice(x["L0_attn_norm1_w"][:, None])[:, :, 0],
        twice(x["L0_attn_norm2_w"][:, None])[:, :, 0],
        np.reshape(x["L0_attn_ssm_norm_w"], (IC, P)).T,
        spread(x["L0_attn_dt_bias"]), spread(x["L0_attn_A_log"]), spread(x["L0_attn_D"]),
        twice(x["L0_ffn_Wg"]).reshape(P, 2 * EXPERTS)], axis=1)
    first = np.stack([np.concatenate([
        twice(x["L0_ffn_W1"][e]).reshape(P, EXPERT_W1),
        np.reshape(x["L0_ffn_b1"][e], (HC, P)).T], axis=1) for e in range(EXPERTS)])
    arrays = {
        "patches": np.concatenate([patches, tok_w], axis=2),
        "posbias": posbias,
        "vectors": vectors,
        "in_proj": twice(x["L0_attn_in_proj_W"]),
        "out_proj": chunked(x["L0_attn_out_proj_W"]),
        "mlp1": twice(x["L0_attn_mlp_W1"]),
        "mlp2": chunked(x["L0_attn_mlp_W2"]).reshape(P, FC * D),
        "first": first,
        "second": np.stack([chunked(w).reshape(P, EXPERT_W2) for w in x["L0_ffn_W2"]]),
        "b2": x["L0_ffn_b2"],
    }
    nc = bacc.Bacc("TRN2", target_bir_lowering=False, num_devices=1)
    sent, args = {}, []
    for name, a in arrays.items():
        sent[f"in_{name}"] = np.ascontiguousarray(a)
        args.append(nc.dram_tensor(f"in_{name}", a.shape, mybir.dt.from_np(a.dtype), kind="ExternalInput").ap())
    args.append(nc.dram_tensor("out_0", (T, D), F32, kind="ExternalOutput").ap())
    build(nc, *args)
    r = run_bass_kernel_spmd(nc, [sent], core_ids=[0])
    return np.reshape(r.results[0]["out_0"], (IMAGES, LENGTH, D))
```

```python
from contextlib import ExitStack

import concourse.bass as bass
from concourse import mybir

ALU = mybir.AluOpType
ACT = mybir.ActivationFunctionType
F32 = mybir.dt.float32
F32R = mybir.dt.float32r
U32 = mybir.dt.uint32

P = 128
IMAGES, LENGTH = 16, 36
T = IMAGES * LENGTH
D = 192
REST = D - P
PATCH_CHUNKS = 768 // P
INNER = 384
IC = INNER // P
STATE = 128
TAPS = 4
PROJ = 2 * INNER + 2 * STATE + 1
FF = 768
FC = FF // P
EXPERTS = 8
HID = 384
HC = HID // P
EPS = 1e-5

TILES = [(k * P, min(P, T - k * P)) for k in range((T + P - 1) // P)]
NT = len(TILES)
HALF_TILES = [range(0, 2), range(2, NT)]
HALVES = [(0, 2 * P), (2 * P, T - 2 * P)]
PER = 3
GROUP = PER * LENGTH
GROUPS = [(g * GROUP, min(GROUP, T - g * GROUP)) for g in range((T + GROUP - 1) // GROUP)]
NG = len(GROUPS)
FULL = T // GROUP
LAST = T - FULL * GROUP

B_, C_, X0 = 0, 1, 2
CONV_SRC = [3, 4, 0, 1, 2]
PROJ_COL = [INNER + P * s for s in CONV_SRC] + [P * j for j in range(IC)]
NQ = len(CONV_SRC)
ITEMS = [(0, 0), (1, 0), (2, 0), (3, 0), (0, 1), (1, 1), (2, 1), (3, 1)] + \
    [(q, h) for q in range(4, NQ + IC) for h in range(2)]

V_CONVW = 0
V_CONVB = V_CONVW + NQ * TAPS
V_N1A = V_CONVB + NQ
V_N1C = V_N1A + 1
V_N2A = V_N1C + 1
V_N2C = V_N2A + 1
V_SSM = V_N2C + 1
V_DTB = V_SSM + IC
V_ALOG = V_DTB + 1
V_D = V_ALOG + 1
V_WGA = V_D + 1
V_WGC = V_WGA + EXPERTS
V_ALL = V_WGC + EXPERTS

EXPERT_W1 = 2 * HID
EXPERT_W2 = HC * D
SPREAD = 32 + EXPERTS


def build(nc, patches, bias_row, position, vectors, in_proj, out_proj, mlp1, mlp2, first, second, b2, out):
    with ExitStack() as ctx:
        def sb(name, shape, dt=F32):
            return ctx.enter_context(nc.sbuf_tensor(name, shape, dt))

        def sem(name):
            return ctx.enter_context(nc.semaphore(name))

        bank = [ctx.enter_context(nc.psum_tensor(f"bank{i}", [P, 512], F32)) for i in range(8)]
        TILE_BANK = bank[0:5]
        WORK = bank[5:8]
        TURN = [(bank[0][:, 0:256], bank[1][0:REST, 0:256]), (bank[2][:, 0:320], bank[3][0:REST, 0:320])]
        PROJ_RING = [bank[5], bank[6], bank[7], bank[1]]
        DT_ROW = [bank[4][0:1, 0:256], bank[0][0:1, 0:320]]
        DT_COL = bank[2]
        SUMS = [bank[5], bank[6]]
        SEG = [bank[4], bank[2]]
        G = [bank[3], bank[0]]
        LAST_ITEMS = [bank[4], bank[2]]
        XT = [bank[1], bank[3], bank[0], bank[7]]
        WEIGHT1 = [bank[5], bank[6]]
        GATE_T = [(0, 512, bank[3]), (512, T, bank[4])]

        def scan_pair(n, m, first_bank, second_bank):
            return first_bank[0:m, n * GROUP:n * GROUP + m] if n < 4 else \
                second_bank[0:m, (n - 4) * GROUP:(n - 4) * GROUP + m]

        pt = sb("pt", [P, PATCH_CHUNKS, T + D])
        pos = sb("pos", [P, NT, D])
        bias = sb("bias", [1, D])
        bias_parts = sb("bias_parts", [33, D], F32R)
        vec = sb("vec", [P, V_ALL])
        w_in = sb("w_in", [P, 2, PROJ])
        w_out = sb("w_out", [P, IC, D])
        w_m1 = sb("w_m1", [P, 2, FF])
        w_m2 = sb("w_m2", [P, FC, D])
        w_e1 = [sb(f"w_e1{s}", [P, EXPERT_W1 + HC]) for s in range(2)]
        w_e2 = [sb(f"w_e2{s}", [P, HC, D]) for s in range(2)]
        b2_sb = sb("b2_sb", [SPREAD, D])

        in_h = sb("in_h", [P, 2, PROJ], F32R)
        in_l = sb("in_l", [P, 2, PROJ], F32R)
        out_h = sb("out_h", [P, IC, D], F32R)
        out_l = sb("out_l", [P, IC, D], F32R)
        m1_h = sb("m1_h", [P, 2, FF], F32R)
        m1_l = sb("m1_l", [P, 2, FF], F32R)
        m2 = sb("m2", [P, FC, 2, D], F32R)
        e1_h = [sb(f"e1_h{s}", [P, 2, HID], F32R) for s in range(2)]
        e1_l = [sb(f"e1_l{s}", [P, 2, HID], F32R) for s in range(2)]
        e2 = [sb(f"e2{s}", [P, HC, 2, D], F32R) for s in range(2)]
        wg_h = sb("wg_h", [P, 2, EXPERTS], F32R)
        wg_l = sb("wg_l", [P, 2, EXPERTS], F32R)
        b2s = sb("b2s", [SPREAD, 2, D], F32R)

        ident = sb("ident", [P, P])
        upto = sb("upto", [GROUP, GROUP])
        after = sb("after", [GROUP, GROUP])
        skip = sb("skip", [GROUP, GROUP])
        ones = sb("ones", [P, 1])
        ones_rows = sb("ones_rows", [33, P], F32R)
        minus_half = sb("minus_half", [P, NT])
        column = sb("column", [P, EXPERTS])

        h0 = sb("h0", [P, NT, D])
        xln = sb("xln", [P, NT, D])
        rows = sb("rows", [P, NT, D])
        res = sb("res", [P, NT, D])
        acc = sb("acc", [P, NT, D])
        stats = sb("stats", [P, NT, 6])
        mv = sb("mv", [P, NT, 2])
        rstd = sb("rstd", [P, NT])
        ustd = sb("ustd", [P, NT])
        ss3 = sb("ss3", [P, NT])
        ss4 = sb("ss4", [P, NT])
        squares = sb("squares", [P, D])

        xa_h = sb("xa_h", [P, T], F32R)
        xa_l = sb("xa_l", [P, T], F32R)
        xc = sb("xc", [P, T], F32R)
        xraw = sb("xraw", [P, NQ, T])
        hid = sb("hid", [P, FC, T])
        conv = hid[:, 0:NQ, :]
        pt_flat = pt[:, :, :].rearrange("p c n -> p (c n)")
        zs = pt_flat[:, 0:IC * T].rearrange("p (c t) -> p c t", c=IC)
        yz = pt_flat[:, IC * T:2 * IC * T].rearrange("p (c t) -> p c t", c=IC)
        cb = pt_flat[:, 0:EXPERTS * T]
        yz2 = w_in[:, :, :].rearrange("p a n -> p (a n)")[:, 0:IC * T].rearrange("p (c t) -> p c t", c=IC)
        hid_h = sb("hid_h", [P, FC, T], F32R)
        hid_l = sb("hid_l", [P, FC, T], F32R)
        yz_h = hid_h[:, 0:IC, :]
        yz_l = hid_l[:, 0:IC, :]

        dt_row = sb("dt_row", [1, T])
        dtv = sb("dtv", [GROUP, NG])
        dt_abs = sb("dt_abs", [GROUP, NG])
        dt_exp = sb("dt_exp", [GROUP, NG])
        dt_ln = sb("dt_ln", [GROUP, NG])
        dt_pos = sb("dt_pos", [GROUP, NG])
        dt = sb("dt", [GROUP, NG])
        exp_a = sb("exp_a", [GROUP, 1])
        da = sb("da", [GROUP, NG])
        da_after, decay, mix = (
            t[0:GROUP, :, :].rearrange("p k n -> p (k n)")[:, 0:NG * GROUP].rearrange("p (g n) -> p g n", g=NG)
            for t in (rows, res, acc))
        xt = xraw[0:GROUP, :, :].rearrange("p q t -> p (q t)")[:, 0:NG * INNER].rearrange(
            "p (g c) -> p g c", g=NG)

        scoreT = rows[0:EXPERTS, :, :].rearrange("e k n -> e (k n)")[:, 0:T]
        cwT = res[0:EXPERTS, :, :].rearrange("e k n -> e (k n)")[:, 0:T]
        gate_rows = nc.dram_tensor("gate_rows", (EXPERTS, T), F32).ap()
        cs = sb("cs", [SPREAD, T], F32R)
        gs = sb("gs", [P, NT, EXPERTS])
        top = sb("top", [P, NT, EXPERTS])
        top_i = sb("top_i", [P, NT, EXPERTS], U32)
        top_f = sb("top_f", [P, NT, 2])
        gap = sb("gap", [P, NT])
        th = sb("th", [P, NT])
        prob = sb("prob", [P, NT, 2])
        chosen = sb("chosen", [P, NT, 2, EXPERTS])
        share = sb("share", [P, NT, 2, EXPERTS])
        cw = sb("cw", [P, NT, EXPERTS])

        ld_patch = [sem(f"ld_patch{c}") for c in range(PATCH_CHUNKS)]
        ld_bias, ld_pos, ld_pos_rest = sem("ld_bias"), sem("ld_pos"), sem("ld_pos_rest")
        ld_vec, ld_in, ld_out = sem("ld_vec"), sem("ld_in"), sem("ld_out")
        ld_m1, ld_m2, ld_b2 = sem("ld_m1"), sem("ld_m2"), sem("ld_b2")
        ld_e1 = [sem("ld_e10"), sem("ld_e11")]
        ld_e2 = [sem("ld_e20"), sem("ld_e21")]
        ld_cb2, ld_cb3, ld_cb, st_gate = sem("ld_cb2"), sem("ld_cb3"), sem("ld_cb"), sem("st_gate")
        stored = sem("stored")
        pool_own, act_own, dve_own = sem("pool_own"), sem("act_own"), sem("dve_own")
        consts, skip_ready, zeroed = sem("consts"), sem("skip_ready"), sem("zeroed")
        in_hi, in_lo = sem("in_hi"), sem("in_lo")
        out_hi, out_lo = sem("out_hi"), sem("out_lo")
        m1_hi, m1_lo = sem("m1_hi"), sem("m1_lo")
        m2_hi, m2_lo = sem("m2_hi"), sem("m2_lo")
        row_ready, parts_zeroed, bias_hi, bias_lo = (sem("row_ready"), sem("parts_zeroed"), sem("bias_hi"),
                                                     sem("bias_lo"))
        wg_ready, b2_hi, b2_ready = sem("wg_ready"), sem("b2_hi"), sem("b2_ready")
        b2_zeroed = sem("b2_zeroed")
        ex_hi, ex_lo = sem("ex_hi"), sem("ex_lo")
        tok_done, h0_done = sem("tok_done"), sem("h0_done")
        base_ready, power_done = sem("base_ready"), sem("power_done")
        xln_done, rows_done = sem("xln_done"), sem("rows_done")
        turned, turned_hi, turned_lo = sem("turned"), sem("turned_hi"), sem("turned_lo")
        proj_done, proj_used = sem("proj_done"), sem("proj_used")
        dtr_done, dtr_read, dtc_done, dt_in, dt_soft = (sem("dtr_done"), sem("dtr_read"), sem("dtc_done"),
                                                        sem("dt_in"), sem("dt_soft"))
        a_ready, da_in, da_ready, da_rest = sem("a_ready"), sem("da_in"), sem("da_ready"), sem("da_rest")
        seg_done, exp_done, decay_done = sem("seg_done"), sem("exp_done"), sem("decay_done")
        tapped, conv_done = sem("tapped"), sem("conv_done")
        silu_done = sem("silu_done")
        g_done, mix_raw, mix_done = sem("g_done"), sem("mix_raw"), sem("mix_done")
        xt_done, xt_even, xt_odd = sem("xt_done"), sem("xt_even"), sem("xt_odd")
        y_done, yz_done, yz_hi, yz_lo = sem("y_done"), sem("yz_done"), sem("yz_hi"), sem("yz_lo")
        yz_sq, yz_sum = sem("yz_sq"), sem("yz_sum")
        ss3_sum, ss3_most, ss3_base = sem("ss3_sum"), sem("ss3_most"), sem("ss3_base")
        out_done, res_done, ss4_done = sem("out_done"), sem("res_done"), sem("ss4_done")
        up_done, up_used = sem("up_done"), sem("up_used")
        mlp_hi = sem("mlp_hi")
        scaled, hid_hi, hid_split = sem("scaled"), sem("hid_hi"), sem("hid_split")
        mlp_done, h1_half, h1_done = sem("mlp_done"), sem("h1_half"), sem("h1_done")
        gate_done, gate_read, score_done = sem("gate_done"), sem("gate_read"), sem("score_done")
        gs_done, gap_done, th_done, cw_done = (sem("gs_done"), sem("gap_done"), sem("th_done"),
                                               sem("cw_done"))
        weight1_done = sem("weight1_done")
        y0_done, y0_half, y0_used = sem("y0_done"), sem("y0_half"), sem("y0_used")
        cwT_done, cwT_hi, cwT_copy, cwT_lo = (sem("cwT_done"), sem("cwT_hi"), sem("cwT_copy"),
                                              sem("cwT_lo"))
        moe_done, sum_half, sum_done = sem("moe_done"), sem("sum_half"), sem("sum_done")

        MLP_UPS = 2 * FC
        UPS = 2 * HC
        LAG = 2
        PERIODS = EXPERTS - 2

        def w1_at(e):
            return 1 if isinstance(e, int) and e == 0 else e * 2

        def w2_at(e):
            return 2 * e + 2 if isinstance(e, int) and e == EXPERTS - 1 else e * 2 + 3

        POW_U, POW_X, POW_3, POW_4, POW_2 = 0, 2, (4, 6), (5, 7), 7

        def work(n):
            return WORK[n % len(WORK)]

        def item_bank(n):
            return PROJ_RING[n % 4] if n < len(ITEMS) - 2 else LAST_ITEMS[n - len(ITEMS) + 2]

        def covering(k):
            return -(-(TILES[k][0] + TILES[k][1]) // GROUP)

        block = ctx.enter_context(nc.Block())

        @block.sync
        def _(sp):
            for c in range(PATCH_CHUNKS):
                sp.dma_start(pt[:, c, :], patches[c]).then_inc(ld_patch[c], 16)
                if c == 0:
                    sp.dma_start(bias[:, :], bias_row).then_inc(ld_bias, 16)
                if c == 1:
                    sp.dma_start(vec[:, :], vectors).then_inc(ld_vec, 16)
                if c == 2:
                    sp.dma_start(w_in[:, :, :], in_proj).then_inc(ld_in, 16)
                if c == PATCH_CHUNKS - 2:
                    sp.dma_start(pos[:, 0:2, :], position[:, 0:2, :]).then_inc(ld_pos, 16)
            sp.dma_start(pos[:, 2:NT, :], position[:, 2:NT, :]).then_inc(ld_pos_rest, 16)
            sp.dma_start(w_out[:, :, :], out_proj).then_inc(ld_out, 16)
            sp.dma_start(b2_sb[0:EXPERTS, :], b2).then_inc(ld_b2, 16)
            sp.dma_start(b2_sb[32:SPREAD, :], b2).then_inc(ld_b2, 16)
            sp.dma_start(w_m1[:, :, :], mlp1).then_inc(ld_m1, 16)
            sp.dma_start(w_m2[:, :, :], mlp2).then_inc(ld_m2, 16)
            for e in range(2):
                sp.dma_start(w_e1[e][:, :], first[e]).then_inc(ld_e1[e], 16)
                sp.dma_start(w_e2[e][:, :, :], second[e]).then_inc(ld_e2[e], 16)
            sp.wait_ge(up_used, MLP_UPS + UPS + HC)
            sp.dma_start(w_e1[0][:, :], first[2]).then_inc(ld_e1[0], 16)
            sp.wait_ge(cwT_copy, 2)
            sp.dma_start(gate_rows[:, :], cwT).then_inc(st_gate, 16)
            sp.wait_ge(st_gate, 16)

            def gate_weights(e, landed):
                sp.dma_start(cb[:, e * T:(e + 1) * T], gate_rows[e:e + 1, :].broadcast_to([P, T]))\
                    .then_inc(landed, 16)

            gate_weights(2, ld_cb2)
            sp.wait_ge(ex_lo, w2_at(0))
            sp.dma_start(w_e2[0][:, :, :], second[2]).then_inc(ld_e2[0], 16)
            sp.wait_ge(up_used, MLP_UPS + 2 * UPS)
            sp.dma_start(w_e1[1][:, :], first[3]).then_inc(ld_e1[1], 16)
            gate_weights(3, ld_cb3)
            sp.wait_ge(ex_lo, w2_at(1))
            sp.dma_start(w_e2[1][:, :, :], second[3]).then_inc(ld_e2[1], 16)
            for e in range(4, EXPERTS):
                gate_weights(e, ld_cb)
            with sp.Fori(0, PERIODS // 2 - 1) as i:
                for s in range(2):
                    sp.wait_ge(up_used, i * (2 * UPS) + (MLP_UPS + (s + 3) * UPS))
                    sp.dma_start(w_e1[s][:, :], first[bass.ds(i * 2 + (s + 4), 1), :, :].rearrange(
                        "a p n -> (a p) n")).then_inc(ld_e1[s], 16)
                    sp.wait_ge(ex_lo, i * 4 + (2 * s + 7))
                    sp.dma_start(w_e2[s][:, :, :].rearrange("p c n -> p (c n)"),
                                 second[bass.ds(i * 2 + (s + 4), 1), :, :].rearrange(
                                     "a p n -> (a p) n")).then_inc(ld_e2[s], 16)
            for k, (t0, m) in enumerate(TILES):
                sp.wait_ge(sum_done, k + 1)
                sp.dma_start(out[t0:t0 + m, :], acc[0:m, k, :]).then_inc(stored, 16)
            sp.wait_ge(stored, 16 * NT)

        @block.gpsimd
        def _(pool):
            own = [0]

            def link(ins):
                own[0] += 1
                ins.then_inc(pool_own, 1)
                pool.wait_ge(pool_own, own[0])

            g = nc.gpsimd

            def power(t, a, b):
                g.tensor_tensor(t[:, a:b], t[:, a:b], minus_half[:, 0:b - a], ALU.pow).then_inc(power_done, 1)

            link(g.memset(ident[:, :], 0.0))
            g.affine_select(out=ident[:, :], in_=ident[:, :], compare_op=ALU.not_equal, fill=1.0, base=0,
                            pattern=[[-1, P]], channel_multiplier=1).then_inc(consts, 1)
            g.memset(ones[:, :], 1.0).then_inc(consts, 1)
            g.memset(minus_half[:, :], -0.5).then_inc(consts, 1)
            for m, low, high in ((upto, (0, 0), (0, 1)), (after, (-1, -1), (LENGTH - 1, 0))):
                v = m[:, :].rearrange("r (j c) -> r j c", j=PER)
                link(g.memset(m[:, :], 1.0))
                link(g.affine_select(out=v, in_=v, compare_op=ALU.is_ge, fill=0.0, base=low[0],
                                     pattern=[[-LENGTH, PER], [low[1], LENGTH]], channel_multiplier=1))
                g.affine_select(out=v, in_=v, compare_op=ALU.is_ge, fill=0.0, base=high[0],
                                pattern=[[LENGTH, PER], [high[1], LENGTH]],
                                channel_multiplier=-1).then_inc(consts, 1)
            g.iota(column[:, :], pattern=[[1, EXPERTS]], base=0, channel_multiplier=0,
                   allow_small_or_imprecise_dtypes=True).then_inc(consts, 1)
            g.memset(cs[:, :].bitcast(F32), 0.0).then_inc(zeroed, 1)
            g.memset(b2s[:, :, :].bitcast(F32), 0.0).then_inc(b2_zeroed, 1)
            pool.wait_ge(ld_vec, 16)
            pool.wait_ge(consts, 6)
            g.tensor_scalar(skip[:, :], ident[0:GROUP, 0:GROUP], vec[0:GROUP, V_D:V_D + 1], 0.0, ALU.mult,
                            ALU.add).then_inc(skip_ready, 1)
            for n, tiles in enumerate(HALF_TILES):
                pool.wait_ge(base_ready, n + 1)
                power(ustd, tiles.start, tiles.stop)
            power(rstd, 0, NT)
            pool.wait_ge(power_done, POW_X + 1)
            pool.wait_ge(ld_b2, 32)
            pool.wait_ge(b2_zeroed, 1)
            for row in (0, 32):
                g.tensor_scalar(b2s[row:row + EXPERTS, 0, :], b2_sb[row:row + EXPERTS, :], 1.0, 0.0, ALU.mult,
                                ALU.add).then_inc(b2_hi, 1)
            pool.wait_ge(b2_hi, 2)
            g.tensor_tensor(b2s[0:EXPERTS, 1, :], b2_sb[0:EXPERTS, :], b2s[0:EXPERTS, 0, :].bitcast(F32),
                            ALU.subtract).then_inc(b2_ready, 1)
            pool.wait_ge(ld_m1, 16)
            for j, col in enumerate((V_N2A, V_N2C)):
                n2 = vec[:, col:col + 1]
                g.tensor_scalar(m1_h[:, j, :], w_m1[:, j, :], n2, 0.0, ALU.mult, ALU.add).then_inc(m1_hi, 1)
                pool.wait_ge(m1_hi, j + 1)
                link(g.tensor_scalar(w_m1[:, j, :], w_m1[:, j, :], n2, 0.0, ALU.mult, ALU.add))
                g.tensor_tensor(m1_l[:, j, :], w_m1[:, j, :], m1_h[:, j, :].bitcast(F32), ALU.subtract)\
                    .then_inc(m1_lo, 1)
            pool.wait_ge(da_in, 1)
            for n in range(4):
                g.tensor_scalar(da_after[:, n, :], after[:, :], da[:, n:n + 1], 0.0, ALU.mult, ALU.add)\
                    .then_inc(da_ready, 1)
            pool.wait_ge(exp_done, 3)
            g.tensor_tensor(decay[:, 0:FULL, :], decay[:, 0:FULL, :],
                            upto[:, :].rearrange("r (a c) -> r a c", a=1).broadcast_to([GROUP, FULL, GROUP]),
                            ALU.mult).then_inc(decay_done, 1)
            g.tensor_tensor(decay[0:LAST, FULL, 0:LAST], decay[0:LAST, FULL, 0:LAST], upto[0:LAST, 0:LAST],
                            ALU.mult).then_inc(decay_done, 1)
            for n, (t0, m) in enumerate(GROUPS):
                pool.wait_ge(mix_raw, n + 1)
                g.tensor_tensor(mix[0:m, n, 0:m], mix[0:m, n, 0:m], skip[0:m, 0:m], ALU.add)\
                    .then_inc(mix_done, 1)

            def squares_added(n):
                t0, m = GROUPS[n]
                pool.wait_ge(yz_sq, n + 1)
                total = yz2[:, 0, t0:t0 + m]
                link(g.tensor_tensor(total, total, yz2[:, 1, t0:t0 + m], ALU.add))
                g.tensor_tensor(total, total, yz2[:, 2, t0:t0 + m], ALU.add).then_inc(yz_sum, 1)

            def mlp_factors(n):
                tiles = HALF_TILES[n]
                pool.wait_ge(ss4_done, tiles.stop)
                t = ss4[:, tiles.start:tiles.stop]
                link(g.tensor_scalar(t, t, 1.0 / D, EPS, ALU.mult, ALU.add))
                power(ss4, tiles.start, tiles.stop)

            for n in range(4):
                squares_added(n)
            pool.wait_ge(ss3_base, 1)
            power(ss3, 0, 2)
            squares_added(4)
            mlp_factors(0)
            squares_added(5)
            pool.wait_ge(ss3_most, 1)
            pool.wait_ge(ss3_base, 2)
            power(ss3, 2, NT)
            mlp_factors(1)
            pool.wait_ge(ld_m2, 16)
            g.tensor_scalar(m2[:, :, 0, :], w_m2[:, :, :], 1.0, 0.0, ALU.mult, ALU.add).then_inc(m2_hi, 1)
            pool.wait_ge(m2_hi, 1)
            g.tensor_tensor(m2[:, :, 1, :], w_m2[:, :, :], m2[:, :, 0, :].bitcast(F32), ALU.subtract)\
                .then_inc(m2_lo, 1)

            def low1(s, count):
                pool.wait_ge(ex_hi, count)
                g.tensor_tensor(e1_l[s][:, :, :].rearrange("p a n -> p (a n)"), w_e1[s][:, 0:EXPERT_W1],
                                e1_h[s][:, :, :].rearrange("p a n -> p (a n)").bitcast(F32),
                                ALU.subtract).then_inc(ex_lo, 1)

            def low2(s, count):
                pool.wait_ge(ex_hi, count)
                g.tensor_tensor(e2[s][:, :, 1, :], w_e2[s][:, :, :], e2[s][:, :, 0, :].bitcast(F32),
                                ALU.subtract).then_inc(ex_lo, 1)

            low1(0, 1)
            low1(1, 2)
            for n, tiles in enumerate(HALF_TILES):
                pool.wait_ge(base_ready, 3 + n)
                power(rstd, tiles.start, tiles.stop)
            low2(0, 3)
            low1(0, w1_at(2))
            low2(1, w2_at(1))
            pool.wait_ge(zeroed, 1)
            pool.wait_ge(cwT_copy, 2)
            g.tensor_scalar(cs[0:EXPERTS, :], cwT, 1.0, 0.0, ALU.mult, ALU.add).then_inc(cwT_hi, 1)
            pool.wait_ge(cwT_hi, 1)
            g.tensor_tensor(cs[32:SPREAD, :], cwT, cs[0:EXPERTS, :].bitcast(F32), ALU.subtract)\
                .then_inc(cwT_lo, 1)
            pool.wait_ge(cwT_lo, 1)
            low1(1, w1_at(3))
            low2(0, w2_at(2))
            with pool.Fori(0, PERIODS // 2 - 1) as i:
                for s in range(2):
                    low1(s, i * 4 + (2 * s + 8))
                    low2(1 - s, i * 4 + (2 * s + 9))
            low2(1, w2_at(EXPERTS - 1))

        @block.scalar
        def _(act):
            a = nc.scalar
            own = [0]

            def link(ins):
                own[0] += 1
                ins.then_inc(act_own, 1)
                act.wait_ge(act_own, own[0])

            a.preload_act_table_set("natural_log_exp_and_others")
            act.wait_ge(ld_vec, 16)
            a.activation(exp_a[:, :], vec[0:GROUP, V_ALOG:V_ALOG + 1], ACT.Exp).then_inc(a_ready, 1)
            act.wait_ge(ld_in, 16)
            for j, v in enumerate((V_N1A, V_N1C)):
                a.activation(in_h[:, j, :], w_in[:, j, :], ACT.Copy, scale=vec[:, v:v + 1]).then_inc(in_hi, 1)
            act.wait_ge(ld_out, 16)
            for c in range(IC):
                a.activation(out_h[:, c, :], w_out[:, c, :], ACT.Copy,
                             scale=vec[:, V_SSM + c:V_SSM + c + 1]).then_inc(out_hi, 1)

            def turn_high(n):
                t0, m = HALVES[n % 2]
                srcA, srcB = TURN[n % 2]
                act.wait_ge(turned, n + 1)
                a.copy(xa_h[:, t0:t0 + m], srcA).then_inc(turned_hi, 1)
                a.copy(xc[0:REST, t0:t0 + m], srcB).then_inc(turned_hi, 1)

            def take_item(n):
                q, h = ITEMS[n]
                t0, m = HALVES[h]
                src = item_bank(n)[:, 0:m]
                act.wait_ge(proj_done, n + 1)
                if q >= NQ:
                    a.activation(zs[:, q - NQ, t0:t0 + m], src, ACT.Silu).then_inc(proj_used, 1)
                    return
                w = V_CONVW + CONV_SRC[q] * TAPS + TAPS - 1
                b = V_CONVB + CONV_SRC[q]
                a.copy(xraw[:, q, t0:t0 + m], src)
                a.activation(conv[:, q, t0:t0 + m], src, ACT.Identity, scale=vec[:, w:w + 1],
                             bias=vec[:, b:b + 1]).then_inc(proj_used, 1)

            turn_high(0)
            take_item(0)
            take_item(1)
            turn_high(1)
            for n in range(2, 6):
                take_item(n)
            act.wait_ge(dtr_done, 1)
            for (t0, m), src in zip(HALVES, DT_ROW):
                a.copy(dt_row[:, t0:t0 + m], src).then_inc(dtr_read, 1)
            take_item(6)
            take_item(7)
            act.wait_ge(dt_in, 1)
            link(a.activation(dt_abs[:, :], dtv[:, :], ACT.Abs))
            link(a.activation(dt_exp[:, :], dt_abs[:, :], ACT.Exp, scale=-1.0))
            a.activation(dt_ln[:, :], dt_exp[:, :], ACT.Ln, bias=1.0).then_inc(dt_soft, 1)
            take_item(8)
            take_item(9)
            act.wait_ge(seg_done, 1)
            a.activation(decay[:, 0:4, :].rearrange("p g t -> p (g t)"), SEG[0][0:GROUP, 0:4 * GROUP],
                         ACT.Exp).then_inc(exp_done, 1)
            act.wait_ge(seg_done, 2)
            a.activation(decay[:, 4, :], SEG[1][0:GROUP, 0:GROUP], ACT.Exp).then_inc(exp_done, 1)
            a.activation(decay[0:LAST, FULL, 0:LAST], SEG[1][0:LAST, GROUP:GROUP + LAST], ACT.Exp)\
                .then_inc(exp_done, 1)
            a.preload_act_table_set("silu_and_others")

            def silu(q):
                act.wait_ge(conv_done, q + 1)
                a.activation(conv[:, q, :], conv[:, q, :], ACT.Silu).then_inc(silu_done, 1)

            silu(B_)
            silu(C_)
            silu(X0)
            silu(X0 + 1)
            take_item(10)
            take_item(11)
            silu(X0 + 2)
            take_item(12)
            take_item(13)
            for n in range(0, NG, 2):
                m = GROUPS[n][1]
                act.wait_ge(xt_done, n + 1)
                a.copy(xt[0:m, n, :], XT[n % 4][0:m, 0:INNER]).then_inc(xt_even, 1)
                if n < 4:
                    take_item(14 + n // 2)

            def output_parts(n):
                t0, m = GROUPS[n]
                act.wait_ge(yz_done, n + 1)
                a.copy(yz_h[:, :, t0:t0 + m], yz[:, :, t0:t0 + m]).then_inc(yz_hi, 1)
                a.activation(yz2[:, :, t0:t0 + m], yz[:, :, t0:t0 + m], ACT.Square).then_inc(yz_sq, 1)

            def stream_squares(k):
                m = TILES[k][1]
                act.wait_ge(res_done, k + 1)
                if k:
                    act.wait_ge(ss4_done, k)
                a.activation(squares[0:m, :], res[0:m, k, :], ACT.Square, accum_out=ss4[0:m, k:k + 1])\
                    .then_inc(ss4_done, 1)

            for n in range(NG - 1):
                output_parts(n)
            stream_squares(0)
            stream_squares(1)
            output_parts(NG - 1)
            a.preload_act_table_set("gelu_and_others")
            turn_high(2)
            for k in range(2, NT):
                stream_squares(k)

            def gelu(bk, chunk, h, ups, bias):
                t0, m = HALVES[h]
                act.wait_ge(up_done, ups)
                a.activation(hid[:, chunk, t0:t0 + m], bk[:, 0:m], ACT.Gelu, bias=bias)\
                    .then_inc(up_used, 1)

            def high1(s, loads):
                act.wait_ge(ld_e1[s], loads)
                a.copy(e1_h[s][:, :, :].rearrange("p a n -> p (a n)"), w_e1[s][:, 0:EXPERT_W1])\
                    .then_inc(ex_hi, 1)

            def high2(s, loads):
                act.wait_ge(ld_e2[s], loads)
                a.copy(e2[s][:, :, 0, :], w_e2[s][:, :, :]).then_inc(ex_hi, 1)

            for n in range(MLP_UPS):
                gelu(work(n), n % FC, n // FC, n + 1, 0.0)
                if n >= FC:
                    t0, m = HALVES[1]
                    act.wait_ge(up_used, n + 1)
                    a.copy(hid_h[:, n - FC, t0:t0 + m], hid[:, n - FC, t0:t0 + m]).then_inc(mlp_hi, 1)
                if n == 3:
                    turn_high(3)
                if n == 5:
                    high1(0, 16)
            high1(1, 16)
            high2(0, 16)

            def expert_gelu(s, j, ups):
                h, c = divmod(j, HC)
                gelu(work(j), s * HC + c, h, ups, w_e1[s][:, EXPERT_W1 + c:EXPERT_W1 + c + 1])

            def expert_high(s, j, before):
                h, c = divmod(j, HC)
                t0, m = HALVES[h]
                if isinstance(before, int) and before == 0:
                    act.wait_ge(up_used, MLP_UPS + j + 1 if h == 0 else MLP_UPS + UPS + j - HC + 1)
                else:
                    act.wait_ge(scaled, before + (j + 1 - UPS))
                a.copy(hid_h[:, s * HC + c, t0:t0 + m], hid[:, s * HC + c, t0:t0 + m]).then_inc(hid_hi, 1)

            turn_high(4)
            for j in range(2 * HC):
                expert_gelu(j // HC, j % HC, MLP_UPS + j + 1)
                if j == 0:
                    turn_high(5)
            expert_high(0, 0, 0)
            act.wait_ge(gate_done, 1)
            for (t0, m), bk in zip(HALVES, (bank[1], bank[4])):
                a.copy(scoreT[:, t0:t0 + m], bk[0:EXPERTS, 0:m]).then_inc(gate_read, 1)
            expert_high(0, 1, 0)
            expert_gelu(0, HC, MLP_UPS + UPS + 1)
            expert_high(0, 2, 0)
            expert_gelu(0, HC + 1, MLP_UPS + UPS + 2)
            act.wait_ge(gap_done, 1)
            a.activation(th[:, :], gap[:, :], ACT.Tanh, scale=0.5).then_inc(th_done, 1)
            expert_gelu(0, HC + 2, MLP_UPS + UPS + 3)
            for j in range(HC):
                expert_gelu(1, HC + j, MLP_UPS + UPS + HC + j + 1)
                expert_high(0, HC + j, 0)
            act.wait_ge(cwT_done, 1)
            for t0, t1, bk in GATE_T:
                a.copy(cwT[:, t0:t1], bk[0:EXPERTS, 0:t1 - t0]).then_inc(cwT_copy, 1)
            expert_high(1, 0, UPS)
            high1(0, 32)
            expert_high(1, 1, UPS)
            expert_high(1, 2, UPS)
            high2(1, 16)
            for j in range(HC, UPS):
                expert_high(1, j, UPS)

            def expert(s, before, loads1, loads2, lag=LAG):
                for j in range(UPS + lag):
                    if j < UPS:
                        expert_gelu(s, j, before + (MLP_UPS + j + 1))
                    if j >= lag:
                        expert_high(s, j - lag, before)
                    if j == 2 and loads1 is not None:
                        high1(1 - s, loads1)
                    if j == 4:
                        high2(s, loads2)

            expert(0, 2 * UPS, 32, 32, UPS - 1)
            with act.Fori(0, PERIODS // 2 - 1) as i:
                for s in range(2):
                    expert(1 - s, i * (2 * UPS) + (s + 3) * UPS, i * 16 + 48, i * 16 + (32 if s == 0 else 48))
            expert(1, (EXPERTS - 1) * UPS, None, 16 * (EXPERTS // 2))

        @block.vector
        def _(dve):
            v = nc.vector
            own = [0]

            def step(ins):
                own[0] += 1
                ins.then_inc(dve_own, 1)

            def link(ins):
                step(ins)
                dve.wait_ge(dve_own, own[0])

            v.memset(bias_parts[:, :].bitcast(F32), 0.0).then_inc(parts_zeroed, 1)
            v.memset(ones_rows[:, :].bitcast(F32), 1.0).then_inc(row_ready, 1)
            for small in (mv, rstd, ustd, ss3, ss4, dtv, gs):
                step(v.memset(small[:], 1.0))
            dve.wait_ge(parts_zeroed, 1)
            dve.wait_ge(ld_bias, 16)
            v.tensor_copy(bias_parts[0:1, :], bias[:, :]).then_inc(bias_hi, 1)
            dve.wait_ge(bias_hi, 1)
            v.tensor_tensor(bias_parts[32:33, :], bias[:, :], bias_parts[0:1, :].bitcast(F32), ALU.subtract)\
                .then_inc(bias_lo, 1)
            dve.wait_ge(ld_vec, 16)
            wg = vec[:, V_WGA:V_ALL].rearrange("p (a e) -> p a e", a=2)
            link(v.tensor_copy(wg_h[:, :, :], wg))
            v.tensor_tensor(wg_l[:, :, :], wg, wg_h[:, :, :].bitcast(F32), ALU.subtract).then_inc(wg_ready, 1)
            for j, (w, r) in enumerate(((V_N1A, P), (V_N1C, REST))):
                dve.wait_ge(in_hi, j + 1)
                v.scalar_tensor_tensor(in_l[0:r, j, :], w_in[0:r, j, :], vec[0:r, w:w + 1],
                                       in_h[0:r, j, :].bitcast(F32), ALU.mult, ALU.subtract).then_inc(in_lo, 1)
            def embed(k):
                m = TILES[k][1]
                if k in (0, 2):
                    dve.wait_ge(ld_pos if k == 0 else ld_pos_rest, 16)
                dve.wait_ge(tok_done, k + 1)
                v.tensor_tensor(h0[0:m, k, :], TILE_BANK[k][0:m, 0:D], pos[0:m, k, :], ALU.add)\
                    .then_inc(h0_done, 1)

            def embed_stats(k, last):
                m = TILES[k][1]
                dve.wait_ge(h0_done, k + 1)
                link(v.bn_stats(stats[0:m, k, :], h0[0:m, k, :]))
                ins = v.bn_aggr(mv[0:m, k, :], stats[0:m, k, :])
                (link if last else step)(ins)

            def embed_base(tiles):
                a, b = tiles.start, tiles.stop
                v.tensor_scalar(ustd[:, a:b], mv[:, a:b, 1], 1.0 + EPS, EPS * EPS, ALU.mult, ALU.add)\
                    .then_inc(base_ready, 1)

            def embed_rows(n):
                dve.wait_ge(power_done, POW_U + n + 1)
                for k in HALF_TILES[n]:
                    m = TILES[k][1]
                    v.tensor_scalar(rows[0:m, k, :], h0[0:m, k, :], mv[0:m, k, 0:1], ustd[0:m, k:k + 1],
                                    ALU.subtract, ALU.mult).then_inc(rows_done, 1)

            def turn_low(n):
                t0, m = HALVES[n % 2]
                srcA, srcB = TURN[n % 2]
                dve.wait_ge(turned_hi, 2 * n + 1)
                v.tensor_tensor(xa_l[:, t0:t0 + m], srcA, xa_h[:, t0:t0 + m].bitcast(F32), ALU.subtract)\
                    .then_inc(turned_lo, 1)
                dve.wait_ge(turned_hi, 2 * n + 2)
                v.tensor_tensor(xc[REST:P, t0:t0 + m], srcB, xc[0:REST, t0:t0 + m].bitcast(F32),
                                ALU.subtract).then_inc(turned_lo, 1)

            embed(0)
            embed(1)
            embed_stats(0, False)
            embed_stats(1, True)
            embed_base(HALF_TILES[0])
            embed(2)
            embed_stats(2, False)
            embed_rows(0)
            embed(3)
            embed(4)
            for k in (3, 4):
                m = TILES[k][1]
                dve.wait_ge(h0_done, k + 1)
                step(v.bn_stats(stats[0:m, k, :], h0[0:m, k, :]))
            turn_low(0)
            dve.wait_ge(dve_own, own[0])
            for k in (3, 4):
                m = TILES[k][1]
                step(v.bn_aggr(mv[0:m, k, :], stats[0:m, k, :]))
            dve.wait_ge(dve_own, own[0])
            link(v.tensor_scalar(rstd[:, :], mv[:, :, 1], EPS, None, ALU.add))
            embed_base(HALF_TILES[1])
            embed_rows(1)
            dve.wait_ge(power_done, POW_X + 1)
            for k, (t0, m) in enumerate(TILES[0:2]):
                v.tensor_scalar(xln[0:m, k, :], h0[0:m, k, :], mv[0:m, k, 0:1], rstd[0:m, k:k + 1],
                                ALU.subtract, ALU.mult).then_inc(xln_done, 1)
            turn_low(1)
            for k in range(2, NT):
                m = TILES[k][1]
                v.tensor_scalar(xln[0:m, k, :], h0[0:m, k, :], mv[0:m, k, 0:1], rstd[0:m, k:k + 1],
                                ALU.subtract, ALU.mult).then_inc(xln_done, 1)
            for c in range(IC):
                dve.wait_ge(out_hi, c + 1)
                v.scalar_tensor_tensor(out_l[:, c, :], w_out[:, c, :], vec[:, V_SSM + c:V_SSM + c + 1],
                                       out_h[:, c, :].bitcast(F32), ALU.mult, ALU.subtract).then_inc(out_lo, 1)

            def tap(qs, items, k):
                for n, (q, item) in enumerate(zip(qs, items)):
                    cv = conv[:, q, :].rearrange("p (i l) -> p i l", i=IMAGES)
                    xv = xraw[:, q, :].rearrange("p (i l) -> p i l", i=IMAGES)
                    w = V_CONVW + CONV_SRC[q] * TAPS + TAPS - 1 - k
                    if k == 1:
                        dve.wait_ge(proj_used, item)
                    else:
                        dve.wait_ge(tapped, tap_count[q])
                    ins = v.scalar_tensor_tensor(cv[:, :, k:], xv[:, :, 0:LENGTH - k], vec[:, w:w + 1],
                                                 cv[:, :, k:], ALU.mult, ALU.add)
                    if k < TAPS - 1:
                        ins.then_inc(tapped, 1)
                        tap_count[NQ] += 1
                        tap_count[q] = tap_count[NQ]
                    else:
                        ins.then_inc(conv_done, 1)

            tap_count = [0] * (NQ + 1)
            tap((B_, C_), (5, 6), 1)
            tap((B_, C_), (5, 6), 2)
            dve.wait_ge(dtc_done, 1)
            link(v.tensor_scalar(dtv[:, 0:FULL], DT_COL[0:GROUP, 0:FULL], vec[0:GROUP, V_DTB:V_DTB + 1], None,
                                 ALU.add))
            v.tensor_scalar(dtv[0:LAST, FULL:NG], DT_COL[0:LAST, FULL:NG], vec[0:LAST, V_DTB:V_DTB + 1], None,
                            ALU.add).then_inc(dt_in, 1)
            tap((B_, C_), (5, 6), 3)
            dve.wait_ge(dt_in, 1)
            link(v.tensor_scalar(dt_pos[:, :], dtv[:, :], 0.0, None, ALU.max))
            dve.wait_ge(dt_soft, 1)
            link(v.tensor_tensor(dt[:, :], dt_pos[:, :], dt_ln[:, :], ALU.add))
            dve.wait_ge(a_ready, 1)
            v.tensor_scalar(da[:, :], dt[:, :], exp_a[:, 0:1], -1.0, ALU.mult, ALU.mult).then_inc(da_in, 1)
            dve.wait_ge(da_in, 1)
            dve.wait_ge(consts, 6)
            for n in range(4, NG):
                v.tensor_scalar(da_after[:, n, :], after[:, :], da[:, n:n + 1], None, ALU.mult)\
                    .then_inc(da_rest, 1)
            for k in range(1, TAPS):
                tap((X0, X0 + 1), (7, 8), k)
            for k in range(1, TAPS):
                tap((X0 + 2,), (10,), k)
            for n, (t0, m) in enumerate(GROUPS):
                dve.wait_ge(g_done, 1 if n < 4 else 2)
                dve.wait_ge(decay_done, 2 if n == FULL else 1)
                v.scalar_tensor_tensor(mix[0:m, n, 0:m], scan_pair(n, m, G[0], G[1]), dt[0:m, n:n + 1],
                                       decay[0:m, n, 0:m], ALU.mult, ALU.mult).then_inc(mix_raw, 1)
            for n in range(1, NG, 2):
                m = GROUPS[n][1]
                dve.wait_ge(xt_done, n + 1)
                v.tensor_copy(xt[0:m, n, :], XT[n % 4][0:m, 0:INNER]).then_inc(xt_odd, 1)
            dve.wait_ge(xln_done, NT)
            dve.wait_ge(proj_used, len(ITEMS))
            def residual(k):
                m = TILES[k][1]
                dve.wait_ge(power_done, POW_3[0 if k in HALF_TILES[0] else 1])
                dve.wait_ge(out_done, k + 1)
                v.scalar_tensor_tensor(res[0:m, k, :], TILE_BANK[k][0:m, 0:D], ss3[0:m, k:k + 1],
                                       xln[0:m, k, :], ALU.mult, ALU.add).then_inc(res_done, 1)

            def mlp_rows(n):
                dve.wait_ge(power_done, POW_4[n])
                for k in HALF_TILES[n]:
                    m = TILES[k][1]
                    v.tensor_scalar(rows[0:m, k, :], res[0:m, k, :], ss4[0:m, k:k + 1], None, ALU.mult)\
                        .then_inc(rows_done, 1)

            for n in range(NG + 1):
                if n == NG - 2:
                    dve.wait_ge(ss3_sum, 1)
                    v.tensor_scalar(ss3[:, 0:2], SUMS[0][:, 0:2], 1.0 / INNER, EPS, ALU.mult, ALU.add)\
                        .then_inc(ss3_base, 1)
                if n == NG - 1:
                    residual(0)
                    residual(1)
                if n < NG:
                    t0, m = GROUPS[n]
                    dve.wait_ge(y_done, n + 1)
                    src = work(n)[:, 0:IC * m].rearrange("p (c t) -> p c t", c=IC)
                    v.tensor_tensor(yz[:, :, t0:t0 + m], src, zs[:, :, t0:t0 + m], ALU.mult)\
                        .then_inc(yz_done, 1)
                if 1 <= n <= NG:
                    t0, m = GROUPS[n - 1]
                    dve.wait_ge(yz_hi, n)
                    v.tensor_tensor(yz_l[:, :, t0:t0 + m], yz[:, :, t0:t0 + m],
                                    yz_h[:, :, t0:t0 + m].bitcast(F32), ALU.subtract).then_inc(yz_lo, 1)
            mlp_rows(0)
            dve.wait_ge(ss3_sum, 2)
            v.tensor_scalar(ss3[:, 2:NT - 1], SUMS[1][:, 0:NT - 3], 1.0 / INNER, EPS, ALU.mult, ALU.add)\
                .then_inc(ss3_most, 1)
            m = TILES[-1][1]
            v.tensor_scalar(ss3[0:m, NT - 1:NT], SUMS[1][0:m, NT - 3:NT - 2], 1.0 / INNER, EPS, ALU.mult,
                            ALU.add).then_inc(ss3_base, 1)

            turn_low(2)
            residual(2)
            residual(3)
            residual(4)
            mlp_rows(1)

            def split_hidden(n):
                h, c = divmod(n, FC)
                t0, m = HALVES[h]
                dve.wait_ge(up_used, n + 1)
                if h == 0:
                    link(v.tensor_copy(hid_h[:, c, t0:t0 + m], hid[:, c, t0:t0 + m]))
                else:
                    dve.wait_ge(mlp_hi, c + 1)
                v.tensor_tensor(hid_l[:, c, t0:t0 + m], hid[:, c, t0:t0 + m],
                                hid_h[:, c, t0:t0 + m].bitcast(F32), ALU.subtract).then_inc(hid_split, 1)

            for n in range(MLP_UPS):
                split_hidden(n)
                if n == 0:
                    turn_low(3)

            def second_residual(k):
                m = TILES[k][1]
                dve.wait_ge(mlp_done, k + 1)
                v.tensor_tensor(acc[0:m, k, :], TILE_BANK[k][0:m, 0:D], h0[0:m, k, :], ALU.add)\
                    .then_inc(h1_half, 1)
                dve.wait_ge(h1_half, k + 1)
                v.tensor_tensor(acc[0:m, k, :], TILE_BANK[k][0:m, D:2 * D], acc[0:m, k, :], ALU.add)\
                    .then_inc(h1_done, 1)
                dve.wait_ge(h1_done, k + 1)
                link(v.bn_stats(stats[0:m, k, :], acc[0:m, k, :]))
                link(v.bn_aggr(mv[0:m, k, :], stats[0:m, k, :]))

            def second_base(tiles):
                a, b = tiles.start, tiles.stop
                v.tensor_scalar(rstd[:, a:b], mv[:, a:b, 1], EPS, None, ALU.add).then_inc(base_ready, 1)

            def expert_rows(n):
                dve.wait_ge(power_done, POW_2 + n + 1)
                for k in HALF_TILES[n]:
                    m = TILES[k][1]
                    v.tensor_scalar(rows[0:m, k, :], acc[0:m, k, :], mv[0:m, k, 0:1], rstd[0:m, k:k + 1],
                                    ALU.subtract, ALU.mult).then_inc(rows_done, 1)

            second_residual(0)
            second_residual(1)
            second_base(HALF_TILES[0])
            second_residual(2)
            expert_rows(0)
            second_residual(3)
            turn_low(4)
            second_residual(4)
            second_base(HALF_TILES[1])
            expert_rows(1)
            turn_low(5)

            def weigh(e, s, j, before):
                h, c = divmod(j, HC)
                t0, m = HALVES[h]
                if not isinstance(e, int):
                    weight = cb[:, bass.ds(e * T + t0, m)]
                elif e == 1:
                    weight = WEIGHT1[h][:, 0:m]
                else:
                    weight = cb[:, e * T + t0:e * T + t0 + m]
                dve.wait_ge(up_used, before + (MLP_UPS + j + 1))
                v.tensor_tensor(hid[:, s * HC + c, t0:t0 + m], hid[:, s * HC + c, t0:t0 + m], weight,
                                ALU.mult).then_inc(scaled, 1)

            def expert_low(s, j, before):
                h, c = divmod(j, HC)
                t0, m = HALVES[h]
                dve.wait_ge(hid_hi, before + (j + 1))
                v.tensor_tensor(hid_l[:, s * HC + c, t0:t0 + m], hid[:, s * HC + c, t0:t0 + m],
                                hid_h[:, s * HC + c, t0:t0 + m].bitcast(F32), ALU.subtract)\
                    .then_inc(hid_split, 1)

            expert_low(0, 0, 0)
            dve.wait_ge(score_done, 1)
            v.tensor_copy(gs[:, 0:NT - 1, :].rearrange("p k e -> p (k e)"), bank[0][:, 0:(NT - 1) * EXPERTS])\
                .then_inc(gs_done, 1)
            m = TILES[-1][1]
            v.tensor_copy(gs[0:m, NT - 1, :], bank[0][0:m, (NT - 1) * EXPERTS:NT * EXPERTS])\
                .then_inc(gs_done, 1)
            expert_low(0, 1, 0)
            dve.wait_ge(gs_done, 2)
            for k in range(NT):
                step(v.max(top[:, k, :], gs[:, k, :]))
            dve.wait_ge(dve_own, own[0])
            v.tensor_tensor(gap[:, :], top[:, :, 0], top[:, :, 1], ALU.subtract).then_inc(gap_done, 1)
            for k in range(NT):
                step(v.max_index(top_i[:, k, :], top[:, k, :], gs[:, k, :]))
            dve.wait_ge(dve_own, own[0])
            step(v.tensor_copy(top_f[:, :, :], top_i[:, :, 0:2]))
            dve.wait_ge(th_done, 1)
            step(v.tensor_scalar(prob[:, :, 0], th[:, :], 0.5, 0.5, ALU.mult, ALU.add))
            step(v.tensor_scalar(prob[:, :, 1], th[:, :], -0.5, 0.5, ALU.mult, ALU.add))
            dve.wait_ge(dve_own, own[0] - 2)
            dve.wait_ge(consts, 6)
            link(v.tensor_tensor(chosen[:, :, :, :].rearrange("p k j e -> p (k j) e"),
                                 column[:, :].rearrange("p (a e) -> p a e", a=1).broadcast_to(
                                     [P, 2 * NT, EXPERTS]),
                                 top_f[:, :, :].rearrange("p k (j a) -> p (k j) a", a=1).broadcast_to(
                                     [P, 2 * NT, EXPERTS]), ALU.is_equal))
            expert_low(0, 2, 0)
            link(v.tensor_tensor(share[:, :, :, :].rearrange("p k j e -> p (k j) e"),
                                 chosen[:, :, :, :].rearrange("p k j e -> p (k j) e"),
                                 prob[:, :, :].rearrange("p k (j a) -> p (k j) a", a=1).broadcast_to(
                                     [P, 2 * NT, EXPERTS]), ALU.mult))
            v.tensor_tensor(cw[:, :, :], share[:, :, 0, :], share[:, :, 1, :], ALU.add).then_inc(cw_done, 1)

            for j in range(HC, UPS):
                expert_low(0, j, 0)
            dve.wait_ge(weight1_done, 1)
            for j in range(UPS):
                weigh(1, 1, j, UPS)

            def combine(k):
                m = TILES[k][1]
                dve.wait_ge(y0_done, k + 1)
                dve.wait_ge(cw_done, 1)
                v.scalar_tensor_tensor(acc[0:m, k, :], TILE_BANK[k][0:m, 0:D], cw[0:m, k, 0:1],
                                       acc[0:m, k, :], ALU.mult, ALU.add).then_inc(y0_half, 1)

            def combine_rest(k):
                m = TILES[k][1]
                dve.wait_ge(y0_half, k + 1)
                v.scalar_tensor_tensor(acc[0:m, k, :], TILE_BANK[k][0:m, D:2 * D], cw[0:m, k, 0:1],
                                       acc[0:m, k, :], ALU.mult, ALU.add).then_inc(y0_used, 1)

            combine(0)
            expert_low(1, 0, UPS)
            combine_rest(0)
            combine(1)
            expert_low(1, 1, UPS)
            combine_rest(1)
            expert_low(1, 2, UPS)
            combine(2)
            expert_low(1, 3, UPS)
            combine_rest(2)
            combine(3)
            expert_low(1, 4, UPS)
            combine_rest(3)
            combine(4)
            expert_low(1, 5, UPS)
            combine_rest(4)

            def expert(e, s, before):
                for j in range(UPS + LAG):
                    if j < UPS:
                        weigh(e, s, j, before)
                    if j >= LAG:
                        expert_low(s, j - LAG, before)

            dve.wait_ge(ld_cb2, 16)
            expert(2, 0, 2 * UPS)
            dve.wait_ge(ld_cb3, 16)
            expert(3, 1, 3 * UPS)
            dve.wait_ge(ld_cb, 16 * (EXPERTS - 4))
            with dve.Fori(0, PERIODS // 2 - 1) as i:
                for s in range(2):
                    expert(i * 2 + (s + 4), s, i * (2 * UPS) + (s + 4) * UPS)
            for k, (t0, m) in enumerate(TILES):
                dve.wait_ge(moe_done, k + 1)
                v.tensor_tensor(acc[0:m, k, :], TILE_BANK[k][0:m, 0:D], acc[0:m, k, :], ALU.add)\
                    .then_inc(sum_half, 1)
                dve.wait_ge(sum_half, k + 1)
                v.tensor_tensor(acc[0:m, k, :], TILE_BANK[k][0:m, D:2 * D], acc[0:m, k, :], ALU.add)\
                    .then_inc(sum_done, 1)

        @block.tensor
        def _(pe):
            mm = nc.tensor.matmul
            turn_to = nc.tensor.transpose
            for c in range(PATCH_CHUNKS):
                pe.wait_ge(ld_patch[c], 16)
                for k, (t0, m) in enumerate(TILES):
                    ins = mm(TILE_BANK[k][0:m, 0:D], pt[:, c, t0:t0 + m], pt[:, c, T:T + D],
                             start=(c == 0), stop=(c == PATCH_CHUNKS - 1))
                    if c == PATCH_CHUNKS - 1:
                        ins.then_inc(tok_done, 1)
                if c == 1:
                    pe.wait_ge(row_ready, 1)
                    pe.wait_ge(bias_lo, 1)
                    for k, (t0, m) in enumerate(TILES):
                        mm(TILE_BANK[k][0:m, 0:D], ones_rows[:, 0:m], bias_parts[:, :], start=False, stop=False)

            def turn(n):
                at0, width = HALVES[n % 2]
                toA, toB = TURN[n % 2]
                for k in HALF_TILES[n % 2]:
                    t0, m = TILES[k]
                    at = t0 - at0
                    pe.wait_ge(rows_done, NT * (n // 2) + k + 1)
                    turn_to(toA[:, at:at + m], rows[0:m, k, 0:P], ident[0:m, 0:m])
                    ins = turn_to(toB[:, at:at + m], rows[0:m, k, P:D], ident[0:m, 0:m])
                ins.then_inc(turned, 1)

            def product192(dst, w_h, w_l, c0, n, t0, m):
                wah, wch = w_h[:, 0, c0:c0 + n], w_h[:, 1, c0:c0 + n]
                wal, wcl = w_l[:, 0, c0:c0 + n], w_l[0:REST, 1, c0:c0 + n]
                mm(dst, wah, xa_h[:, t0:t0 + m], start=True, stop=False)
                mm(dst, wah, xa_l[:, t0:t0 + m], start=False, stop=False)
                mm(dst, wal, xa_h[:, t0:t0 + m], start=False, stop=False)
                mm(dst, wch, xc[:, t0:t0 + m], start=False, stop=False)
                return mm(dst, wcl, xc[0:REST, t0:t0 + m], start=False, stop=True)

            def item(n):
                q, h = ITEMS[n]
                t0, m = HALVES[h]
                if 4 <= n < len(ITEMS) - 2:
                    pe.wait_ge(proj_used, n - 3)
                product192(item_bank(n)[:, 0:m], in_h, in_l, PROJ_COL[q], P, t0, m).then_inc(proj_done, 1)

            pe.wait_ge(consts, 6)
            turn(0)
            pe.wait_ge(in_lo, 2)
            pe.wait_ge(turned_lo, 2)
            item(0)
            item(1)
            turn(1)
            item(2)
            item(3)
            pe.wait_ge(turned_lo, 4)
            item(4)
            item(5)
            for (t0, m), dst in zip(HALVES, DT_ROW):
                ins = product192(dst, in_h, in_l, PROJ - 1, 1, t0, m)
            ins.then_inc(dtr_done, 1)
            item(6)
            item(7)
            pe.wait_ge(dtr_read, 2)
            for n, (t0, m) in enumerate(GROUPS):
                ins = mm(DT_COL[0:m, n:n + 1], dt_row[:, t0:t0 + m], ones[0:1, :], start=True, stop=True)
            ins.then_inc(dtc_done, 1)
            item(8)
            item(9)
            item(10)
            item(11)
            for n, (t0, m) in enumerate(GROUPS):
                if n < 4:
                    pe.wait_ge(da_ready, n + 1)
                else:
                    pe.wait_ge(da_rest, n - 3)
                ins = mm(scan_pair(n, m, SEG[0], SEG[1]), da_after[0:m, n, 0:m], upto[0:m, 0:m],
                         start=True, stop=True)
                if n in (3, NG - 1):
                    ins.then_inc(seg_done, 1)
            item(12)
            item(13)
            pe.wait_ge(exp_done, 3)
            item(14)
            item(15)
            pe.wait_ge(silu_done, 2)
            for n, (t0, m) in enumerate(GROUPS):
                ins = mm(scan_pair(n, m, G[0], G[1]), conv[:, B_, t0:t0 + m], conv[:, C_, t0:t0 + m],
                         start=True, stop=True)
                if n in (3, NG - 1):
                    ins.then_inc(g_done, 1)
            pe.wait_ge(silu_done, NQ)
            for n, (t0, m) in enumerate(GROUPS):
                if n in (0, 3):
                    pe.wait_ge(proj_used, 12)
                elif n in (1, 2):
                    pe.wait_ge(mix_raw, 4 if n == 1 else NG)
                else:
                    pe.wait_ge(xt_odd if n % 2 else xt_even, 1)
                for c in range(IC):
                    ins = turn_to(XT[n % 4][0:m, c * P:(c + 1) * P], conv[:, X0 + c, t0:t0 + m], ident[:, :])
                ins.then_inc(xt_done, 1)

            def mixed(n):
                t0, m = GROUPS[n]
                pe.wait_ge(xt_odd if n % 2 else xt_even, n // 2 + 1)
                if n == 2:
                    pe.wait_ge(xt_odd, 2)
                pe.wait_ge(mix_done, n + 1)
                if n >= 3:
                    pe.wait_ge(yz_done, n - 2)
                for c in range(IC):
                    ins = mm(work(n)[:, c * m:(c + 1) * m], xt[0:m, n, c * P:(c + 1) * P],
                             mix[0:m, n, 0:m], start=True, stop=True)
                ins.then_inc(y_done, 1)

            def square_sums(n):
                pe.wait_ge(yz_done, n + 4)
                for at, k in enumerate(HALF_TILES[n]):
                    t0, m = TILES[k]
                    pe.wait_ge(yz_sum, covering(k))
                    ins = mm(SUMS[n][0:m, at:at + 1], yz2[:, 0, t0:t0 + m], ones[:, :], start=True, stop=True)
                ins.then_inc(ss3_sum, 1)

            def output(k):
                t0, m = TILES[k]
                pe.wait_ge(yz_lo, covering(k))
                dst = TILE_BANK[k][0:m, 0:D]
                for c in range(IC):
                    mm(dst, yz_h[:, c, t0:t0 + m], out_h[:, c, :], start=(c == 0), stop=False)
                    mm(dst, yz_h[:, c, t0:t0 + m], out_l[:, c, :], start=False, stop=False)
                    ins = mm(dst, yz_l[:, c, t0:t0 + m], out_h[:, c, :], start=False, stop=(c == IC - 1))
                ins.then_inc(out_done, 1)

            pe.wait_ge(proj_used, len(ITEMS) - 2)
            for n in range(4):
                mixed(n)
            pe.wait_ge(proj_used, len(ITEMS))
            pe.wait_ge(xt_even, NG // 2)
            pe.wait_ge(xt_odd, NG // 2)
            pe.wait_ge(mix_raw, NG)
            pe.wait_ge(out_lo, IC)
            output(0)
            mixed(4)
            square_sums(0)
            output(1)
            mixed(5)
            output(2)
            output(3)
            square_sums(1)
            turn(2)
            output(4)

            def down(k, w, chunks, chunk0, start, stop):
                t0, m = TILES[k]
                both, high = TILE_BANK[k][0:m, 0:2 * D], TILE_BANK[k][0:m, 0:D]
                for c in range(chunks):
                    pair = w[:, c, :, :].rearrange("p a n -> p (a n)")
                    mm(both, hid_h[:, chunk0 + c, t0:t0 + m], pair, start=start and c == 0, stop=False)
                    ins = mm(high, hid_l[:, chunk0 + c, t0:t0 + m], w[:, c, 0, :], start=False,
                             stop=stop and c == chunks - 1)
                return ins

            pe.wait_ge(m1_lo, 2)
            pe.wait_ge(turned_lo, 6)
            for n in range(MLP_UPS):
                h, c = divmod(n, FC)
                t0, m = HALVES[h]
                if n == 4:
                    turn(3)
                if n == FC:
                    pe.wait_ge(turned_lo, 8)
                if n >= 3:
                    pe.wait_ge(up_used, n - 2)
                product192(work(n)[:, 0:m], m1_h, m1_l, c * P, P, t0, m).then_inc(up_done, 1)
            pe.wait_ge(m2_lo, 1)
            for k in range(NT):
                if k == NT - 1:
                    turn(4)
                pe.wait_ge(hid_split, FC if k in HALF_TILES[0] else 2 * FC)
                down(k, m2, FC, 0, True, True).then_inc(mlp_done, 1)

            def gate(h, bk):
                t0, m = HALVES[h]
                return product192(bk[0:EXPERTS, 0:m], wg_h, wg_l, 0, EXPERTS, t0, m)

            def up(s, j, before):
                h, c = divmod(j, HC)
                t0, m = HALVES[h]
                pe.wait_ge(up_used, before + (MLP_UPS + j - 2))
                product192(work(j)[:, 0:m], e1_h[s], e1_l[s], c * P, P, t0, m).then_inc(up_done, 1)

            pe.wait_ge(wg_ready, 1)
            pe.wait_ge(turned_lo, 10)
            pe.wait_ge(ex_lo, w1_at(1))
            gate(0, bank[1])
            for j in range(HC):
                up(0, j, 0)
            turn(5)
            for j in range(HC):
                up(1, j, HC)
            pe.wait_ge(turned_lo, 12)
            gate(1, bank[4]).then_inc(gate_done, 1)
            up(0, HC, HC)
            pe.wait_ge(gate_read, 2)
            for k, (t0, m) in enumerate(TILES):
                ins = turn_to(bank[0][0:m, k * EXPERTS:(k + 1) * EXPERTS], scoreT[:, t0:t0 + m],
                              ident[0:EXPERTS, 0:EXPERTS])
            ins.then_inc(score_done, 1)
            for j in range(HC + 1, UPS):
                up(0, j, HC)
            for j in range(HC, UPS):
                up(1, j, UPS)
            pe.wait_ge(cw_done, 1)
            for k, (t0, m) in enumerate(TILES):
                at, _, bk = GATE_T[t0 // 512]
                ins = turn_to(bk[0:EXPERTS, t0 - at:t0 - at + m], cw[0:m, k, :], ident[0:m, 0:m])
            ins.then_inc(cwT_done, 1)
            pe.wait_ge(up_used, MLP_UPS + 2 * UPS - 1)
            for (h0, _), bk, tiles in zip(HALVES, WEIGHT1, HALF_TILES):
                for k in tiles:
                    t0, m = TILES[k]
                    ins = mm(bk[:, t0 - h0:t0 - h0 + m], cw[0:m, k, 1:2].broadcast_to([m, P]),
                             ident[0:m, 0:m], start=True, stop=True)
            ins.then_inc(weight1_done, 1)

            def up_all(s, before, split):
                pe.wait_ge(ex_lo, split)
                for j in range(UPS):
                    up(s, j, before)

            def down_all(s, before, split, start=False, stop=False, done=None):
                pe.wait_ge(ex_lo, split)
                for k in range(NT):
                    if k in (0, HALF_TILES[1].start):
                        pe.wait_ge(hid_split, before + (MLP_UPS + (HC if k == 0 else UPS)))
                    if start and done is None:
                        pe.wait_ge(y0_used, k + 1)
                    ins = down(k, e2[s], HC, s * HC, start, stop)
                    if done is not None:
                        ins.then_inc(done, 1)

            pe.wait_ge(cwT_copy, 2)
            down_all(0, 0, w2_at(0), start=True, stop=True, done=y0_done)
            pe.wait_ge(scaled, UPS)
            up_all(0, 2 * UPS, w1_at(2))
            down_all(1, UPS, w2_at(1), start=True)
            pe.wait_ge(b2_ready, 1)
            pe.wait_ge(cwT_lo, 1)
            for k, (t0, m) in enumerate(TILES):
                mm(TILE_BANK[k][0:m, 0:2 * D], cs[:, t0:t0 + m], b2s[:, :, :].rearrange("e a n -> e (a n)"),
                   start=False, stop=False)
            up_all(1, 3 * UPS, w1_at(3))
            down_all(0, 2 * UPS, w2_at(2))
            with pe.Fori(0, PERIODS // 2 - 1) as i:
                for s in range(2):
                    up_all(s, i * (2 * UPS) + (s + 4) * UPS, i * 4 + (2 * s + 8))
                    down_all(1 - s, i * (2 * UPS) + (s + 3) * UPS, i * 4 + (2 * s + 9))
            down_all(1, (EXPERTS - 1) * UPS, w2_at(EXPERTS - 1), stop=True, done=moe_done)


def _position_ids():
    import numpy as np
    side, n = 32, 6
    boundaries = np.arange(1.0 / side, 1.0, 1.0 / side, dtype=np.float32)
    frac = np.arange(0.0, 1.0 - 1e-06, 1.0 / n, dtype=np.float32)
    at = np.searchsorted(boundaries, frac, side="right")
    return (at[:, None] * side + at).reshape(-1)


def kernel(**inputs):
    import numpy as np
    import concourse.bacc as bacc
    from concourse.bass_utils import run_bass_kernel_spmd

    x = {n: np.asarray(a) for n, a in inputs.items()}

    def spread(v):
        return np.broadcast_to(np.reshape(v, (1, -1)), (P, np.size(v)))

    def twice(w):
        rest = w[P:D]
        return np.stack([w[0:P], np.concatenate([rest, rest])], axis=1)

    def chunked(w):
        return np.reshape(w, (-1, P, w.shape[1])).transpose(1, 0, 2)

    patches = x["x"].reshape(IMAGES, 3, 6, 16, 6, 16).transpose(1, 3, 5, 0, 2, 4)
    patches = patches.reshape(PATCH_CHUNKS, P, T)
    tok_w = x["L0_tok_conv_w"].reshape(D, PATCH_CHUNKS, P).transpose(1, 2, 0)
    pos = x["L0_tok_pos_table"][_position_ids()]
    pos = np.concatenate([pos] * IMAGES + [np.zeros((NT * P - T, D), np.float32)])
    column = lambda v: np.reshape(v, (P, 1))
    vectors = np.concatenate([
        np.reshape(x["L0_attn_conv_w"], (NQ, P, TAPS)).transpose(1, 0, 2).reshape(P, NQ * TAPS),
        np.reshape(x["L0_attn_conv_b"], (NQ, P)).T,
        twice(x["L0_attn_norm1_w"][:, None])[:, :, 0],
        twice(x["L0_attn_norm2_w"][:, None])[:, :, 0],
        np.reshape(x["L0_attn_ssm_norm_w"], (IC, P)).T,
        spread(x["L0_attn_dt_bias"]), spread(x["L0_attn_A_log"]), spread(x["L0_attn_D"]),
        twice(x["L0_ffn_Wg"]).reshape(P, 2 * EXPERTS)], axis=1)
    first = np.stack([np.concatenate([
        twice(x["L0_ffn_W1"][e]).reshape(P, EXPERT_W1),
        np.reshape(x["L0_ffn_b1"][e], (HC, P)).T], axis=1) for e in range(EXPERTS)])
    arrays = {
        "patches": np.concatenate([patches, tok_w], axis=2),
        "bias": np.reshape(x["L0_tok_conv_b"], (1, D)),
        "position": chunked(pos),
        "vectors": vectors,
        "in_proj": twice(x["L0_attn_in_proj_W"]),
        "out_proj": chunked(x["L0_attn_out_proj_W"]),
        "mlp1": twice(x["L0_attn_mlp_W1"]),
        "mlp2": chunked(x["L0_attn_mlp_W2"]).reshape(P, FC * D),
        "first": first,
        "second": np.stack([chunked(w).reshape(P, EXPERT_W2) for w in x["L0_ffn_W2"]]),
        "b2": x["L0_ffn_b2"],
    }
    nc = bacc.Bacc("TRN2", target_bir_lowering=False, num_devices=1)
    sent, args = {}, []
    for name, a in arrays.items():
        sent[f"in_{name}"] = np.ascontiguousarray(a)
        args.append(nc.dram_tensor(f"in_{name}", a.shape, mybir.dt.from_np(a.dtype), kind="ExternalInput").ap())
    args.append(nc.dram_tensor("out_0", (T, D), F32, kind="ExternalOutput").ap())
    build(nc, *args)
    r = run_bass_kernel_spmd(nc, [sent], core_ids=[0])
    return np.reshape(r.results[0]["out_0"], (IMAGES, LENGTH, D))
```
